# Optimizing a Trainium2 kernel written in Bass

```python
import numpy as np
import jax
import jax.numpy as jnp

def _softmax(x, axis=-1):
    return jax.nn.softmax(x, axis=axis)

def _gelu(x):
    return jax.nn.gelu(x, approximate=True)

def _silu(x):
    return jax.nn.silu(x)

def _sigmoid(x):
    return jax.nn.sigmoid(x)

def _layernorm(x, axis=-1, eps=1e-05):
    m = jnp.mean(x, axis=axis, keepdims=True)
    v = jnp.var(x, axis=axis, keepdims=True)
    return (x - m) / jnp.sqrt(v + eps)

def _scatter_add(tgt, idx, src, axis=0):
    return tgt.at[idx].add(src)

def _segment_sum(src, seg, n):
    return jax.ops.segment_sum(src, seg, n)
kernel_name = 'mk_xattn_ffn_d1_seqx_r4_72a2ea'

def setup_inputs(seed: int=0):
    np.random.seed(seed)
    _w = jnp.asarray

    def _rec_inputs():
        import jax
        import jax.numpy as jnp
        _rk = jax.random.key(seed)
        x = -0.0002928 + 1 * jax.random.normal(jax.random.fold_in(_rk, 1), (32, 128, 256), jnp.float32)
        _lenS = 128 - jax.random.randint(jax.random.fold_in(_rk, 7), (32,), 0, max(1, 128 // 4) + 1, jnp.int32)
        _lenS2 = 128 - jax.random.randint(jax.random.fold_in(_rk, 8), (32,), 0, max(1, 128 // 4) + 1, jnp.int32)
        _ctx_1024P = jax.random.normal(jax.random.fold_in(_rk, 11), (32, 16, 256), jnp.float32)
        _ctx_1024c = jax.random.dirichlet(jax.random.fold_in(_rk, 511), 0.3 * jnp.ones((16,), jnp.float32), (32, 128))
        _ctx_1024t = jnp.einsum('bsk,bkd->bsd', _ctx_1024c, _ctx_1024P)
        _ctx_1024t = _ctx_1024t * jax.lax.rsqrt(jnp.mean(jnp.square(_ctx_1024t)) + 1e-12) * 0.953939
        ctx_1024 = -1.39393e-06 + 0.999914 * (_ctx_1024t + 0.3 * jax.random.normal(jax.random.fold_in(_rk, 611), (32, 128, 256), jnp.float32))
        return (x, ctx_1024)
    x, ctx_1024 = _rec_inputs()

    def _L0_xattn_setup():
        import jax, jax.numpy as jnp
        import numpy as np
        B, S, H, NH = (2, 512, 256, 4)
        DH = H // NH
        EPS = 1e-06

        def _parallel_stabilized(qh, kh, vh, ig, fg):
            log_fg = jax.nn.log_sigmoid(fg)
            cs = jnp.cumsum(log_fg, axis=2)
            ltr = jnp.tril(jnp.ones((qh.shape[2], qh.shape[2]), dtype=bool))
            log_fg_mat = jnp.where(ltr, cs - jnp.swapaxes(cs, 2, 3), -jnp.inf)
            log_D = log_fg_mat + jnp.swapaxes(ig, 2, 3)
            max_log_D = jnp.max(log_D, axis=-1, keepdims=True)
            D = jnp.exp(log_D - max_log_D)
            qk = jnp.einsum('bhsd,bhtd->bhst', qh, kh) / jnp.sqrt(jnp.float32(DH))
            C = qk * D
            normalizer = jnp.maximum(jnp.abs(jnp.sum(C, axis=-1, keepdims=True)), jnp.exp(-max_log_D))
            return jnp.einsum('bhst,bhtd->bhsd', C / (normalizer + EPS), vh)
        key = jax.random.key(seed)
        ks = jax.random.split(key, 6)
        q = jax.random.normal(ks[0], (B, S, H), dtype=jnp.float32)
        k = jax.random.normal(ks[1], (B, S, H), dtype=jnp.float32)
        v = jax.random.normal(ks[2], (B, S, H), dtype=jnp.float32)
        igate_kernel = jax.random.normal(ks[3], (3 * H, NH), dtype=jnp.float32) * 0.02
        fgate_kernel = jax.random.normal(ks[4], (3 * H, NH), dtype=jnp.float32) * 0.02
        igate_bias = jax.random.normal(ks[5], (NH,), dtype=jnp.float32) * 0.1
        fgate_bias = jnp.linspace(3.0, 6.0, NH, dtype=jnp.float32)
        outnorm_scale = jnp.ones((H,), dtype=jnp.float32)
        return {'q': q, 'k': k, 'v': v, 'igate_kernel': igate_kernel, 'igate_bias': igate_bias, 'fgate_kernel': fgate_kernel, 'fgate_bias': fgate_bias, 'outnorm_scale': outnorm_scale}
    _L0_xattn_all = _L0_xattn_setup()
    _L0_xattn_in = {k: v for k, v in _L0_xattn_all.items() if k in ('igate_kernel', 'igate_bias', 'fgate_kernel', 'fgate_bias', 'outnorm_scale')}
    del _L0_xattn_all

    def _L0_ffn_setup():
        import jax, jax.numpy as jnp
        import numpy as np
        N_EXPERTS = 8
        TOP_K = 2
        key = jax.random.key(seed)
        k1, k2, k3, k4 = jax.random.split(key, 4)
        B, T, C, H, E = (2, 512, 256, 1024, N_EXPERTS)
        x = jax.random.normal(k1, (B, T, C), dtype=jnp.float32)
        router_w = jax.random.normal(k2, (E, C), dtype=jnp.float32) * 0.02
        w1 = jax.random.normal(k3, (E, C, H), dtype=jnp.float32) * (1.0 / np.sqrt(C))
        w2 = jax.random.normal(k4, (E, H, C), dtype=jnp.float32) * (1.0 / np.sqrt(H))
        return {'x': x, 'router_w': router_w, 'w1': w1, 'w2': w2}
    _L0_ffn_all = _L0_ffn_setup()
    _L0_ffn_in = {k: v for k, v in _L0_ffn_all.items() if k in ('router_w', 'w1', 'w2')}
    del _L0_ffn_all
    return {'x': x, 'ctx_1024': ctx_1024, 'L0_xattn_igate_kernel': _L0_xattn_in['igate_kernel'], 'L0_xattn_igate_bias': _L0_xattn_in['igate_bias'], 'L0_xattn_fgate_kernel': _L0_xattn_in['fgate_kernel'], 'L0_xattn_fgate_bias': _L0_xattn_in['fgate_bias'], 'L0_xattn_outnorm_scale': _L0_xattn_in['outnorm_scale'], 'L0_ffn_router_w': _L0_ffn_in['router_w'], 'L0_ffn_w1': _L0_ffn_in['w1'], 'L0_ffn_w2': _L0_ffn_in['w2']}

def reference(x, ctx_1024, L0_xattn_igate_kernel, L0_xattn_igate_bias, L0_xattn_fgate_kernel, L0_xattn_fgate_bias, L0_xattn_outnorm_scale, L0_ffn_router_w, L0_ffn_w1, L0_ffn_w2):
    import jax
    import jax.numpy as jnp

    def _L0_xattn_ref(q, k, v, igate_kernel, igate_bias, fgate_kernel, fgate_bias, outnorm_scale):
        import jax, jax.numpy as jnp
        import numpy as np
        B, S, H, NH = (2, 512, 256, 4)
        DH = H // NH
        EPS = 1e-06

        def _parallel_stabilized(qh, kh, vh, ig, fg):
            log_fg = jax.nn.log_sigmoid(fg)
            cs = jnp.cumsum(log_fg, axis=2)
            ltr = jnp.tril(jnp.ones((qh.shape[2], qh.shape[2]), dtype=bool))
            log_fg_mat = jnp.where(ltr, cs - jnp.swapaxes(cs, 2, 3), -jnp.inf)
            log_D = log_fg_mat + jnp.swapaxes(ig, 2, 3)
            max_log_D = jnp.max(log_D, axis=-1, keepdims=True)
            D = jnp.exp(log_D - max_log_D)
            qk = jnp.einsum('bhsd,bhtd->bhst', qh, kh) / jnp.sqrt(jnp.float32(DH))
            C = qk * D
            normalizer = jnp.maximum(jnp.abs(jnp.sum(C, axis=-1, keepdims=True)), jnp.exp(-max_log_D))
            return jnp.einsum('bhst,bhtd->bhsd', C / (normalizer + EPS), vh)
        Bq, Sq, Hq = q.shape
        x = jnp.concatenate([q, k, v], axis=-1)
        ig = x @ igate_kernel + igate_bias
        fg = x @ fgate_kernel + fgate_bias
        ig = jnp.transpose(ig, (0, 2, 1))[..., None]
        fg = jnp.transpose(fg, (0, 2, 1))[..., None]
        qh = jnp.transpose(q.reshape(Bq, Sq, NH, DH), (0, 2, 1, 3))
        kh = jnp.transpose(k.reshape(Bq, Sq, NH, DH), (0, 2, 1, 3))
        vh = jnp.transpose(v.reshape(Bq, Sq, NH, DH), (0, 2, 1, 3))
        h = _parallel_stabilized(qh, kh, vh, ig, fg)
        mean = jnp.mean(h, axis=-1, keepdims=True)
        var = jnp.mean((h - mean) ** 2, axis=-1, keepdims=True)
        h_norm = (h - mean) * jax.lax.rsqrt(var + 1e-05)
        h_norm = h_norm * outnorm_scale.reshape(1, NH, 1, DH)
        out = jnp.transpose(h_norm, (0, 2, 1, 3)).reshape(Bq, Sq, Hq)
        return out

    def _L0_ffn_ref(x, router_w, w1, w2):
        import jax, jax.numpy as jnp
        import numpy as np
        N_EXPERTS = 8
        TOP_K = 2
        B, T, C = x.shape
        E = N_EXPERTS
        xf = x.reshape(-1, C)
        logits = jnp.einsum('nc,ec->ne', xf, router_w)
        probs = jax.nn.softmax(logits, axis=-1)
        top_w, top_i = jax.lax.top_k(probs, TOP_K)
        top_w = top_w / jnp.sum(top_w, axis=-1, keepdims=True)
        comb = jnp.einsum('nk,nke->ne', top_w, jax.nn.one_hot(top_i, E, dtype=xf.dtype))
        h = jax.nn.gelu(jnp.einsum('nc,ech->enh', xf, w1), approximate=False)
        y = jnp.einsum('enh,ehc->enc', h, w2)
        out = jnp.einsum('ne,enc->nc', comb, y)
        return out.reshape(B, T, C)
    x = x + _L0_xattn_ref(_layernorm(x, axis=-1), ctx_1024, ctx_1024, L0_xattn_igate_kernel, L0_xattn_igate_bias, L0_xattn_fgate_kernel, L0_xattn_fgate_bias, L0_xattn_outnorm_scale)
    x = x + _L0_ffn_ref(_layernorm(x, axis=-1), L0_ffn_router_w, L0_ffn_w1, L0_ffn_w2)
    return x

_drawn_inputs = setup_inputs


def setup_inputs(seed=0):
    import zlib

    import numpy as np

    out = dict(_drawn_inputs(seed))
    spreads = {'L0_xattn_outnorm_scale': (1.0, 0.2)}
    factors = {}
    for name, (base, spread) in spreads.items():
        noise = np.random.default_rng([zlib.crc32(name.encode()), seed]).standard_normal(out[name].shape)
        drawn = base * np.exp(spread * noise) if base else spread * noise
        out[name] = jnp.asarray(drawn.astype(out[name].dtype))
    for name, factor in factors.items():
        out[name] = (out[name] * factor).astype(out[name].dtype)
    return out
```

```python
from contextlib import ExitStack

import numpy as np

import concourse.bass as bass
from concourse import mybir

ALU = mybir.AluOpType
ACT = mybir.ActivationFunctionType
AX = mybir.AxisListType
F32, F16, BF16, I32 = mybir.dt.float32, mybir.dt.float16, mybir.dt.bfloat16, mybir.dt.int32

P = 128
NB, S, D = 32, 128, 256
NH, DH = 4, 64
NE, HID = 8, 1024
G = 4
NG = NB // G
NT = NB * S
CK = D // P
MK = HID // P
R = G * NH
PARTS = 3
KP = 32 * (PARTS - 1) + 32
ROW = D + 4
REGION = NT + P
RING = 3
TILES = -(-(2 * NT // P + NE - 1) // RING) * RING
SPARE = NE * REGION
WSCALE = 16.0
W1, W2 = CK * HID, MK * D
EPS = 1e-5
NEG = -1e30

C_IDENT = 0
C_W8 = C_IDENT + P
C_EBASE = C_W8 + NE
C_THR = C_EBASE + NE
C_TILE = C_THR + NB
C_TOK = C_TILE + TILES
C_F32 = C_TOK + G
B_IDENT = 0
B_MASK = B_IDENT + P
B_SEL = B_MASK + 2 * P
B_HSEL = B_SEL + G * P
B_HMASK = B_HSEL + G * NH * P
B_TRI = B_HMASK + NH
B_ONES = B_TRI + P
C_BF = B_ONES + P


def after(eng, sem, value):
    if isinstance(value, int) and value <= 0:
        return
    eng.wait_ge(sem, value)


def apart(eng, sem):
    eng.sem_inc(sem, 1)


def build(nc, x, ctx_in, ig_k, ig_b, fg_k, fg_b, gamma, router_w, w1, w2, cf, cb, pad_rows, out):
    with ExitStack() as stack:
        def sb(name, shape, dt=F32):
            return stack.enter_context(nc.sbuf_tensor(name, shape, dt))

        def ps(name, shape, dt=F32):
            return stack.enter_context(nc.psum_tensor(name, shape, dt))

        def sem(name):
            return stack.enter_context(nc.semaphore(name))

        rows = nc.dram_tensor("rows", (SPARE + P, ROW), F32, kind="Internal").ap()
        wsplit = nc.dram_tensor("wsplit", (NE, P, 2 * (W1 + W2)), F16, kind="Internal").ap()

        cst = sb("cst", [P, C_F32])
        cbf = sb("cbf", [P, C_BF], BF16)
        ident = cst[:, C_IDENT:C_IDENT + P]
        ident_h = sb("ident_h", [P, P], F16)
        tri_h = sb("tri_h", [P, P], F16)
        ones_h = sb("ones_h", [P, P], F16)
        pad = sb("pad", [P, ROW])
        gate_w = sb("gate_w", [P, 3 * CK, 2, NH])
        gate_b = sb("gate_b", [R, 2])
        gam = sb("gam", [P, D])
        rw = sb("rw", [NE, D])
        rwT = sb("rwT", [P, CK, NE])
        mhalf = sb("mhalf", [P, R])

        xt = [sb(f"xt{p}", [P, G, D]) for p in range(2)]
        vt = [sb(f"vt{p}", [P, G, NH, DH + 1]) for p in range(2)]
        xn = sb("xn", [P, G, D])
        st1 = sb("st1", [P, G, 6])
        mv1 = sb("mv1", [P, G, 2])
        ve1 = sb("ve1", [P, G])
        rs1 = sb("rs1", [P, G])
        qkT = [sb(f"qkT{p}", [P, G, 2 * CK, P]) for p in range(2)]
        gsb = sb("gsb", [P, 2 * R])
        ga = sb("ga", [R, P])
        ge = sb("ge", [R, P])
        gl_ = sb("gl_", [R, P])
        gmn = sb("gmn", [R, P])
        gcs = sb("gcs", [R, P])
        gm = sb("gm", [R, 2, P])
        gr = sb("gr", [R, 2, P])
        gr2 = sb("gr2", [R, 2, P])
        grb = sb("grb", [R, 2, P], BF16)
        gnm = sb("gnm", [R, P])
        parts = [sb(f"parts{p}", [KP, 2, P], BF16) for p in range(2)]
        mblk = [sb(f"mblk{p}", [KP, NH, P], BF16) for p in range(2)]
        en = [sb(f"en{p}", [P, R]) for p in range(2)]
        dt_ = [sb(f"dt{i}", [P, 2, 512]) for i in range(2)]
        ct = [sb(f"ct{i}", [P, 2, 512]) for i in range(2)]
        u = sb("u", [P, R, DH + 1])
        su = sb("su", [P, R])
        nmu = sb("nmu", [P, R])
        c_ = sb("c_", [P, R, DH])
        ss = sb("ss", [P, R])
        n0 = sb("n0", [P, R])
        n1 = sb("n1", [P, R])
        n2 = sb("n2", [P, R])
        hv = sb("hv", [P, R])
        hrs = sb("hrs", [P, R])
        x1 = [sb(f"x1_{p}", [P, G, D]) for p in range(2)]
        st2 = sb("st2", [P, G, 6])
        mv2 = sb("mv2", [P, G, 2])
        ve2 = sb("ve2", [P, G])
        rs2 = sb("rs2", [P, G])
        xn2 = sb("xn2", [P, G, D])
        sq = xn2[:, :, :].rearrange("p b (h d) -> p (b h) d", h=NH)
        ctn = sb("ctn", [P, G, D])
        rT = sb("rT", [P, G, CK, P])
        rowb = [sb(f"rowb{p}", [P, G, ROW]) for p in range(2)]
        lg = sb("lg", [P, G, NE])
        lg2 = sb("lg2", [P, G, NE])
        eq = sb("eq", [P, G, NE])
        key = sb("key", [P, G, NE])
        m1 = sb("m1", [P, G])
        m2 = sb("m2", [P, G])
        km1 = sb("km1", [P, G])
        km2 = sb("km2", [P, G])
        oh1 = sb("oh1", [P, G, NE])
        oh2 = sb("oh2", [P, G, NE])
        msk = sb("msk", [P, G, NE], F16)
        cum = sb("cum", [P, NE], F16)
        csum = sb("csum", [P, NE])
        sf = sb("sf", [P, 2, G])
        d21 = sb("d21", [P, G])
        e21 = sb("e21", [P, G])
        den = sb("den", [P, G])
        c1 = sb("c1", [P, G])
        c2 = sb("c2", [P, G])
        rb = sb("rb", [P, G, NE])
        a1 = sb("a1", [P, G, NE])
        a2 = sb("a2", [P, G, NE])
        slot = [sb(f"slot{p}", [P, 2, G], I32) for p in range(2)]
        tok = sb("tok", [P, G])
        wcv = [sb(f"wcv{p}", [P, 2 * (W1 + W2)], F16) for p in range(2)]
        wring = sb("wring", [P, RING, 2 * (W1 + W2)], F16)
        wst = [wring[:, p, :].bitcast(F32) for p in range(2)]

        te3 = xn2[:, :, :].rearrange("p r d -> p (r d)")[:, 0:NE * NB].rearrange("p (e j) -> p e j", e=NE)
        te = sb("te", [P, NE])
        ncnt = sb("ncnt", [P, NE])
        ctl = sb("ctl", [P, NE])
        wt = sb("wt", [P, NE])
        le, lw = (t[:, :, :].rearrange("p a n -> p (a n)")[:, 0:TILES * NE].rearrange("p (i e) -> p i e", e=NE)
                  for t in (dt_[0], ct[0]))
        idr = sb("idr", [P, TILES])
        etab = sb("etab", [P, TILES])
        adr = sb("adr", [P, TILES])
        ad2 = sb("ad2", [P, TILES])
        chg = sb("chg", [P, TILES])
        tab = sb("tab", [P, 3, TILES], I32)
        padr = sb("padr", [P, NE], I32)

        xrow = [sb(f"xrow{i}", [P, ROW]) for i in range(RING)]
        xT = [sb(f"xT{i}", [P, 2 * CK, P], F16) for i in range(RING)]
        gf = [dt_[1][:, a, :] for a in range(2)]
        gh = [sb(f"gh{a}", [P, 4, P], F16) for a in range(2)]
        gl = [sb(f"gl{a}", [P, 4, P], F16) for a in range(2)]
        cw0 = sb("cwd", [P, 1])
        cw = [sb(f"cw{i}", [P, 1]) for i in range(RING)]
        yc = sb("yc", [P, D])
        yo = [ct[1][:, :, :].rearrange("p a n -> p (a n)")[:, D * i:D * (i + 1)] for i in range(RING)]
        dst = [sb(f"dst{i}", [P, 1], I32) for i in range(RING)]

        bank = [ps(f"bank{i}", [P, 512]) for i in range(8)]
        T0, T1, KE, KO, DE, DO, UB, SF = bank
        TB, KB, DB = [T0, T1], [KE, KO], [DE, DO]

        s_cst = sem("constants_loaded")
        s_cbf = sem("selectors_cast")
        s_prep = sem("prepared_by_vector")
        s_prepg = sem("prepared_by_pool")
        s_rwt = sem("router_transposed")
        s_rwc = sem("router_copied")
        s_x = [sem(f"x_loaded{p}") for p in range(2)]
        s_c = sem("ctx_loaded")
        s_v = [sem(f"values_loaded{p}") for p in range(2)]
        s_wst = [sem(f"weights_loaded{p}") for p in range(2)]
        s_bn1 = sem("x_stats")
        s_mv1 = sem("x_mean_var")
        s_ve1 = sem("x_var_eps")
        s_rs1 = sem("x_rstd")
        s_xn = sem("x_normed")
        s_tq = sem("qk_transposed")
        s_qk = sem("qk_copied")
        s_gt = sem("gates_summed")
        s_gsb = sem("gates_copied")
        s_gT = sem("gates_transposed")
        s_ga = sem("gate_abs")
        s_ge = sem("gate_exp")
        s_gl = sem("gate_log")
        s_gmn = sem("gate_min")
        s_gcs = sem("gate_cumsum")
        s_ng = sem("gate_ng")
        s_gmx = sem("gate_cummax")
        s_gnm = sem("gate_neg_logd")
        s_pt = sem("gate_parts")
        s_gr = sem("gate_rests")
        s_mb = sem("gate_blocks")
        s_nT = sem("neg_logd_transposed")
        s_en = sem("neg_logd_exp")
        s_d = sem("logd_summed")
        s_dt = sem("decay_ready")
        s_kq = sem("kq_ready")
        s_ct = sem("scores_ready")
        s_pv = sem("pv_ready")
        s_u = sem("pv_copied")
        s_su = sem("pv_sum")
        s_nmu = sem("pv_neg_mean")
        s_cc = sem("pv_centred")
        s_sq = sem("pv_squared")
        s_ss = sem("pv_sumsq")
        s_n = sem("normaliser_steps")
        s_hrs = sem("head_rstd")
        s_tt = sem("head_scaled")
        s_tg = sem("head_gamma")
        s_x1 = sem("x1_ready")
        s_x1o = [sem(f"x1_stored{p}") for p in range(2)]
        s_bn2 = sem("x1_stats")
        s_mv2 = sem("x1_mean_var")
        s_ve2 = sem("x1_var_eps")
        s_rs2 = sem("x1_rstd")
        s_xn2 = sem("x1_normed")
        s_hi = sem("row_high")
        s_lo = sem("row_low")
        s_rt = sem("x1n_transposed")
        s_rTc = sem("x1n_T_copied")
        s_lg = sem("logits_ready")
        s_rk = sem("router_steps")
        s_km = sem("top_two_steps")
        s_sl = sem("slot_steps")
        s_sf = sem("slot_sums")
        s_cu = sem("count_steps")
        s_mt = sem("meta_steps")
        s_msk = sem("expert_masks")
        s_e21 = sem("router_exp")
        s_rank = sem("ranks_ready")
        s_slot = sem("slots_ready")
        s_meta = sem("row_meta")
        s_sc = [sem(f"rows_scattered{p}") for p in range(2)]
        s_w16 = sem("weights_scaled")
        s_wh = sem("weights_high")
        s_wl = sem("weights_low")
        s_wo = [sem(f"weights_stored{p}") for p in range(2)]
        s_cnt = sem("counts_ready")
        s_tb = sem("table_steps")
        s_tab = sem("table_ready")
        s_pad = sem("pads_stored")
        s_init = sem("spare_rows_stored")
        s_xr = [sem(f"tile_loaded{i}") for i in range(RING)]
        s_wr = [sem(f"tile_weights{i}") for i in range(RING)]
        s_xtp = sem("tile_transposed")
        s_xtc = sem("tile_T_copied")
        s_h = sem("hidden_ready")
        s_gf = sem("gelu_full")
        s_gh = sem("gelu_high")
        s_glo = sem("gelu_low")
        s_m2 = sem("out_half_done")
        s_cw0 = sem("row_weight_step")
        s_cw = sem("row_weight")
        s_yc = sem("out_cross_copied")
        s_yo = sem("out_ready")
        s_sa = sem("out_added")
        s_apart = {n: sem(f"waits_apart_{n}") for n in ("pe", "dve", "pool")}
        N_CST = 16 * (7 + 2 * G)

        def groups(eng, front, back):
            front(0, 0, 0)
            front(1, 1, 0)
            back(0, 0, 0)
            front(2, 0, 1)
            back(1, 1, 0)
            with eng.Fori(1, NG // 2 - 1) as q:
                front(2 * q + 1, 1, q)
                back(2 * q, 0, q)
                front(2 * q + 2, 0, q + 1)
                back(2 * q + 1, 1, q)
            front(NG - 1, 1, NG // 2 - 1)
            back(NG - 2, 0, NG // 2 - 1)
            back(NG - 1, 1, NG // 2 - 1)

        def tiles(eng, tile):
            for i in range(RING):
                tile(i, i, 0)
            with eng.Fori(1, TILES // RING - 1) as it:
                for i in range(RING):
                    tile(RING * it + i, i, it)
            for i in range(RING):
                tile(TILES - RING + i, i, TILES // RING - 1)

        block = stack.enter_context(nc.Block())

        @block.sync
        def _(sp):
            gk_i = ig_k.rearrange("(c p) h -> p c h", p=P)
            gk_f = fg_k.rearrange("(c p) h -> p c h", p=P)
            sp.dma_start(xt[0][:, :, :], x[0:G].rearrange("b p d -> p b d")).then_inc(s_x[0], 16)
            sp.dma_start(cst[:, :], cf).then_inc(s_cst, 16)
            sp.dma_start(gate_w[:, :, 0, :], gk_i).then_inc(s_cst, 16)
            sp.dma_start(gate_w[:, :, 1, :], gk_f).then_inc(s_cst, 16)
            for b in range(G):
                sp.dma_start(gate_b[NH * b:NH * b + NH, 0:1], ig_b.rearrange("(h o) -> h o", o=1)).then_inc(s_cst, 16)
                sp.dma_start(gate_b[NH * b:NH * b + NH, 1:2], fg_b.rearrange("(h o) -> h o", o=1)).then_inc(s_cst, 16)
            sp.dma_start(wring[:, RING - 1, :].bitcast(F32)[:, 0:C_BF], cb).then_inc(s_cst, 16)
            sp.dma_start(gam[:, :], gamma.rearrange("(o d) -> o d", o=1).to_broadcast([P, D])).then_inc(s_cst, 16)
            sp.dma_start(rw[:, :], router_w).then_inc(s_cst, 16)
            sp.dma_start(pad[:, :], pad_rows).then_inc(s_cst, 16)

            def front(g, p, q):
                first = isinstance(g, int) and g == 0
                after(sp, s_x1, g - 1)
                if not first:
                    sp.dma_start(xt[p][:, :, :], x[bass.ds(g * G, G)].rearrange("b p d -> p b d")).then_inc(s_x[p], 16)
                after(sp, s_tq, G * g)
                sp.dma_start(ctn[:, :, :], ctx_in[bass.ds(g * G, G)].rearrange("b p d -> p b d")).then_inc(s_c, 16)
                after(sp, s_pv, G * (g - 1))
                for b in range(G):
                    sp.dma_start(vt[p][:, b, :, 0:DH],
                                 ctx_in[bass.ds(g * G + b, 1)].rearrange("o p (h d) -> (o p) h d", h=NH)
                                 ).then_inc(s_v[p], 16)
                after(sp, s_wl, 2 * (g - 1))
                sp.dma_start(wst[p][:, 0:W1].rearrange("p (c n) -> p c n", c=CK),
                             w1[bass.ds(g, 1)].rearrange("o (c p) n -> p (o c) n", p=P)).then_inc(s_wst[p], 16)
                sp.dma_start(wst[p][:, W1:W1 + W2].rearrange("p (m n) -> p m n", m=MK),
                             w2[bass.ds(g, 1)].rearrange("o (m p) n -> p (o m) n", p=P)).then_inc(s_wst[p], 16)

            def back(g, p, q):
                sp.wait_ge(s_x1, g + 1)
                sp.dma_start(out[bass.ds(g * G * P, G * P), :].rearrange("(b p) d -> p b d", p=P),
                             x1[p][:, :, :]).then_inc(s_x1o[p], 16)
                sp.wait_ge(s_wl, 2 * (g + 1))
                sp.wait_ge(s_wh, 2 * (g + 1))
                sp.dma_start(wsplit[bass.ds(g, 1)].rearrange("o p n -> (o p) n"), wcv[p][:, :]).then_inc(s_wo[p], 16)

            sp.wait_ge(s_cst, N_CST)
            sp.dma_start(rows[SPARE:SPARE + P, :], pad[:, :]).then_inc(s_init, 16)
            sp.wait_ge(s_prep, 5)
            sp.dma_start(out[NT:NT + P, :], yc[:, :]).then_inc(s_init, 16)
            groups(sp, front, back)

            sp.wait_ge(s_tab, 1)
            for p in range(2):
                sp.wait_ge(s_sc[p], 16 * 2 * G * NG // 2)
                sp.wait_ge(s_wo[p], 16 * NG // 2)
            for e in range(NE):
                r = sp.value_load(padr[0:1, e:e + 1], min_val=e * REGION, max_val=e * REGION + NT)
                sp.dma_start(rows[bass.ds(r, P), :], pad[:, :]).then_inc(s_pad, 16)
            sp.wait_ge(s_pad, 16 * NE)
            sp.wait_ge(s_init, 32)

            def tile(i, k, it):
                after(sp, s_xtp, i - RING + 1)
                after(sp, s_cw, i - RING + 1)
                r = sp.value_load(tab[0:1, 1, bass.ds(i, 1)], min_val=0, max_val=SPARE)
                sp.dma_start(xrow[k][:, :], rows[bass.ds(r, P), :]).then_inc(s_xr[k], 16)
                after(sp, s_m2, 2 * (i - RING + 1))
                e = sp.value_load(tab[0:1, 0, bass.ds(i, 1)], min_val=0, max_val=NE - 1)
                need = sp.value_load(tab[0:1, 2, bass.ds(i, 1)], min_val=0, max_val=1)
                sp.dma_start(wring[:, k, :], wsplit[bass.ds(e, 1)].rearrange("o p n -> (o p) n"),
                             cond=need).then_inc(s_wr[k], 16)

            tiles(sp, tile)
            sp.wait_ge(s_sa, 16 * TILES)

        @block.tensor
        def _(pe):
            pe.wait_ge(s_cst, N_CST)
            for c in range(CK):
                mm = pe.transpose(SF[:, c * NE:(c + 1) * NE], rw[:, c * P:(c + 1) * P], ident[0:NE, 0:NE])
            mm.then_inc(s_rwt, 1)
            pe.wait_ge(s_rwc, 1)
            pe.wait_ge(s_prep, 6)
            pe.wait_ge(s_prepg, 3)

            def front(g, p, q):
                pe.wait_ge(s_c, 16 * (g + 1))

                def turn(b):
                    pe.wait_ge(s_xn, G * g + b + 1)
                    after(pe, s_qk, G * g + b - 1)
                    for j in range(CK):
                        pe.transpose(TB[b % 2][:, j * P:(j + 1) * P], xn[:, b, j * P:(j + 1) * P], ident)
                    for j in range(CK):
                        mm = pe.transpose(TB[b % 2][:, (CK + j) * P:(CK + j + 1) * P],
                                          ctn[:, b, j * P:(j + 1) * P], ident)
                    mm.then_inc(s_tq, 1)

                def gates(b):
                    pe.wait_ge(s_qk, G * g + b + 1)
                    dst_ = SF[:, 0:2 * R].rearrange("p (i r) -> p i r", i=2)[:, :, NH * b:NH * (b + 1)]
                    for j in range(2 * CK):
                        mm = pe.matmul(dst_, qkT[p][:, b, j, :], gate_w[:, j, :, :], start=(j == 0),
                                       stop=(j == 2 * CK - 1))
                    mm.then_inc(s_gt, 1)

                turn(0)
                turn(1)
                after(pe, s_en, g)
                gates(0)
                turn(2)
                gates(1)
                turn(3)
                gates(2)
                gates(3)
                pe.wait_ge(s_gsb, g + 1)
                for i in range(2):
                    mm = pe.transpose(SF[0:R, P + i * P:2 * P + i * P], gsb[:, i * R:(i + 1) * R], ident)
                mm.then_inc(s_gT, 1)
                pe.wait_ge(s_gnm, g + 1)
                apart(pe, s_apart["pe"])
                pe.transpose(SF[:, 3 * P:3 * P + R], gnm[:, :], ident[0:R, 0:R]).then_inc(s_nT, 1)

            def back(g, p, q):
                def logd(h):
                    after(pe, s_dt, 2 * (2 * g + h))
                    if h == 0:
                        pe.wait_ge(s_mb, g + 1)
                        pe.wait_ge(s_pt, PARTS * (g + 1))
                    for par in range(2):
                        for b2 in range(2):
                            b = 2 * h + b2
                            o = DB[par][:, b2 * 2 * P:(b2 + 1) * 2 * P]
                            hs = B_HSEL + (b * 2 + par) * 2 * P
                            pe.matmul(o, cbf[0:KP, B_SEL + b * P:B_SEL + (b + 1) * P],
                                      mblk[p][:, 2 * par:2 * par + 2, :], start=True, stop=False)
                            pe.matmul(o, parts[p][:, 0, :], cbf[0:KP, hs:hs + 2 * P], start=False, stop=False)
                            mm = pe.matmul(o, cbf[:, B_IDENT:B_IDENT + P], cbf[:, B_MASK:B_MASK + 2 * P],
                                           start=False, stop=True)
                        mm.then_inc(s_d, 1)

                def scores(h):
                    after(pe, s_ct, 2 * (2 * g + h))
                    if h == 0:
                        after(pe, s_rTc, 2 * g)
                    for b2 in range(2):
                        b = 2 * h + b2
                        for hp in range(2):
                            for par in range(2):
                                rows_ = slice(DH * par, DH * par + DH)
                                o = KB[par][:, (2 * b2 + hp) * P:(2 * b2 + hp + 1) * P]
                                mm = pe.matmul(o, qkT[p][rows_, b, CK + hp, :], qkT[p][rows_, b, hp, :],
                                               start=True, stop=True)
                    mm.then_inc(s_kq, 1)

                def values(h):
                    pe.wait_ge(s_ct, 2 * (2 * g + h + 1))
                    pe.wait_ge(s_v[p], 16 * G * (q + 1))
                    for b2 in range(2):
                        b = 2 * h + b2
                        after(pe, s_u, G * g + b)
                        if b == 0:
                            after(pe, s_slot, 2 * g)
                        for h4 in range(NH):
                            c0 = (2 * b2 + h4 // 2) * P
                            mm = pe.matmul(UB[:, h4 * (DH + 1):(h4 + 1) * (DH + 1)],
                                           ct[h][:, h4 % 2, c0:c0 + P], vt[p][:, b, h4, :],
                                           start=True, stop=True)
                        mm.then_inc(s_pv, 1)

                logd(0)
                scores(0)
                logd(1)
                scores(1)
                values(0)
                values(1)
                for h in range(2):
                    pe.wait_ge(s_xn2, G * g + 2 * h + 2)
                    pe.wait_ge(s_ct, 2 * (2 * g + 2))
                    for b2 in range(2):
                        for j in range(CK):
                            mm = pe.transpose(KB[h][:, (2 * b2 + j) * P:(2 * b2 + j + 1) * P],
                                              xn2[:, 2 * h + b2, j * P:(j + 1) * P], ident)
                    mm.then_inc(s_rt, 1)
                pe.wait_ge(s_u, G * (g + 1))
                for b in range(G):
                    pe.wait_ge(s_rTc, 2 * g + b // 2 + 1)
                    for j in range(CK):
                        mm = pe.matmul(UB[:, b * NE:(b + 1) * NE], rT[:, b, j, :], rwT[:, j, :],
                                       start=(j == 0), stop=(j == CK - 1))
                mm.then_inc(s_lg, 1)
                pe.wait_ge(s_msk, g + 1)
                rk = UB[:, P:P + G * NE]
                pe.matmul(rk, tri_h[:, :], msk[:, :, :], start=True, stop=False, skip_group_check=True)
                for n in range(1, G):
                    pe.matmul(UB[:, P + n * NE:P + G * NE], ones_h[:, :], msk[:, 0:G - n, :], start=False,
                              stop=False, skip_group_check=True)
                for b in range(G):
                    mm = pe.matmul(UB[:, P + b * NE:P + (b + 1) * NE], ones_h[:, :], cum[:, :], start=False,
                                   stop=(b == G - 1), skip_group_check=True)
                mm.then_inc(s_rank, 1)

            groups(pe, front, back)

            pe.wait_ge(s_meta, NG)
            pe.matmul(T0[:, 0:NE], ones_h[:, :], cum[:, :], start=True, stop=True).then_inc(s_cnt, 1)

            XP, YP, HPS = SF, [KE, KO, UB], [DE, DO]
            xp = XP[:, 0:CK * P].bitcast(F16)

            def turn(i, k, it):
                pe.wait_ge(s_xr[k], 16 * (it + 1))
                after(pe, s_xtc, i)
                xr = xrow[k][:, :].bitcast(F16)
                for j in range(2 * CK):
                    mm = pe.transpose(xp[:, j * P:(j + 1) * P], xr[:, j * P:(j + 1) * P], ident_h[:, :])
                mm.then_inc(s_xtp, 1)

            def hidden(i, k, it, a):
                if a == 0:
                    pe.wait_ge(s_wr[k], 16 * (it + 1))
                    pe.wait_ge(s_xtc, i + 1)
                after(pe, s_gf, 2 * i + a - 1)
                after(pe, s_gh, 2 * i + a - 1)
                for m4 in range(4):
                    m = 4 * a + m4
                    o = HPS[a][:, m4 * P:(m4 + 1) * P]
                    for c in range(CK):
                        hi = wring[:, k, c * HID + m * P:c * HID + (m + 1) * P]
                        lo = wring[:, k, W1 + c * HID + m * P:W1 + c * HID + (m + 1) * P]
                        pe.matmul(o, hi, xT[k][:, c, :], start=(c == 0), stop=False)
                        pe.matmul(o, hi, xT[k][:, CK + c, :], start=False, stop=False)
                        mm = pe.matmul(o, lo, xT[k][:, c, :], start=False, stop=(c == CK - 1))
                mm.then_inc(s_h, 1)

            def output(i, k, a):
                pe.wait_ge(s_gh, 2 * i + a + 1)
                pe.wait_ge(s_glo, 2 * i + a + 1)
                if a == 0:
                    after(pe, s_yo, i - RING + 1)
                for m4 in range(4):
                    w = 2 * W1 + (4 * a + m4) * 2 * D
                    pe.matmul(YP[k][:, 0:2 * D], gh[a][:, m4, :], wring[:, k, w:w + 2 * D],
                              start=(a == 0 and m4 == 0), stop=False, skip_group_check=True)
                    mm = pe.matmul(YP[k][:, D:2 * D], gl[a][:, m4, :], wring[:, k, w:w + D],
                                   start=False, stop=(a == 1 and m4 == 3), skip_group_check=True)
                mm.then_inc(s_m2, 1)

            def tile(i, k, it):
                hidden(i, k, it, 0)
                if not (isinstance(i, int) and i == 0):
                    output(i - 1, (k - 1) % RING, 1)
                hidden(i, k, it, 1)
                if not (isinstance(i, int) and i == TILES - 1):
                    turn(i + 1, (k + 1) % RING, it + (k + 1) // RING)
                output(i, k, 0)

            pe.wait_ge(s_slot, 2 * NG)
            turn(0, 0, 0)
            tiles(pe, tile)
            output(TILES - 1, RING - 1, 1)

        @block.scalar
        def _(act):
            def front(g, p, q):
                for b in range(G):
                    act.wait_ge(s_tq, G * g + b + 1)
                    if b == 0:
                        after(act, s_kq, 2 * (g - 1))
                    act.activation(qkT[p][:, b, :, :], TB[b % 2][:, :].rearrange("p (j n) -> p j n", j=2 * CK),
                                   ACT.Copy).then_inc(s_qk, 1)
                act.wait_ge(s_gT, g + 1)
                after(act, s_gcs, g)
                act.activation(ga[:, :], SF[0:R, 2 * P:3 * P], ACT.Abs, bias=gate_b[:, 1:2]).then_inc(s_ga, 1)
                act.wait_ge(s_ga, g + 1)
                act.activation(ge[:, :], ga[:, :], ACT.Exp, scale=-1.0).then_inc(s_ge, 1)
                act.wait_ge(s_ge, g + 1)
                act.activation(gl_[:, :], ge[:, :], ACT.Ln, bias=1.0).then_inc(s_gl, 1)
                act.wait_ge(s_nT, g + 1)
                after(act, s_n, 5 * (g - 1))
                act.activation(en[p][:, :], SF[:, 3 * P:3 * P + R], ACT.Exp).then_inc(s_en, 1)

            def back(g, p, q):
                for h in range(2):
                    for par in range(2):
                        act.wait_ge(s_d, 2 * (2 * g + h) + par + 1)
                        after(act, s_ct, 2 * (2 * g + h - 2) + par + 1)
                        act.activation(dt_[h][:, par, :], DB[par][:, :], ACT.Exp).then_inc(s_dt, 1)
                for b in range(G):
                    act.wait_ge(s_pv, G * g + b + 1)
                    if b == 0:
                        after(act, s_cc, g)
                        after(act, s_n, 5 * g)
                        after(act, s_su, g)
                    act.activation(u[:, NH * b:NH * (b + 1), :],
                                   UB[:, 0:NH * (DH + 1)].rearrange("p (h d) -> p h d", h=NH),
                                   ACT.Copy).then_inc(s_u, 1)
                act.wait_ge(s_cc, g + 1)
                after(act, s_rt, 2 * g)
                after(act, s_lo, g)
                after(act, s_hi, g)
                act.activation(sq, c_[:, :, :], ACT.Square).then_inc(s_sq, 1)
                act.wait_ge(s_wst[p], 32 * (q + 1))
                after(act, s_wo[p], 16 * q)
                for n, (a, w) in enumerate(((0, W1), (W1, W2))):
                    act.activation(wst[p][:, a:a + w], wst[p][:, a:a + w], ACT.Copy, scale=WSCALE).then_inc(s_w16, 1)
                    act.wait_ge(s_w16, 2 * g + n + 1)
                    if n == 0:
                        o, src = wcv[p][:, 0:W1], wst[p][:, 0:W1]
                    else:
                        o = wcv[p][:, 2 * W1:].rearrange("p (m k n) -> p m k n", m=MK, k=2)[:, :, 0, :]
                        src = wst[p][:, W1:W1 + W2].rearrange("p (m n) -> p m n", m=MK)
                    act.activation(o, src, ACT.Copy).then_inc(s_wh, 1)
                act.wait_ge(s_xn2, G * (g + 1))
                after(act, s_sc[p], 16 * 2 * G * q)
                act.activation(rowb[p][:, :, 0:D // 2].bitcast(F16), xn2[:, :, :], ACT.Copy).then_inc(s_hi, 1)
                for h in range(2):
                    act.wait_ge(s_rt, 2 * g + h + 1)
                    if h == 0:
                        after(act, s_lg, g)
                    act.activation(rT[:, 2 * h:2 * h + 2, :, :],
                                   KB[h][:, :].rearrange("p (b j n) -> p b j n", b=2, j=CK),
                                   ACT.Copy).then_inc(s_rTc, 1)
                act.wait_ge(s_rk, 10 * g + 8)
                after(act, s_meta, g)
                act.activation(e21[:, :], d21[:, :], ACT.Exp).then_inc(s_e21, 1)

            act.wait_ge(s_cst, N_CST)
            groups(act, front, back)

            HPS, YP = [DE, DO], [KE, KO, UB]

            def gelu(i, a):
                act.wait_ge(s_h, 2 * i + a + 1)
                after(act, s_glo, 2 * i + a - 1)
                act.activation(gf[a], HPS[a][:, :], ACT.Gelu, scale=1.0 / WSCALE).then_inc(s_gf, 1)
                after(act, s_m2, 2 * i + a - 1)
                act.activation(gh[a][:, :, :], HPS[a][:, :].rearrange("p (m n) -> p m n", m=4), ACT.Gelu,
                               scale=1.0 / WSCALE).then_inc(s_gh, 1)

            def cross(i, k):
                act.wait_ge(s_m2, 2 * i + 2)
                act.wait_ge(s_cw, i + 1)
                after(act, s_yo, i)
                act.activation(yc[:, :], YP[k][:, D:2 * D], ACT.Copy, scale=cw[k][:, :]).then_inc(s_yc, 1)

            def tile(i, k, it):
                gelu(i, 0)
                if not (isinstance(i, int) and i == 0):
                    cross(i - 1, (k - 1) % RING)
                gelu(i, 1)

            act.wait_ge(s_init, 32)
            act.wait_ge(s_ct, 4 * NG)
            tiles(act, tile)
            cross(TILES - 1, RING - 1)

        @block.vector
        def _(dve):
            dve.memset(yc[:, :], 0.0).then_inc(s_prep, 1)
            for p in range(2):
                dve.memset(parts[p][:, :, :], 0.0).then_inc(s_prep, 1)
            dve.memset(cum[:, :], 0.0).then_inc(s_prep, 1)
            dve.wait_ge(s_cst, N_CST)
            dve.tensor_tensor(gate_w[:, CK:2 * CK, :, :], gate_w[:, CK:2 * CK, :, :],
                              gate_w[:, 2 * CK:3 * CK, :, :], ALU.add).then_inc(s_prep, 1)
            dve.tensor_copy(cbf[:, :], wring[:, RING - 1, :].bitcast(F32)[:, 0:C_BF]).then_inc(s_cbf, 1)
            dve.wait_ge(s_rwt, 1)
            dve.tensor_copy(rwT[:, :, :], SF[:, 0:CK * NE].rearrange("p (c e) -> p c e", c=CK)).then_inc(s_rwc, 1)
            dve.wait_ge(s_prep, 5)

            def front(g, p, q):
                dve.wait_ge(s_x[p], 16 * (q + 1))
                for b in range(G):
                    after(dve, s_mv1, G * (g - 1) + b + 1)
                    dve.bn_stats(st1[:, b, :], xt[p][:, b, :]).then_inc(s_bn1, 1)
                after(dve, s_xn, G * g)
                after(dve, s_ve1, g)
                for b in range(G):
                    dve.wait_ge(s_bn1, G * g + b + 1)
                    apart(dve, s_apart["dve"])
                    dve.bn_aggr(mv1[:, b, :], st1[:, b, :]).then_inc(s_mv1, 1)
                dve.wait_ge(s_rs1, g + 1)
                after(dve, s_tq, G * g)
                for b in range(G):
                    dve.tensor_scalar(xn[:, b, :], xt[p][:, b, :], mv1[:, b, 0:1], rs1[:, b:b + 1],
                                      ALU.subtract, ALU.mult).then_inc(s_xn, 1)
                dve.wait_ge(s_gt, G * (g + 1))
                after(dve, s_gT, g)
                dve.tensor_copy(gsb[:, :], SF[:, 0:2 * R]).then_inc(s_gsb, 1)
                dve.wait_ge(s_gT, g + 1)
                dve.wait_ge(s_ga, g + 1)
                dve.tensor_scalar(gmn[:, :], SF[0:R, 2 * P:3 * P], gate_b[:, 1:2], 0.0, ALU.add, ALU.min
                                  ).then_inc(s_gmn, 1)
                dve.wait_ge(s_gl, g + 1)
                dve.wait_ge(s_gmn, g + 1)
                dve.tensor_tensor_scan(gcs[:, :], gmn[:, :], gl_[:, :], 0.0, ALU.add, ALU.subtract).then_inc(s_gcs, 1)
                dve.wait_ge(s_gcs, g + 1)
                dve.tensor_scalar(gnm[:, :], SF[0:R, P:2 * P], gate_b[:, 0:1], -1.0, ALU.add, ALU.mult
                                  ).then_inc(s_ng, 1)
                dve.wait_ge(s_ng, 2 * g + 1)
                dve.tensor_tensor(gm[:, 0, :], gnm[:, :], gcs[:, :], ALU.add).then_inc(s_ng, 1)
                dve.wait_ge(s_ng, 2 * g + 2)
                dve.tensor_tensor_scan(gm[:, 1, :], gm[:, 0, :], gm[:, 0, :], 3e38, ALU.min, ALU.min).then_inc(s_gmx, 1)
                dve.wait_ge(s_gmx, g + 1)
                dve.tensor_tensor(gnm[:, :], gm[:, 1, :], gcs[:, :], ALU.subtract).then_inc(s_gnm, 1)
                after(dve, s_d, 4 * (g - 1))
                dve.tensor_copy(parts[p][0:R, :, :], gm[:, :, :]).then_inc(s_pt, 1)
                dve.wait_ge(s_pt, PARTS * g + 1)
                dve.tensor_tensor(gr[:, :, :], gm[:, :, :], parts[p][0:R, :, :], ALU.subtract).then_inc(s_gr, 1)
                dve.wait_ge(s_gr, 3 * g + 1)
                dve.tensor_copy(parts[p][32:32 + R, :, :], gr[:, :, :]).then_inc(s_pt, 1)
                dve.tensor_copy(grb[:, :, :], gr[:, :, :]).then_inc(s_gr, 1)
                dve.wait_ge(s_gr, 3 * g + 2)
                dve.tensor_tensor(gr2[:, :, :], gr[:, :, :], grb[:, :, :], ALU.subtract).then_inc(s_gr, 1)
                dve.wait_ge(s_gr, 3 * g + 3)
                dve.tensor_copy(parts[p][64:64 + R, :, :], gr2[:, :, :]).then_inc(s_pt, 1)
                dve.wait_ge(s_pt, PARTS * (g + 1))
                dve.tensor_tensor(mblk[p][:, :, :], parts[p][:, 1:2, :].to_broadcast([KP, NH, P]),
                                  cbf[0:KP, B_HMASK:B_HMASK + NH].unsqueeze(2).to_broadcast([KP, NH, P]),
                                  ALU.mult).then_inc(s_mb, 1)

            def back(g, p, q):
                for h in range(2):
                    dve.wait_ge(s_kq, 2 * g + h + 1)
                    after(dve, s_pv, G * (g - 1) + 2 * h + 2)
                    for par in range(2):
                        dve.wait_ge(s_dt, 2 * (2 * g + h) + par + 1)
                        dve.scalar_tensor_tensor(ct[h][:, par, :], KB[par][:, :], DH ** -0.5, dt_[h][:, par, :],
                                                 ALU.mult, ALU.mult).then_inc(s_ct, 1)
                dve.wait_ge(s_u, G * (g + 1))
                after(dve, s_nmu, g)
                dve.reduce_sum(su[:, :], u[:, :, 0:DH], AX.X).then_inc(s_su, 1)
                dve.wait_ge(s_su, g + 1)
                after(dve, s_cc, g)
                dve.tensor_scalar(nmu[:, :], su[:, :], -1.0 / DH, None, ALU.mult).then_inc(s_nmu, 1)
                dve.wait_ge(s_en, g + 1)
                dve.scalar_tensor_tensor(n0[:, :], u[:, :, DH], -1.0, u[:, :, DH], ALU.mult, ALU.max
                                         ).then_inc(s_n, 1)
                dve.wait_ge(s_n, 5 * g + 1)
                dve.tensor_tensor(n2[:, :], n0[:, :], en[p][:, :], ALU.max).then_inc(s_n, 1)
                dve.wait_ge(s_n, 5 * g + 2)
                dve.tensor_scalar(n1[:, :], n2[:, :], 1e-6, None, ALU.add).then_inc(s_n, 1)
                dve.wait_ge(s_n, 5 * g + 3)
                dve.scalar_tensor_tensor(n2[:, :], n1[:, :], EPS, n1[:, :], ALU.mult, ALU.mult).then_inc(s_n, 1)
                dve.wait_ge(s_sq, g + 1)
                dve.reduce_sum(ss[:, :], sq, AX.X).then_inc(s_ss, 1)
                dve.wait_ge(s_ss, g + 1)
                dve.wait_ge(s_n, 5 * g + 4)
                after(dve, s_hrs, g)
                dve.scalar_tensor_tensor(hv[:, :], ss[:, :], 1.0 / DH, n2[:, :], ALU.mult, ALU.add).then_inc(s_n, 1)
                dve.wait_ge(s_hrs, g + 1)
                dve.tensor_tensor(c_[:, :, :], c_[:, :, :], hrs[:, :].unsqueeze(2).to_broadcast([P, R, DH]),
                                  ALU.mult).then_inc(s_tt, 1)
                dve.wait_ge(s_x1, g + 1)
                for b in range(G):
                    after(dve, s_mv2, G * (g - 1) + b + 1)
                    dve.bn_stats(st2[:, b, :], x1[p][:, b, :]).then_inc(s_bn2, 1)
                after(dve, s_xn2, G * g)
                after(dve, s_ve2, g)
                for b in range(G):
                    dve.wait_ge(s_bn2, G * g + b + 1)
                    apart(dve, s_apart["dve"])
                    dve.bn_aggr(mv2[:, b, :], st2[:, b, :]).then_inc(s_mv2, 1)
                dve.wait_ge(s_rs2, g + 1)
                after(dve, s_rt, 2 * g)
                after(dve, s_hi, g)
                after(dve, s_lo, g)
                for b in range(G):
                    dve.tensor_scalar(xn2[:, b, :], x1[p][:, b, :], mv2[:, b, 0:1], rs2[:, b:b + 1],
                                      ALU.subtract, ALU.mult).then_inc(s_xn2, 1)
                w8 = cst[:, C_W8:C_W8 + NE].unsqueeze(1).to_broadcast([P, G, NE])

                def spread(t):
                    return t[:, :].unsqueeze(2).to_broadcast([P, G, NE])

                step = [0]

                def link(ins):
                    step[0] += 1
                    ins.then_inc(s_rk, 1)
                    dve.wait_ge(s_rk, 10 * g + step[0])

                dve.wait_ge(s_lg, g + 1)
                after(dve, s_rk, 10 * g)
                link(dve.tensor_copy(lg[:, :, :], UB[:, 0:G * NE].rearrange("p (b e) -> p b e", b=G)))
                link(dve.reduce_max(m1[:, :], lg[:, :, :], AX.X))
                link(dve.tensor_tensor(eq[:, :, :], lg[:, :, :], spread(m1), ALU.is_equal))
                link(dve.tensor_tensor(key[:, :, :], eq[:, :, :], w8, ALU.mult))
                dve.reduce_max(km1[:, :], key[:, :, :], AX.X).then_inc(s_km, 1)
                dve.wait_ge(s_km, 4 * g + 1)
                dve.tensor_tensor(oh1[:, :, :], w8, spread(km1), ALU.is_equal).then_inc(s_km, 1)
                dve.wait_ge(s_km, 4 * g + 2)
                link(dve.scalar_tensor_tensor(lg2[:, :, :], oh1[:, :, :], -3e38, lg[:, :, :], ALU.mult, ALU.add))
                link(dve.reduce_max(m2[:, :], lg2[:, :, :], AX.X))
                link(dve.tensor_tensor(eq[:, :, :], lg2[:, :, :], spread(m2), ALU.is_equal))
                link(dve.tensor_tensor(d21[:, :], m2[:, :], m1[:, :], ALU.subtract))
                link(dve.tensor_tensor(key[:, :, :], eq[:, :, :], w8, ALU.mult))
                dve.reduce_max(km2[:, :], key[:, :, :], AX.X).then_inc(s_km, 1)
                dve.wait_ge(s_km, 4 * g + 3)
                dve.tensor_tensor(oh2[:, :, :], w8, spread(km2), ALU.is_equal).then_inc(s_km, 1)
                dve.wait_ge(s_km, 4 * g + 4)
                link(dve.tensor_tensor(key[:, :, :], oh1[:, :, :], oh2[:, :, :], ALU.add))
                dve.tensor_copy(msk[:, :, :], key[:, :, :]).then_inc(s_msk, 1)
                dve.wait_ge(s_rank, g + 1)
                dve.tensor_tensor(rb[:, :, :], UB[:, P:P + G * NE].rearrange("p (b e) -> p b e", b=G),
                                  cst[:, C_EBASE:C_EBASE + NE].unsqueeze(1).to_broadcast([P, G, NE]),
                                  ALU.add).then_inc(s_sl, 1)
                dve.reduce_sum(csum[:, :], key[:, :, :].rearrange("p b e -> p e b"), AX.X).then_inc(s_cu, 1)
                dve.wait_ge(s_cu, 2 * g + 1)
                dve.tensor_tensor(cum[:, :], cum[:, :], csum[:, :], ALU.add).then_inc(s_cu, 1)
                dve.wait_ge(s_sl, 3 * g + 1)
                dve.tensor_tensor(a1[:, :, :], oh1[:, :, :], rb[:, :, :], ALU.mult).then_inc(s_sl, 1)
                dve.tensor_tensor(a2[:, :, :], oh2[:, :, :], rb[:, :, :], ALU.mult).then_inc(s_sl, 1)
                after(dve, s_sc[p], 16 * 2 * G * q)
                dve.wait_ge(s_sl, 3 * g + 3)
                for k, a in enumerate((a1, a2)):
                    dve.reduce_sum(sf[:, k, :], a[:, :, :], AX.X).then_inc(s_sf, 1)
                dve.wait_ge(s_sf, 2 * g + 2)
                dve.tensor_copy(slot[p][:, :, :], sf[:, :, :]).then_inc(s_slot, 2)
                dve.wait_ge(s_e21, g + 1)
                dve.tensor_scalar(den[:, :], e21[:, :], 1.0, None, ALU.add).then_inc(s_mt, 1)
                dve.wait_ge(s_mt, 5 * g + 1)
                dve.reciprocal(c1[:, :], den[:, :]).then_inc(s_mt, 1)
                dve.wait_ge(s_mt, 5 * g + 2)
                dve.tensor_tensor(c2[:, :], e21[:, :], c1[:, :], ALU.mult).then_inc(s_mt, 1)
                dve.wait_ge(s_mt, 5 * g + 3)
                dve.tensor_tensor(den[:, :], c1[:, :], c2[:, :], ALU.subtract).then_inc(s_mt, 1)
                dve.tensor_scalar(rowb[p][:, :, D + 2], c2[:, :], 1.0 / WSCALE, None, ALU.mult)
                dve.tensor_scalar(rowb[p][:, :, D + 3], km1[:, :], -1.0, float(NE), ALU.mult, ALU.add)
                dve.tensor_copy(rowb[p][:, :, D].bitcast(I32), tok[:, :]).then_inc(s_mt, 1)
                dve.wait_ge(s_mt, 5 * g + 5)
                dve.tensor_scalar(tok[:, :], tok[:, :], float(G * P), None, ALU.add)
                dve.tensor_scalar(rowb[p][:, :, D + 1], den[:, :], 1.0 / WSCALE, None, ALU.mult).then_inc(s_meta, 1)

            dve.tensor_copy(ident_h[:, :], ident)
            dve.wait_ge(s_cbf, 1)
            dve.tensor_copy(tri_h[:, :], cbf[:, B_TRI:B_TRI + P])
            dve.tensor_copy(tok[:, :], cst[:, C_TOK:C_TOK + G])
            dve.tensor_copy(ones_h[:, :], cbf[:, B_ONES:B_ONES + P]).then_inc(s_prep, 1)
            groups(dve, front, back)

            step = [0]

            def link(ins):
                step[0] += 1
                ins.then_inc(s_tb, 1)
                dve.wait_ge(s_tb, step[0])

            i_b = cst[:, C_TILE:C_TILE + TILES]
            dve.wait_ge(s_cnt, 1)
            dve.wait_ge(s_lo, NG)
            link(dve.tensor_copy(ncnt[:, :], T0[:, 0:NE]))
            link(dve.tensor_tensor(te3[:, :, :], ncnt[:, :].unsqueeze(2).to_broadcast([P, NE, NB]),
                                   cst[:, C_THR:C_THR + NB].unsqueeze(1).to_broadcast([P, NE, NB]), ALU.is_gt))
            link(dve.reduce_sum(te[:, :], te3[:, :, :], AX.X))
            link(dve.tensor_tensor_scan(ctl[:, :], te[:, :], te[:, :], 0.0, ALU.add, ALU.bypass))
            link(dve.tensor_scalar(wt[:, :], te[:, :], -1.0, float(REGION // P), ALU.mult, ALU.add))
            link(dve.tensor_tensor(le[:, :, :], i_b.unsqueeze(2).to_broadcast([P, TILES, NE]),
                                   ctl[:, :].unsqueeze(1).to_broadcast([P, TILES, NE]), ALU.is_ge))
            link(dve.reduce_sum(idr[:, :], le[:, :, :], AX.X))
            link(dve.tensor_scalar(etab[:, :], idr[:, :], float(NE - 1), None, ALU.min))
            link(dve.tensor_tensor(lw[:, :, :], le[:, :, :], wt[:, :].unsqueeze(1).to_broadcast([P, TILES, NE]),
                                   ALU.mult))
            link(dve.reduce_sum(adr[:, :], lw[:, :, :], AX.X))
            link(dve.tensor_tensor(ad2[:, :], adr[:, :], i_b, ALU.add))
            link(dve.tensor_scalar(adr[:, :], ad2[:, :], float(SPARE // P), float(P), ALU.min, ALU.mult))
            link(dve.memset(chg[:, 0:RING], 1.0))
            link(dve.tensor_tensor(chg[:, RING:TILES], etab[:, RING:TILES], etab[:, 0:TILES - RING], ALU.not_equal))
            link(dve.tensor_copy(tab[:, 0, :], etab[:, :]))
            link(dve.tensor_copy(tab[:, 1, :], adr[:, :]))
            link(dve.tensor_copy(tab[:, 2, :], chg[:, :]))
            dve.tensor_tensor(padr[:, :], ncnt[:, :], cst[:, C_EBASE:C_EBASE + NE], ALU.add).then_inc(s_tab, 1)

            YP = [KE, KO, UB]
            xp = SF[:, 0:CK * P].bitcast(F16)

            def copies(i, k, it):
                dve.wait_ge(s_xtp, i + 1)
                after(dve, s_h, 2 * (i - RING + 1))
                dve.tensor_copy(xT[k][:, :, :], xp.rearrange("p (j n) -> p j n", j=2 * CK)).then_inc(s_xtc, 1)
                after(dve, s_yo, i - RING + 1)
                after(dve, s_yc, i - RING + 1)
                after(dve, s_cw, i)
                dve.tensor_scalar(cw0[:, :], xrow[k][:, D + 3:D + 4], etab[:, bass.ds(i, 1)],
                                  xrow[k][:, D + 1:D + 2], ALU.is_equal, ALU.mult).then_inc(s_cw0, 1)
                dve.wait_ge(s_cw0, i + 1)
                after(dve, s_sa, 16 * (i - RING + 1))
                dve.tensor_copy(dst[k][:, :], xrow[k][:, D:D + 1].bitcast(I32))
                dve.tensor_tensor(cw[k][:, :], cw0[:, :], xrow[k][:, D + 2:D + 3], ALU.add).then_inc(s_cw, 1)

            def low(i, a):
                dve.wait_ge(s_gf, 2 * i + a + 1)
                dve.wait_ge(s_gh, 2 * i + a + 1)
                after(dve, s_m2, 2 * i + a - 1)
                dve.tensor_tensor(gl[a][:, :, :], gf[a].rearrange("p (m n) -> p m n", m=4),
                                  gh[a][:, :, :], ALU.subtract).then_inc(s_glo, 1)

            def sum_up(i, k):
                dve.wait_ge(s_yc, i + 1)
                after(dve, s_sa, 16 * (i - RING + 1))
                dve.scalar_tensor_tensor(yo[k], YP[k][:, 0:D], cw[k][:, 0:1], yc[:, :], ALU.mult, ALU.add
                                         ).then_inc(s_yo, 1)

            def tile(i, k, it):
                low(i, 0)
                if not (isinstance(i, int) and i == 0):
                    sum_up(i - 1, (k - 1) % RING)
                if not (isinstance(i, int) and i == TILES - 1):
                    copies(i + 1, (k + 1) % RING, it + (k + 1) // RING)
                low(i, 1)

            copies(0, 0, 0)
            tiles(dve, tile)
            sum_up(TILES - 1, RING - 1)

        @block.gpsimd
        def _(pool):
            for p in range(2):
                pool.memset(vt[p][:, :, :, DH:DH + 1], 1.0).then_inc(s_prepg, 1)
            pool.memset(mhalf[:, :], -0.5).then_inc(s_prepg, 1)
            pool.wait_ge(s_prepg, 3)
            pool.wait_ge(s_cst, N_CST)

            def front(g, p, q):
                pool.wait_ge(s_mv1, G * (g + 1))
                after(pool, s_rs1, g)
                apart(pool, s_apart["pool"])
                pool.tensor_scalar(ve1[:, :], mv1[:, :, 1], EPS, None, ALU.add).then_inc(s_ve1, 1)
                pool.wait_ge(s_ve1, g + 1)
                after(pool, s_xn, G * g)
                pool.tensor_tensor(rs1[:, :], ve1[:, :], mhalf[:, 0:G], ALU.pow).then_inc(s_rs1, 1)

            def back(g, p, q):
                pool.wait_ge(s_nmu, g + 1)
                pool.wait_ge(s_u, G * (g + 1))
                after(pool, s_tg, g)
                after(pool, s_sq, g)
                pool.tensor_tensor(c_[:, :, :], u[:, :, 0:DH], nmu[:, :].unsqueeze(2).to_broadcast([P, R, DH]),
                                   ALU.add).then_inc(s_cc, 1)
                pool.wait_ge(s_n, 5 * g + 5)
                after(pool, s_tt, g)
                pool.tensor_tensor(hrs[:, :], hv[:, :], mhalf[:, :], ALU.pow).then_inc(s_hrs, 1)
                pool.wait_ge(s_tt, g + 1)
                c4 = c_[:, :, :].rearrange("p (b h) d -> p b (h d)", b=G)
                after(pool, s_x1o[p], 16 * q)
                after(pool, s_xn2, G * (g - 1))
                pool.tensor_tensor(x1[p][:, :, :], c4, gam[:, :].unsqueeze(1).to_broadcast([P, G, D]),
                                   ALU.mult).then_inc(s_tg, 1)
                pool.wait_ge(s_tg, g + 1)
                pool.tensor_tensor(x1[p][:, :, :], x1[p][:, :, :], xt[p][:, :, :], ALU.add).then_inc(s_x1, 1)
                pool.wait_ge(s_mv2, G * (g + 1))
                after(pool, s_rs2, g)
                apart(pool, s_apart["pool"])
                pool.tensor_scalar(ve2[:, :], mv2[:, :, 1], EPS, None, ALU.add).then_inc(s_ve2, 1)
                pool.wait_ge(s_ve2, g + 1)
                after(pool, s_xn2, G * g)
                pool.tensor_tensor(rs2[:, :], ve2[:, :], mhalf[:, 0:G], ALU.pow).then_inc(s_rs2, 1)
                for n in range(2):
                    pool.wait_ge(s_wh, 2 * g + n + 1)
                    if n == 0:
                        hi, lo, src = wcv[p][:, 0:W1], wcv[p][:, W1:2 * W1], wst[p][:, 0:W1]
                    else:
                        v = wcv[p][:, 2 * W1:].rearrange("p (m k n) -> p m k n", m=MK, k=2)
                        hi, lo = v[:, :, 0, :], v[:, :, 1, :]
                        src = wst[p][:, W1:W1 + W2].rearrange("p (m n) -> p m n", m=MK)
                    after(pool, s_wo[p], 16 * q)
                    pool.tensor_tensor(lo, src, hi, ALU.subtract).then_inc(s_wl, 1)
                pool.wait_ge(s_hi, g + 1)
                after(pool, s_sc[p], 16 * 2 * G * q)
                pool.tensor_tensor(rowb[p][:, :, D // 2:D].bitcast(F16), xn2[:, :, :],
                                   rowb[p][:, :, 0:D // 2].bitcast(F16), ALU.subtract).then_inc(s_lo, 1)
                pool.wait_ge(s_lo, g + 1)
                pool.wait_ge(s_meta, g + 1)
                pool.wait_ge(s_slot, 2 * (g + 1))
                apart(pool, s_apart["pool"])
                for b in range(G):
                    for k in range(2):
                        pool.indirect_dma_start(
                            out=rows[:, :], out_offset=bass.IndirectOffsetOnAxis(ap=slot[p][:, k, b:b + 1], axis=0),
                            in_=rowb[p][:, b, :], in_offset=None).then_inc(s_sc[p], 16)

            groups(pool, front, back)

            for p in range(2):
                pool.wait_ge(s_x1o[p], 16 * NG // 2)
            pool.wait_ge(s_init, 32)

            def tile(i, k, it):
                pool.wait_ge(s_yo, i + 1)
                pool.wait_ge(s_cw, i + 1)
                after(pool, s_sa, 16 * i)
                apart(pool, s_apart["pool"])
                pool.indirect_dma_start(
                    out=out[:, :], out_offset=bass.IndirectOffsetOnAxis(ap=dst[k][:, 0:1], axis=0),
                    in_=yo[k], in_offset=None, compute_op=ALU.add).then_inc(s_sa, 16)

            tiles(pool, tile)
            pool.wait_ge(s_sa, 16 * TILES)


def constants():
    part = np.arange(P)
    cf = np.zeros((P, C_F32), np.float32)
    cf[:, C_IDENT:C_IDENT + P] = np.eye(P)
    cf[:, C_W8:C_W8 + NE] = NE - np.arange(NE)
    cf[:, C_EBASE:C_EBASE + NE] = REGION * np.arange(NE)
    cf[:, C_THR:C_THR + NB] = P * np.arange(NB)
    cf[:, C_TILE:C_TILE + TILES] = np.arange(TILES)
    cf[:, C_TOK:C_TOK + G] = P * np.arange(G)[None] + part[:, None]
    cb = np.zeros((P, C_BF), np.float32)
    cb[:, B_IDENT:B_IDENT + P] = np.eye(P)
    mask = np.where(part[None] < part[:, None], NEG, 0.0)
    cb[:, B_MASK:B_MASK + 2 * P] = np.concatenate([mask, mask], 1)
    for q in range(PARTS):
        for b in range(G):
            for h in range(NH):
                r = 32 * q + NH * b + h
                cb[r, B_SEL + b * P:B_SEL + (b + 1) * P] = 1.0
                col = B_HSEL + ((b * 2 + h % 2) * 2 + h // 2) * P
                cb[r, col:col + P] = -1.0
                cb[r, B_HMASK + 2 * (h % 2) + h // 2] = 1.0
    cb[:, B_TRI:B_TRI + P] = part[:, None] < part[None]
    cb[:, B_ONES:B_ONES + P] = 1.0
    pad = np.zeros((P, ROW), np.float32)
    pad[:, D] = (NT + part).astype(np.int32).view(np.float32)
    return cf, cb, pad


_INS = ["x", "ctx_1024", "L0_xattn_igate_kernel", "L0_xattn_igate_bias", "L0_xattn_fgate_kernel",
        "L0_xattn_fgate_bias", "L0_xattn_outnorm_scale", "L0_ffn_router_w", "L0_ffn_w1", "L0_ffn_w2"]


def kernel(**inputs):
    import concourse.bacc as bacc
    from concourse.bass_utils import run_bass_kernel_spmd

    nc = bacc.Bacc("TRN2", target_bir_lowering=False, num_devices=1)
    arrays, args = {}, []
    named = [(n, np.ascontiguousarray(inputs[n])) for n in _INS]
    named += list(zip(("const_f32", "const_selectors", "const_pad"), constants()))
    for name, a in named:
        arrays[f"in_{name}"] = a
        args.append(nc.dram_tensor(f"in_{name}", a.shape, mybir.dt.from_np(a.dtype), kind="ExternalInput").ap())
    out = nc.dram_tensor("out", (NT + P, D), F32, kind="ExternalOutput").ap()
    build(nc, *args, out)
    r = run_bass_kernel_spmd(nc, [arrays], core_ids=[0])
    return r.results[0]["out"][:NT].reshape(NB, S, D)
```

```python
from contextlib import ExitStack

import numpy as np

import concourse.bass as bass
from concourse import mybir

ALU = mybir.AluOpType
ACT = mybir.ActivationFunctionType
AX = mybir.AxisListType
F32, F16, BF16, I32 = mybir.dt.float32, mybir.dt.float16, mybir.dt.bfloat16, mybir.dt.int32

P = 128
NB, S, D = 32, 128, 256
NH, DH = 4, 64
NE, HID = 8, 1024
G = 4
NG = NB // G
NT = NB * S
CK = D // P
MK = HID // P
R = G * NH
PARTS = 3
KP = 32 * (PARTS - 1) + 32
ROW = D + 4
REGION = NT + P
RING = 3
TILES = -(-(2 * NT // P + NE - 1) // RING) * RING
SPARE = NE * REGION
WSCALE = 16.0
W1, W2 = CK * HID, MK * D
EPS = 1e-5
NEG = -1e30

C_IDENT = 0
C_W8 = C_IDENT + P
C_EBASE = C_W8 + NE
C_THR = C_EBASE + NE
C_TILE = C_THR + NB
C_TOK = C_TILE + TILES
C_MEAN = C_TOK + G
C_F32 = C_MEAN + CK * NH
B_IDENT = 0
B_MASK = B_IDENT + P
B_SEL = B_MASK + 2 * P
B_HSEL = B_SEL + G * P
B_HMASK = B_HSEL + G * NH * P
B_TRI = B_HMASK + NH
B_ONES = B_TRI + P
C_BF = B_ONES + P


def after(eng, sem, value):
    if isinstance(value, int) and value <= 0:
        return
    eng.wait_ge(sem, value)


def apart(eng, sem):
    eng.sem_inc(sem, 1)


def build(nc, x, ctx_in, ig_k, ig_b, fg_k, fg_b, gamma, router_w, w1, w2, cf, cb, pad_rows, out):
    with ExitStack() as stack:
        def sb(name, shape, dt=F32):
            return stack.enter_context(nc.sbuf_tensor(name, shape, dt))

        def ps(name, shape, dt=F32):
            return stack.enter_context(nc.psum_tensor(name, shape, dt))

        def sem(name):
            return stack.enter_context(nc.semaphore(name))

        rows = nc.dram_tensor("rows", (SPARE + P, ROW), F32, kind="Internal").ap()
        wsplit = nc.dram_tensor("wsplit", (NE, P, 2 * (W1 + W2)), F16, kind="Internal").ap()

        cst = sb("cst", [P, C_F32])
        cbf = sb("cbf", [P, C_BF], BF16)
        ident = cst[:, C_IDENT:C_IDENT + P]
        ident_h = sb("ident_h", [P, P], F16)
        tri_h = sb("tri_h", [P, P], F16)
        ones_h = sb("ones_h", [P, P], F16)
        pad = sb("pad", [P, ROW])
        gate_w = sb("gate_w", [P, 3 * CK, 3, NH])
        gate_b = sb("gate_b", [R, 2])
        gam = sb("gam", [P, D])
        rw = sb("rw", [NE, D])
        rwT = sb("rwT", [P, CK, NE])
        mhalf = sb("mhalf", [P, R])

        xt = [sb(f"xt{p}", [P, G, D]) for p in range(2)]
        vt = [sb(f"vt{p}", [P, G, NH, DH + 1]) for p in range(2)]
        xn = sb("xn", [P, G, D])
        st1 = sb("st1", [P, G, 6])
        mv1 = sb("mv1", [P, G, 2])
        ve1 = sb("ve1", [P, G])
        rs1 = sb("rs1", [P, G])
        qkT = [sb(f"qkT{p}", [P, G, 2 * CK, P]) for p in range(2)]
        gsb = sb("gsb", [P, 3 * R])
        ga = sb("ga", [R, P])
        ge = sb("ge", [R, P])
        gl_ = sb("gl_", [R, P])
        gmn = sb("gmn", [R, P])
        gcs = sb("gcs", [R, P])
        gi = sb("gi", [R, P])
        gm = sb("gm", [R, 2, P])
        gr = sb("gr", [R, 2, P])
        gr2 = sb("gr2", [R, 2, P])
        grb = sb("grb", [R, 2, P], BF16)
        gnm = sb("gnm", [R, P])
        parts = [sb(f"parts{p}", [KP, 2, P], BF16) for p in range(2)]
        mblk = [sb(f"mblk{p}", [KP, NH, P], BF16) for p in range(2)]
        en = [sb(f"en{p}", [P, R]) for p in range(2)]
        dt_ = [sb(f"dt{i}", [P, 2, 512]) for i in range(2)]
        ct = [sb(f"ct{i}", [P, 2, 512]) for i in range(2)]
        u = sb("u", [P, R, DH + 1])
        ss = sb("ss", [P, R])
        n0 = sb("n0", [P, R])
        n1 = sb("n1", [P, R])
        n2 = sb("n2", [P, R])
        hv = sb("hv", [P, R])
        hrs = sb("hrs", [P, R])
        x1 = [sb(f"x1_{p}", [P, G, D]) for p in range(2)]
        st2 = sb("st2", [P, G, 6])
        mv2 = sb("mv2", [P, G, 2])
        ve2 = sb("ve2", [P, G])
        rs2 = sb("rs2", [P, G])
        xn2 = sb("xn2", [P, G, D])
        sq = xn2[:, :, :].rearrange("p b (h d) -> p (b h) d", h=NH)
        ctn = [sb(f"ctn{p}", [P, G, D]) for p in range(2)]
        rT = sb("rT", [P, G, CK, P])
        rowb = [sb(f"rowb{p}", [P, G, ROW]) for p in range(2)]
        lg = sb("lg", [P, G, NE])
        lg2 = sb("lg2", [P, G, NE])
        eq = sb("eq", [P, G, NE])
        key = sb("key", [P, G, NE])
        m1 = sb("m1", [P, G])
        m2 = sb("m2", [P, G])
        km1 = sb("km1", [P, G])
        km2 = sb("km2", [P, G])
        oh1 = sb("oh1", [P, G, NE])
        oh2 = sb("oh2", [P, G, NE])
        msk = sb("msk", [P, G, NE], F16)
        cum = sb("cum", [P, NE], F16)
        csum = sb("csum", [P, NE])
        sf = sb("sf", [P, 2, G])
        d21 = sb("d21", [P, G])
        e21 = sb("e21", [P, G])
        den = sb("den", [P, G])
        c1 = sb("c1", [P, G])
        c2 = sb("c2", [P, G])
        rb = sb("rb", [P, G, NE])
        a1 = sb("a1", [P, G, NE])
        a2 = sb("a2", [P, G, NE])
        slot = [sb(f"slot{p}", [P, 2, G], I32) for p in range(2)]
        tok = sb("tok", [P, G])
        wcv = [sb(f"wcv{p}", [P, 2 * (W1 + W2)], F16) for p in range(2)]
        wring = sb("wring", [P, RING, 2 * (W1 + W2)], F16)
        wst = [wring[:, p, :].bitcast(F32) for p in range(2)]

        te3 = xn2[:, :, :].rearrange("p r d -> p (r d)")[:, 0:NE * NB].rearrange("p (e j) -> p e j", e=NE)
        te = sb("te", [P, NE])
        ncnt = sb("ncnt", [P, NE])
        ctl = sb("ctl", [P, NE])
        wt = sb("wt", [P, NE])
        le, lw = (t[:, :, :].rearrange("p a n -> p (a n)")[:, 0:TILES * NE].rearrange("p (i e) -> p i e", e=NE)
                  for t in (dt_[0], ct[0]))
        idr = sb("idr", [P, TILES])
        etab = sb("etab", [P, TILES])
        adr = sb("adr", [P, TILES])
        ad2 = sb("ad2", [P, TILES])
        chg = sb("chg", [P, TILES])
        tab = sb("tab", [P, 3, TILES], I32)
        padr = sb("padr", [P, NE], I32)

        xrow = [sb(f"xrow{i}", [P, ROW]) for i in range(RING)]
        xT = [sb(f"xT{i}", [P, 2 * CK, P], F16) for i in range(RING)]
        gf = [dt_[1][:, a, :] for a in range(2)]
        gh = [sb(f"gh{a}", [P, 4, P], F16) for a in range(2)]
        gl = [sb(f"gl{a}", [P, 4, P], F16) for a in range(2)]
        cw0 = sb("cwd", [P, 1])
        cw = [sb(f"cw{i}", [P, 1]) for i in range(RING)]
        yc = sb("yc", [P, D])
        yo = [ct[1][:, :, :].rearrange("p a n -> p (a n)")[:, D * i:D * (i + 1)] for i in range(RING)]
        dst = [sb(f"dst{i}", [P, 1], I32) for i in range(RING)]

        bank = [ps(f"bank{i}", [P, 512]) for i in range(8)]
        T0, T1, KE, KO, DE, DO, UB, SF = bank
        TB, KB, DB = [T0, T1], [KE, KO], [DE, DO]
        LG, RK = DE[:, 0:G * NE], DO[:, 0:G * NE]

        s_cst = sem("constants_loaded")
        s_cbf = sem("selectors_cast")
        s_prep = sem("prepared_by_vector")
        s_prepg = sem("prepared_by_pool")
        s_rwt = sem("router_transposed")
        s_rwc = sem("router_copied")
        s_x = [sem(f"x_loaded{p}") for p in range(2)]
        s_c = [sem(f"ctx_loaded{p}") for p in range(2)]
        s_xc = [sem(f"x_copied{p}") for p in range(2)]
        s_vc = sem("values_centred")
        s_wst = [sem(f"weights_loaded{p}") for p in range(2)]
        s_bn1 = sem("x_stats")
        s_mv1 = sem("x_mean_var")
        s_ve1 = sem("x_var_eps")
        s_rs1 = sem("x_rstd")
        s_xn = sem("x_normed")
        s_tq = sem("qk_transposed")
        s_qk = sem("qk_copied")
        s_gt = sem("gates_summed")
        s_gsb = sem("gates_copied")
        s_gT = sem("gates_transposed")
        s_ga = sem("gate_abs")
        s_ge = sem("gate_exp")
        s_gl = sem("gate_log")
        s_gmn = sem("gate_min")
        s_gcs = sem("gate_cumsum")
        s_gi = sem("gate_input")
        s_ng = sem("gate_ng")
        s_gmx = sem("gate_cummax")
        s_gnm = sem("gate_neg_logd")
        s_pt = sem("gate_parts")
        s_gr = sem("gate_rests")
        s_mb = sem("gate_blocks")
        s_nT = sem("neg_logd_transposed")
        s_en = sem("neg_logd_exp")
        s_d = sem("logd_summed")
        s_dt = sem("decay_ready")
        s_kq = sem("kq_ready")
        s_ct = sem("scores_ready")
        s_pv = sem("pv_ready")
        s_u = sem("pv_copied")
        s_sq = sem("pv_squared")
        s_ss = sem("pv_sumsq")
        s_n = sem("normaliser_steps")
        s_hrs = sem("head_rstd")
        s_tt = sem("head_scaled")
        s_tg = sem("head_gamma")
        s_x1 = sem("x1_ready")
        s_x1o = [sem(f"x1_stored{p}") for p in range(2)]
        s_bn2 = sem("x1_stats")
        s_mv2 = sem("x1_mean_var")
        s_ve2 = sem("x1_var_eps")
        s_rs2 = sem("x1_rstd")
        s_xn2 = sem("x1_normed")
        s_hi = sem("row_high")
        s_lo = sem("row_low")
        s_rt = sem("x1n_transposed")
        s_rTc = sem("x1n_T_copied")
        s_lg = sem("logits_ready")
        s_lgc = sem("logits_copied")
        s_rk = sem("router_steps")
        s_km = sem("top_two_steps")
        s_sl = sem("slot_steps")
        s_sf = sem("slot_sums")
        s_cu = sem("count_steps")
        s_mt = sem("meta_steps")
        s_msk = sem("expert_masks")
        s_e21 = sem("router_exp")
        s_rank = sem("ranks_ready")
        s_slot = sem("slots_ready")
        s_meta = sem("row_meta")
        s_sc = [sem(f"rows_scattered{p}") for p in range(2)]
        s_w16 = sem("second_weights_scaled")
        s_wh1 = sem("first_weights_high")
        s_wh2 = sem("second_weights_high")
        s_wl1 = sem("first_weights_low")
        s_wl2 = sem("second_weights_low")
        s_wo = [sem(f"weights_stored{p}") for p in range(2)]
        s_cnt = sem("counts_ready")
        s_tb = sem("table_steps")
        s_tab = sem("table_ready")
        s_pad = sem("pads_stored")
        s_init = sem("spare_rows_stored")
        s_xr = [sem(f"tile_loaded{i}") for i in range(RING)]
        s_wr = [sem(f"tile_weights{i}") for i in range(RING)]
        s_xtp = sem("tile_transposed")
        s_xtc = sem("tile_T_copied")
        s_h = sem("hidden_ready")
        s_gf = sem("gelu_full")
        s_gh = sem("gelu_high")
        s_glo = sem("gelu_low")
        s_m2 = sem("out_half_done")
        s_cw0 = sem("row_weight_step")
        s_cw = sem("row_weight")
        s_yc = sem("out_cross_copied")
        s_yo = sem("out_ready")
        s_sa = sem("out_added")
        s_apart = {n: sem(f"waits_apart_{n}") for n in ("sp", "pe", "dve", "pool")}
        N_CST = 16 * (7 + 2 * G)
        N_PREP = 7

        def groups(eng, step):
            def group(g):
                return (g, g % 2, g // 2) if 0 <= g < NG else None

            for t in range(-1, 3):
                step(group(t + 1), group(t), group(t - 1))
            with eng.Fori(2, NG // 2) as q:
                step((2 * q, 0, q), (2 * q - 1, 1, q - 1), (2 * q - 2, 0, q - 1))
                step((2 * q + 1, 1, q), (2 * q, 0, q), (2 * q - 1, 1, q - 1))
            for t in range(NG - 1, NG + 1):
                step(group(t + 1), group(t), group(t - 1))

        def tiles(eng, tile):
            for i in range(RING):
                tile(i, i, 0)
            with eng.Fori(1, TILES // RING - 1) as it:
                for i in range(RING):
                    tile(RING * it + i, i, it)
            for i in range(RING):
                tile(TILES - RING + i, i, TILES // RING - 1)

        block = stack.enter_context(nc.Block())

        @block.sync
        def _(sp):
            gk_i = ig_k.rearrange("(c p) h -> p c h", p=P)
            gk_f = fg_k.rearrange("(c p) h -> p c h", p=P)
            sp.dma_start(xt[0][:, :, :], x[0:G].rearrange("b p d -> p b d")).then_inc(s_x[0], 16)
            sp.dma_start(cst[:, :], cf).then_inc(s_cst, 16)
            sp.dma_start(gate_w[:, :, 0, :], gk_i).then_inc(s_cst, 16)
            sp.dma_start(gate_w[:, :, 1, :], gk_f).then_inc(s_cst, 16)
            for b in range(G):
                sp.dma_start(gate_b[NH * b:NH * b + NH, 0:1], ig_b.rearrange("(h o) -> h o", o=1)).then_inc(s_cst, 16)
                sp.dma_start(gate_b[NH * b:NH * b + NH, 1:2], fg_b.rearrange("(h o) -> h o", o=1)).then_inc(s_cst, 16)
            sp.dma_start(wring[:, RING - 1, :].bitcast(F32)[:, 0:C_BF], cb).then_inc(s_cst, 16)
            sp.dma_start(gam[:, :], gamma.rearrange("(o d) -> o d", o=1).to_broadcast([P, D])).then_inc(s_cst, 16)
            sp.dma_start(rw[:, :], router_w).then_inc(s_cst, 16)
            sp.dma_start(pad[:, :], pad_rows).then_inc(s_cst, 16)

            def load_x(g, p, q):
                after(sp, s_xn, G * (g - 1))
                apart(sp, s_apart["sp"])
                after(sp, s_xc[p], 16 * q)
                if isinstance(g, int) and g == 0:
                    return
                sp.dma_start(xt[p][:, :, :], x[bass.ds(g * G, G)].rearrange("b p d -> p b d")).then_inc(s_x[p], 16)

            def load_c(g, p, q):
                after(sp, s_tq, G * (g - 1))
                after(sp, s_vc, g - 1)
                sp.dma_start(ctn[p][:, :, :], ctx_in[bass.ds(g * G, G)].rearrange("b p d -> p b d")
                             ).then_inc(s_c[p], 16)

            def load_w(g, p, q):
                after(sp, s_wl1, g - 1)
                after(sp, s_wl2, g - 1)
                sp.dma_start(wst[p][:, 0:W1].rearrange("p (c n) -> p c n", c=CK),
                             w1[bass.ds(g, 1)].rearrange("o (c p) n -> p (o c) n", p=P)).then_inc(s_wst[p], 16)
                sp.dma_start(wst[p][:, W1:W1 + W2].rearrange("p (m n) -> p m n", m=MK),
                             w2[bass.ds(g, 1)].rearrange("o (m p) n -> p (o m) n", p=P)).then_inc(s_wst[p], 16)

            def copy_x(g, p, q):
                sp.wait_ge(s_x[p], 16 * (q + 1))
                apart(sp, s_apart["sp"])
                after(sp, s_xn2, G * (g - 1))
                after(sp, s_x1o[p], 16 * q)
                sp.dma_start(x1[p][:, :, :], xt[p][:, :, :]).then_inc(s_xc[p], 16)

            def store_x1(g, p, q):
                sp.wait_ge(s_x1, g + 1)
                sp.dma_start(out[bass.ds(g * G * P, G * P), :].rearrange("(b p) d -> p b d", p=P),
                             x1[p][:, :, :]).then_inc(s_x1o[p], 16)

            def store_w(g, p, q):
                sp.wait_ge(s_wl1, g + 1)
                sp.wait_ge(s_wl2, g + 1)
                sp.dma_start(wsplit[bass.ds(g, 1)].rearrange("o p n -> (o p) n"), wcv[p][:, :]).then_inc(s_wo[p], 16)

            def step(n, t, m):
                if n:
                    load_x(*n)
                    load_c(*n)
                if t:
                    load_w(*t)
                    copy_x(*t)
                if m:
                    store_w(*m)
                    store_x1(*m)

            sp.wait_ge(s_cst, N_CST)
            sp.dma_start(rows[SPARE:SPARE + P, :], pad[:, :]).then_inc(s_init, 16)
            sp.wait_ge(s_prep, N_PREP)
            sp.dma_start(out[NT:NT + P, :], yc[:, :]).then_inc(s_init, 16)
            groups(sp, step)

            sp.wait_ge(s_tab, 1)
            for p in range(2):
                sp.wait_ge(s_sc[p], 16 * 2 * G * NG // 2)
                sp.wait_ge(s_wo[p], 16 * NG // 2)
            for e in range(NE):
                r = sp.value_load(padr[0:1, e:e + 1], min_val=e * REGION, max_val=e * REGION + NT)
                sp.dma_start(rows[bass.ds(r, P), :], pad[:, :]).then_inc(s_pad, 16)
            sp.wait_ge(s_pad, 16 * NE)
            sp.wait_ge(s_init, 32)

            def tile(i, k, it):
                after(sp, s_xtp, i - RING + 1)
                after(sp, s_cw, i - RING + 1)
                r = sp.value_load(tab[0:1, 1, bass.ds(i, 1)], min_val=0, max_val=SPARE)
                sp.dma_start(xrow[k][:, :], rows[bass.ds(r, P), :]).then_inc(s_xr[k], 16)
                after(sp, s_m2, 2 * (i - RING + 1))
                e = sp.value_load(tab[0:1, 0, bass.ds(i, 1)], min_val=0, max_val=NE - 1)
                need = sp.value_load(tab[0:1, 2, bass.ds(i, 1)], min_val=0, max_val=1)
                sp.dma_start(wring[:, k, :], wsplit[bass.ds(e, 1)].rearrange("o p n -> (o p) n"),
                             cond=need).then_inc(s_wr[k], 16)

            tiles(sp, tile)
            sp.wait_ge(s_sa, 16 * TILES)

        @block.tensor
        def _(pe):
            pe.wait_ge(s_cst, N_CST)
            for c in range(CK):
                mm = pe.transpose(SF[:, c * NE:(c + 1) * NE], rw[:, c * P:(c + 1) * P], ident[0:NE, 0:NE])
            mm.then_inc(s_rwt, 1)
            pe.wait_ge(s_rwc, 1)
            pe.wait_ge(s_prep, N_PREP + 1)
            pe.wait_ge(s_prepg, 3)

            def turn(g, p, q, b):
                pe.wait_ge(s_xn, G * g + b + 1)
                after(pe, s_qk, G * g + b - 1)
                if b < 2:
                    after(pe, s_rTc, 2 * (g - 2) + b + 1)
                if b == 0:
                    pe.wait_ge(s_c[p], 16 * (q + 1))
                for j in range(CK):
                    pe.transpose(TB[b % 2][:, j * P:(j + 1) * P], xn[:, b, j * P:(j + 1) * P], ident)
                for j in range(CK):
                    mm = pe.transpose(TB[b % 2][:, (CK + j) * P:(CK + j + 1) * P],
                                      ctn[p][:, b, j * P:(j + 1) * P], ident)
                mm.then_inc(s_tq, 1)

            def gates(g, p, q, b):
                pe.wait_ge(s_qk, G * g + b + 1)
                if b == 0:
                    after(pe, s_en, g)
                sums = SF[:, 0:3 * R].rearrange("p (i r) -> p i r", i=3)[:, :, NH * b:NH * (b + 1)]
                for j in range(2 * CK):
                    mm = pe.matmul(sums, qkT[p][:, b, j, :], gate_w[:, j, :, :], start=(j == 0),
                                   stop=(j == 2 * CK - 1))
                mm.then_inc(s_gt, 1)

            def gates_turn(g, p, q):
                pe.wait_ge(s_gsb, g + 1)
                after(pe, s_gnm, g)
                after(pe, s_gl, g)
                for i in range(2):
                    mm = pe.transpose(SF[0:R, P + i * P:2 * P + i * P], gsb[:, i * R:(i + 1) * R], ident)
                mm.then_inc(s_gT, 1)

            def neg_logd_turn(g, p, q):
                pe.wait_ge(s_gnm, g + 1)
                after(pe, s_en, g)
                apart(pe, s_apart["pe"])
                pe.transpose(SF[:, 3 * P:3 * P + R], gnm[:, :], ident[0:R, 0:R]).then_inc(s_nT, 1)

            def logd(g, p, q, h):
                after(pe, s_dt, 2 * (2 * g + h))
                if h == 0:
                    after(pe, s_lgc, g - 1)
                    after(pe, s_sl, 3 * g - 5)
                    pe.wait_ge(s_mb, g + 1)
                    pe.wait_ge(s_pt, PARTS * (g + 1))
                for par in range(2):
                    for b2 in range(2):
                        b = 2 * h + b2
                        o = DB[par][:, b2 * 2 * P:(b2 + 1) * 2 * P]
                        hs = B_HSEL + (b * 2 + par) * 2 * P
                        pe.matmul(o, cbf[0:KP, B_SEL + b * P:B_SEL + (b + 1) * P],
                                  mblk[p][:, 2 * par:2 * par + 2, :], start=True, stop=False)
                        pe.matmul(o, parts[p][:, 0, :], cbf[0:KP, hs:hs + 2 * P], start=False, stop=False)
                        mm = pe.matmul(o, cbf[:, B_IDENT:B_IDENT + P], cbf[:, B_MASK:B_MASK + 2 * P],
                                       start=False, stop=True)
                    mm.then_inc(s_d, 1)

            def scores(g, p, q, h):
                after(pe, s_ct, 2 * (2 * g + h))
                for b2 in range(2):
                    b = 2 * h + b2
                    for hp in range(2):
                        for par in range(2):
                            rows_ = slice(DH * par, DH * par + DH)
                            o = KB[par][:, (2 * b2 + hp) * P:(2 * b2 + hp + 1) * P]
                            mm = pe.matmul(o, qkT[p][rows_, b, CK + hp, :], qkT[p][rows_, b, hp, :],
                                           start=True, stop=True)
                mm.then_inc(s_kq, 1)

            def values(g, p, q, b):
                pe.wait_ge(s_ct, 2 * (2 * g + b // 2 + 1))
                pe.wait_ge(s_vc, g + 1)
                after(pe, s_u, G * g + b)
                after(pe, s_sq, G * g + b)
                for h4 in range(NH):
                    c0 = (2 * (b % 2) + h4 // 2) * P
                    mm = pe.matmul(UB[:, h4 * (DH + 1):(h4 + 1) * (DH + 1)],
                                   ct[b // 2][:, h4 % 2, c0:c0 + P], vt[p][:, b, h4, :],
                                   start=True, stop=True)
                mm.then_inc(s_pv, 1)

            def router_turn(g, p, q, h):
                pe.wait_ge(s_xn2, G * g + 2 * h + 2)
                after(pe, s_qk, G * (min(g + 2, NG) if isinstance(g, int) else g + 2))
                for b2 in range(2):
                    for j in range(CK):
                        mm = pe.transpose(TB[h][:, (2 * b2 + j) * P:(2 * b2 + j + 1) * P],
                                          xn2[:, 2 * h + b2, j * P:(j + 1) * P], ident)
                mm.then_inc(s_rt, 1)

            def logits(g, p, q):
                after(pe, s_dt, 4 * (min(g + 2, NG) if isinstance(g, int) else g + 2) - 1)
                for b in range(G):
                    pe.wait_ge(s_rTc, 2 * g + b // 2 + 1)
                    for j in range(CK):
                        mm = pe.matmul(LG[:, b * NE:(b + 1) * NE], rT[:, b, j, :], rwT[:, j, :],
                                       start=(j == 0), stop=(j == CK - 1))
                mm.then_inc(s_lg, 1)

            def ranks(g, p, q):
                pe.wait_ge(s_msk, g + 1)
                after(pe, s_dt, 4 * (min(g + 2, NG) if isinstance(g, int) else g + 2))
                after(pe, s_cu, 2 * g)
                pe.matmul(RK, tri_h[:, :], msk[:, :, :], start=True, stop=False, skip_group_check=True)
                for n in range(1, G):
                    pe.matmul(RK[:, n * NE:], ones_h[:, :], msk[:, 0:G - n, :], start=False,
                              stop=False, skip_group_check=True)
                for b in range(G):
                    mm = pe.matmul(RK[:, b * NE:(b + 1) * NE], ones_h[:, :], cum[:, :], start=False,
                                   stop=(b == G - 1), skip_group_check=True)
                mm.then_inc(s_rank, 1)

            def step(n, t, m):
                if t:
                    logd(*t, 0)
                    scores(*t, 0)
                if m:
                    router_turn(*m, 0)
                    router_turn(*m, 1)
                if t:
                    logd(*t, 1)
                    scores(*t, 1)
                if n:
                    turn(*n, 0)
                    turn(*n, 1)
                if m:
                    logits(*m)
                if t:
                    values(*t, 0)
                if n:
                    gates(*n, 0)
                    turn(*n, 2)
                if t:
                    values(*t, 1)
                if n:
                    gates(*n, 1)
                    turn(*n, 3)
                if t:
                    values(*t, 2)
                if n:
                    gates(*n, 2)
                if t:
                    values(*t, 3)
                if n:
                    gates(*n, 3)
                if m:
                    ranks(*m)
                if n:
                    gates_turn(*n)
                    neg_logd_turn(*n)

            groups(pe, step)

            pe.wait_ge(s_meta, NG)
            pe.matmul(T0[:, 0:NE], ones_h[:, :], cum[:, :], start=True, stop=True).then_inc(s_cnt, 1)

            XP, YP, HPS = SF, [KE, KO, UB], [DE, DO]
            xp = XP[:, 0:CK * P].bitcast(F16)

            def turn(i, k, it):
                pe.wait_ge(s_xr[k], 16 * (it + 1))
                after(pe, s_xtc, i)
                xr = xrow[k][:, :].bitcast(F16)
                for j in range(2 * CK):
                    mm = pe.transpose(xp[:, j * P:(j + 1) * P], xr[:, j * P:(j + 1) * P], ident_h[:, :])
                mm.then_inc(s_xtp, 1)

            def hidden(i, k, it, a):
                if a == 0:
                    pe.wait_ge(s_wr[k], 16 * (it + 1))
                    pe.wait_ge(s_xtc, i + 1)
                after(pe, s_gf, 2 * i + a - 1)
                after(pe, s_gh, 2 * i + a - 1)
                for m4 in range(4):
                    m = 4 * a + m4
                    o = HPS[a][:, m4 * P:(m4 + 1) * P]
                    for c in range(CK):
                        hi = wring[:, k, c * HID + m * P:c * HID + (m + 1) * P]
                        lo = wring[:, k, W1 + c * HID + m * P:W1 + c * HID + (m + 1) * P]
                        pe.matmul(o, hi, xT[k][:, c, :], start=(c == 0), stop=False)
                        pe.matmul(o, hi, xT[k][:, CK + c, :], start=False, stop=False)
                        mm = pe.matmul(o, lo, xT[k][:, c, :], start=False, stop=(c == CK - 1))
                mm.then_inc(s_h, 1)

            def output(i, k, a):
                pe.wait_ge(s_gh, 2 * i + a + 1)
                pe.wait_ge(s_glo, 2 * i + a + 1)
                if a == 0:
                    after(pe, s_yo, i - RING + 1)
                for m4 in range(4):
                    w = 2 * W1 + (4 * a + m4) * 2 * D
                    pe.matmul(YP[k][:, 0:2 * D], gh[a][:, m4, :], wring[:, k, w:w + 2 * D],
                              start=(a == 0 and m4 == 0), stop=False, skip_group_check=True)
                    mm = pe.matmul(YP[k][:, D:2 * D], gl[a][:, m4, :], wring[:, k, w:w + D],
                                   start=False, stop=(a == 1 and m4 == 3), skip_group_check=True)
                mm.then_inc(s_m2, 1)

            def tile(i, k, it):
                hidden(i, k, it, 0)
                if not (isinstance(i, int) and i == 0):
                    output(i - 1, (k - 1) % RING, 1)
                hidden(i, k, it, 1)
                if not (isinstance(i, int) and i == TILES - 1):
                    turn(i + 1, (k + 1) % RING, it + (k + 1) // RING)
                output(i, k, 0)

            pe.wait_ge(s_slot, 2 * NG)
            turn(0, 0, 0)
            tiles(pe, tile)
            output(TILES - 1, RING - 1, 1)

        @block.scalar
        def _(act):
            def turned(g, p, q, b):
                act.wait_ge(s_tq, G * g + b + 1)
                if b == 0:
                    after(act, s_kq, 2 * (g - 1))
                act.activation(qkT[p][:, b, :, :], TB[b % 2][:, :].rearrange("p (j n) -> p j n", j=2 * CK),
                               ACT.Copy).then_inc(s_qk, 1)

            def log_sigmoid(g, p, q):
                act.wait_ge(s_gT, g + 1)
                after(act, s_gcs, g)
                act.activation(ga[:, :], SF[0:R, 2 * P:3 * P], ACT.Abs, bias=gate_b[:, 1:2]).then_inc(s_ga, 1)
                act.wait_ge(s_ga, g + 1)
                act.activation(ge[:, :], ga[:, :], ACT.Exp, scale=-1.0).then_inc(s_ge, 1)
                act.wait_ge(s_ge, g + 1)
                act.activation(gl_[:, :], ge[:, :], ACT.Ln, bias=1.0).then_inc(s_gl, 1)

            def exp_neg_logd(g, p, q):
                act.wait_ge(s_nT, g + 1)
                after(act, s_n, 5 * (g - 1))
                act.activation(en[p][:, :], SF[:, 3 * P:3 * P + R], ACT.Exp).then_inc(s_en, 1)

            def decay(g, p, q, h):
                for par in range(2):
                    act.wait_ge(s_d, 2 * (2 * g + h) + par + 1)
                    after(act, s_ct, 2 * (2 * g + h - 2) + par + 1)
                    act.activation(dt_[h][:, par, :], DB[par][:, :], ACT.Exp).then_inc(s_dt, 1)

            def values(g, p, q, b):
                act.wait_ge(s_pv, G * g + b + 1)
                if b == 0:
                    after(act, s_tt, g)
                    after(act, s_n, 5 * g)
                    after(act, s_rt, 2 * g)
                    after(act, s_lo, g)
                    after(act, s_hi, g)
                hd = UB[:, 0:NH * (DH + 1)].rearrange("p (h d) -> p h d", h=NH)
                act.activation(u[:, NH * b:NH * (b + 1), :], hd, ACT.Copy).then_inc(s_u, 1)
                act.activation(sq[:, NH * b:NH * (b + 1), :], hd[:, :, 0:DH], ACT.Square).then_inc(s_sq, 1)

            def split_w1(g, p, q):
                act.wait_ge(s_wst[p], 32 * (q + 1))
                after(act, s_wo[p], 16 * q)
                act.activation(wcv[p][:, 0:W1], wst[p][:, 0:W1], ACT.Copy, scale=WSCALE).then_inc(s_wh1, 1)

            def split_w2(g, p, q):
                act.activation(wst[p][:, W1:W1 + W2], wst[p][:, W1:W1 + W2], ACT.Copy, scale=WSCALE).then_inc(s_w16, 1)
                act.wait_ge(s_w16, g + 1)
                act.activation(wcv[p][:, 2 * W1:].rearrange("p (m k n) -> p m k n", m=MK, k=2)[:, :, 0, :],
                               wst[p][:, W1:W1 + W2].rearrange("p (m n) -> p m n", m=MK), ACT.Copy
                               ).then_inc(s_wh2, 1)

            def row_high(g, p, q):
                act.wait_ge(s_xn2, G * (g + 1))
                after(act, s_sc[p], 16 * 2 * G * q)
                act.activation(rowb[p][:, :, 0:D // 2].bitcast(F16), xn2[:, :, :], ACT.Copy).then_inc(s_hi, 1)

            def router_turned(g, p, q, h):
                act.wait_ge(s_rt, 2 * g + h + 1)
                if h == 0:
                    after(act, s_lg, g)
                act.activation(rT[:, 2 * h:2 * h + 2, :, :],
                               TB[h][:, :].rearrange("p (b j n) -> p b j n", b=2, j=CK),
                               ACT.Copy).then_inc(s_rTc, 1)

            def router_exp(g, p, q):
                act.wait_ge(s_rk, 10 * g + 8)
                after(act, s_meta, g)
                act.activation(e21[:, :], d21[:, :], ACT.Exp).then_inc(s_e21, 1)

            def step(n, t, m):
                if t:
                    decay(*t, 0)
                if m:
                    row_high(*m)
                    router_turned(*m, 0)
                    router_turned(*m, 1)
                if t:
                    decay(*t, 1)
                if n:
                    turned(*n, 0)
                    turned(*n, 1)
                if t:
                    values(*t, 0)
                if n:
                    turned(*n, 2)
                if t:
                    values(*t, 1)
                if n:
                    turned(*n, 3)
                if t:
                    values(*t, 2)
                    values(*t, 3)
                if m:
                    router_exp(*m)
                if t:
                    split_w1(*t)
                if n:
                    log_sigmoid(*n)
                if t:
                    split_w2(*t)
                if n:
                    exp_neg_logd(*n)

            act.wait_ge(s_cst, N_CST)
            groups(act, step)

            HPS, YP = [DE, DO], [KE, KO, UB]

            def gelu(i, a):
                act.wait_ge(s_h, 2 * i + a + 1)
                after(act, s_glo, 2 * i + a - 1)
                act.activation(gf[a], HPS[a][:, :], ACT.Gelu, scale=1.0 / WSCALE).then_inc(s_gf, 1)
                after(act, s_m2, 2 * i + a - 1)
                act.activation(gh[a][:, :, :], HPS[a][:, :].rearrange("p (m n) -> p m n", m=4), ACT.Gelu,
                               scale=1.0 / WSCALE).then_inc(s_gh, 1)

            def cross(i, k):
                act.wait_ge(s_m2, 2 * i + 2)
                act.wait_ge(s_cw, i + 1)
                after(act, s_yo, i)
                act.activation(yc[:, :], YP[k][:, D:2 * D], ACT.Copy, scale=cw[k][:, :]).then_inc(s_yc, 1)

            def tile(i, k, it):
                gelu(i, 0)
                if not (isinstance(i, int) and i == 0):
                    cross(i - 1, (k - 1) % RING)
                gelu(i, 1)

            act.wait_ge(s_init, 32)
            act.wait_ge(s_ct, 4 * NG)
            tiles(act, tile)
            cross(TILES - 1, RING - 1)

        @block.vector
        def _(dve):
            dve.memset(yc[:, :], 0.0).then_inc(s_prep, 1)
            for p in range(2):
                dve.memset(parts[p][:, :, :], 0.0).then_inc(s_prep, 1)
            dve.memset(cum[:, :], 0.0).then_inc(s_prep, 1)
            dve.wait_ge(s_cst, N_CST)
            dve.tensor_tensor(gate_w[:, CK:2 * CK, 0:2, :], gate_w[:, CK:2 * CK, 0:2, :],
                              gate_w[:, 2 * CK:3 * CK, 0:2, :], ALU.add).then_inc(s_prep, 1)
            dve.memset(gate_w[:, 0:CK, 2, :], 0.0).then_inc(s_prep, 1)
            dve.tensor_copy(gate_w[:, CK:2 * CK, 2, :], cst[:, C_MEAN:C_F32].rearrange("p (c h) -> p c h", c=CK)
                            ).then_inc(s_prep, 1)
            dve.tensor_copy(cbf[:, :], wring[:, RING - 1, :].bitcast(F32)[:, 0:C_BF]).then_inc(s_cbf, 1)
            dve.wait_ge(s_rwt, 1)
            dve.tensor_copy(rwT[:, :, :], SF[:, 0:CK * NE].rearrange("p (c e) -> p c e", c=CK)).then_inc(s_rwc, 1)
            dve.wait_ge(s_prep, N_PREP)

            w8 = cst[:, C_W8:C_W8 + NE].unsqueeze(1).to_broadcast([P, G, NE])

            def spread(t):
                return t[:, :].unsqueeze(2).to_broadcast([P, G, NE])

            def x_stats(g, p, q):
                dve.wait_ge(s_x[p], 16 * (q + 1))
                for b in range(G):
                    after(dve, s_mv1, G * (g - 1) + b + 1)
                    dve.bn_stats(st1[:, b, :], xt[p][:, b, :]).then_inc(s_bn1, 1)
                after(dve, s_xn, G * g)
                after(dve, s_ve1, g)
                for b in range(G):
                    dve.wait_ge(s_bn1, G * g + b + 1)
                    apart(dve, s_apart["dve"])
                    dve.bn_aggr(mv1[:, b, :], st1[:, b, :]).then_inc(s_mv1, 1)

            def x_norm(g, p, q):
                dve.wait_ge(s_rs1, g + 1)
                after(dve, s_tq, G * g)
                for b in range(G):
                    dve.tensor_scalar(xn[:, b, :], xt[p][:, b, :], mv1[:, b, 0:1], rs1[:, b:b + 1],
                                      ALU.subtract, ALU.mult).then_inc(s_xn, 1)

            def gate_sums(g, p, q):
                dve.wait_ge(s_gt, G * (g + 1))
                after(dve, s_gT, g)
                after(dve, s_vc, g)
                dve.tensor_copy(gsb[:, :], SF[:, 0:3 * R]).then_inc(s_gsb, 1)

            def scores(g, p, q, h):
                dve.wait_ge(s_kq, 2 * g + h + 1)
                after(dve, s_pv, G * (g - 1) + 2 * h + 2)
                for par in range(2):
                    dve.wait_ge(s_dt, 2 * (2 * g + h) + par + 1)
                    dve.scalar_tensor_tensor(ct[h][:, par, :], KB[par][:, :], DH ** -0.5, dt_[h][:, par, :],
                                             ALU.mult, ALU.mult).then_inc(s_ct, 1)

            def x1_stats(g, p, q):
                dve.wait_ge(s_x1, g + 1)
                for b in range(G):
                    after(dve, s_mv2, G * (g - 1) + b + 1)
                    dve.bn_stats(st2[:, b, :], x1[p][:, b, :]).then_inc(s_bn2, 1)
                after(dve, s_xn2, G * g)
                after(dve, s_ve2, g)
                for b in range(G):
                    dve.wait_ge(s_bn2, G * g + b + 1)
                    apart(dve, s_apart["dve"])
                    dve.bn_aggr(mv2[:, b, :], st2[:, b, :]).then_inc(s_mv2, 1)

            def x1_norm(g, p, q):
                dve.wait_ge(s_rs2, g + 1)
                after(dve, s_rt, 2 * g)
                after(dve, s_hi, g)
                after(dve, s_lo, g)
                for b in range(G):
                    dve.tensor_scalar(xn2[:, b, :], x1[p][:, b, :], mv2[:, b, 0:1], rs2[:, b:b + 1],
                                      ALU.subtract, ALU.mult).then_inc(s_xn2, 1)

            def split_w1(g, p, q):
                dve.wait_ge(s_wh1, g + 1)
                dve.scalar_tensor_tensor(wcv[p][:, W1:2 * W1], wst[p][:, 0:W1], WSCALE, wcv[p][:, 0:W1],
                                         ALU.mult, ALU.subtract).then_inc(s_wl1, 1)

            def top_two(t, m):
                if t:
                    gt, pt, _ = t
                    dve.wait_ge(s_en, gt + 1)
                    dve.wait_ge(s_u, G * (gt + 1))
                    after(dve, s_n, 5 * gt)
                if m:
                    g = m[0]
                    dve.wait_ge(s_lg, g + 1)
                    after(dve, s_rk, 10 * g)
                    dve.tensor_copy(lg[:, :, :], LG.rearrange("p (b e) -> p b e", b=G)).then_inc(s_lgc, 1)
                if t:
                    dve.scalar_tensor_tensor(n0[:, :], u[:, :, DH], -1.0, u[:, :, DH], ALU.mult, ALU.max
                                             ).then_inc(s_n, 1)
                if m:
                    dve.wait_ge(s_lgc, g + 1)
                    dve.reduce_max(m1[:, :], lg[:, :, :], AX.X).then_inc(s_rk, 1)
                if t:
                    dve.wait_ge(s_n, 5 * gt + 1)
                    dve.tensor_tensor(n2[:, :], n0[:, :], en[pt][:, :], ALU.max).then_inc(s_n, 1)
                if m:
                    dve.wait_ge(s_rk, 10 * g + 1)
                    dve.tensor_tensor(eq[:, :, :], lg[:, :, :], spread(m1), ALU.is_equal).then_inc(s_rk, 1)
                if t:
                    dve.wait_ge(s_n, 5 * gt + 2)
                    dve.tensor_scalar(n1[:, :], n2[:, :], 1e-6, None, ALU.add).then_inc(s_n, 1)
                if m:
                    dve.wait_ge(s_rk, 10 * g + 2)
                    dve.tensor_tensor(key[:, :, :], eq[:, :, :], w8, ALU.mult).then_inc(s_rk, 1)
                if t:
                    dve.wait_ge(s_n, 5 * gt + 3)
                    dve.scalar_tensor_tensor(n2[:, :], n1[:, :], EPS, n1[:, :], ALU.mult, ALU.mult
                                             ).then_inc(s_n, 1)
                if m:
                    dve.wait_ge(s_rk, 10 * g + 3)
                    dve.reduce_max(km1[:, :], key[:, :, :], AX.X).then_inc(s_km, 1)
                    dve.wait_ge(s_km, 4 * g + 1)
                    dve.tensor_tensor(oh1[:, :, :], w8, spread(km1), ALU.is_equal).then_inc(s_km, 1)
                if t:
                    dve.wait_ge(s_sq, G * (gt + 1))
                    dve.reduce_sum(ss[:, :], sq, AX.X).then_inc(s_ss, 1)
                if m:
                    dve.wait_ge(s_km, 4 * g + 2)
                    dve.scalar_tensor_tensor(lg2[:, :, :], oh1[:, :, :], -3e38, lg[:, :, :], ALU.mult, ALU.add
                                             ).then_inc(s_rk, 1)
                if t:
                    dve.wait_ge(s_ss, gt + 1)
                    dve.wait_ge(s_n, 5 * gt + 4)
                    after(dve, s_hrs, gt)
                    dve.scalar_tensor_tensor(hv[:, :], ss[:, :], 1.0 / DH, n2[:, :], ALU.mult, ALU.add
                                             ).then_inc(s_n, 1)
                if m:
                    dve.wait_ge(s_rk, 10 * g + 4)
                    dve.reduce_max(m2[:, :], lg2[:, :, :], AX.X).then_inc(s_rk, 1)
                    dve.wait_ge(s_rk, 10 * g + 5)
                    dve.tensor_tensor(eq[:, :, :], lg2[:, :, :], spread(m2), ALU.is_equal).then_inc(s_rk, 1)
                    after(dve, s_e21, g)
                    dve.tensor_tensor(d21[:, :], m2[:, :], m1[:, :], ALU.subtract).then_inc(s_rk, 1)
                    dve.wait_ge(s_rk, 10 * g + 6)
                    dve.tensor_tensor(key[:, :, :], eq[:, :, :], w8, ALU.mult).then_inc(s_rk, 1)
                    dve.wait_ge(s_rk, 10 * g + 8)
                    dve.reduce_max(km2[:, :], key[:, :, :], AX.X).then_inc(s_km, 1)
                    dve.wait_ge(s_km, 4 * g + 3)
                    dve.tensor_tensor(oh2[:, :, :], w8, spread(km2), ALU.is_equal).then_inc(s_km, 1)
                    dve.wait_ge(s_km, 4 * g + 4)
                    dve.tensor_tensor(key[:, :, :], oh1[:, :, :], oh2[:, :, :], ALU.add).then_inc(s_rk, 1)
                    dve.wait_ge(s_rk, 10 * g + 9)
                    dve.tensor_copy(msk[:, :, :], key[:, :, :]).then_inc(s_msk, 1)
                    dve.reduce_sum(csum[:, :], key[:, :, :].rearrange("p b e -> p e b"), AX.X).then_inc(s_rk, 1)

            def gates_and_slots(n, m):
                if n:
                    gn, pn, _ = n
                    dve.wait_ge(s_gT, gn + 1)
                    dve.wait_ge(s_ga, gn + 1)
                    dve.tensor_scalar(gmn[:, :], SF[0:R, 2 * P:3 * P], gate_b[:, 1:2], 0.0, ALU.add, ALU.min
                                      ).then_inc(s_gmn, 1)
                    dve.tensor_scalar(gi[:, :], SF[0:R, P:2 * P], gate_b[:, 0:1], -1.0, ALU.add, ALU.mult
                                      ).then_inc(s_gi, 1)
                if m:
                    g, p, q = m
                    dve.wait_ge(s_rank, g + 1)
                    dve.wait_ge(s_rk, 10 * g + 10)
                    dve.tensor_tensor(rb[:, :, :], RK.rearrange("p (b e) -> p b e", b=G),
                                      cst[:, C_EBASE:C_EBASE + NE].unsqueeze(1).to_broadcast([P, G, NE]),
                                      ALU.add).then_inc(s_sl, 1)
                    dve.tensor_tensor(cum[:, :], cum[:, :], csum[:, :], ALU.add).then_inc(s_cu, 2)
                    dve.wait_ge(s_e21, g + 1)
                    dve.tensor_scalar(den[:, :], e21[:, :], 1.0, None, ALU.add).then_inc(s_mt, 1)
                    dve.wait_ge(s_sl, 3 * g + 1)
                    dve.tensor_tensor(a1[:, :, :], oh1[:, :, :], rb[:, :, :], ALU.mult).then_inc(s_sl, 1)
                    dve.tensor_tensor(a2[:, :, :], oh2[:, :, :], rb[:, :, :], ALU.mult).then_inc(s_sl, 1)
                    dve.wait_ge(s_mt, 5 * g + 1)
                    dve.reciprocal(c1[:, :], den[:, :]).then_inc(s_mt, 1)
                    after(dve, s_sc[p], 16 * 2 * G * q)
                    dve.wait_ge(s_sl, 3 * g + 3)
                    for k, a in enumerate((a1, a2)):
                        dve.reduce_sum(sf[:, k, :], a[:, :, :], AX.X).then_inc(s_sf, 1)
                    dve.wait_ge(s_mt, 5 * g + 2)
                    dve.tensor_tensor(c2[:, :], e21[:, :], c1[:, :], ALU.mult).then_inc(s_mt, 1)
                    dve.wait_ge(s_sf, 2 * g + 2)
                    dve.tensor_copy(slot[p][:, :, :], sf[:, :, :]).then_inc(s_slot, 2)
                    dve.wait_ge(s_mt, 5 * g + 3)
                    dve.tensor_tensor(den[:, :], c1[:, :], c2[:, :], ALU.subtract).then_inc(s_mt, 1)
                    dve.tensor_scalar(rowb[p][:, :, D + 2], c2[:, :], 1.0 / WSCALE, None, ALU.mult)
                    dve.tensor_scalar(rowb[p][:, :, D + 3], km1[:, :], -1.0, float(NE), ALU.mult, ALU.add)
                    dve.tensor_copy(rowb[p][:, :, D].bitcast(I32), tok[:, :]).then_inc(s_mt, 1)
                    dve.wait_ge(s_mt, 5 * g + 5)
                    dve.tensor_scalar(tok[:, :], tok[:, :], float(G * P), None, ALU.add)
                    dve.tensor_scalar(rowb[p][:, :, D + 1], den[:, :], 1.0 / WSCALE, None, ALU.mult
                                      ).then_inc(s_meta, 1)

            def scans(g, p, q):
                dve.wait_ge(s_gl, g + 1)
                dve.wait_ge(s_gmn, g + 1)
                dve.tensor_tensor_scan(gcs[:, :], gmn[:, :], gl_[:, :], 0.0, ALU.add, ALU.subtract).then_inc(s_gcs, 1)
                dve.wait_ge(s_gcs, g + 1)
                dve.wait_ge(s_gi, g + 1)
                dve.tensor_tensor(gm[:, 0, :], gi[:, :], gcs[:, :], ALU.add).then_inc(s_ng, 1)
                dve.wait_ge(s_ng, g + 1)
                dve.tensor_tensor_scan(gm[:, 1, :], gm[:, 0, :], gm[:, 0, :], 3e38, ALU.min, ALU.min).then_inc(s_gmx, 1)
                dve.wait_ge(s_gmx, g + 1)
                after(dve, s_nT, g)
                dve.tensor_tensor(gnm[:, :], gm[:, 1, :], gcs[:, :], ALU.subtract).then_inc(s_gnm, 1)
                after(dve, s_d, 4 * (g - 1))
                dve.tensor_copy(parts[p][0:R, :, :], gm[:, :, :]).then_inc(s_pt, 1)
                dve.wait_ge(s_pt, PARTS * g + 1)
                dve.tensor_tensor(gr[:, :, :], gm[:, :, :], parts[p][0:R, :, :], ALU.subtract).then_inc(s_gr, 1)
                dve.wait_ge(s_gr, 3 * g + 1)
                dve.tensor_copy(parts[p][32:32 + R, :, :], gr[:, :, :]).then_inc(s_pt, 1)
                dve.tensor_copy(grb[:, :, :], gr[:, :, :]).then_inc(s_gr, 1)
                dve.wait_ge(s_gr, 3 * g + 2)
                dve.tensor_tensor(gr2[:, :, :], gr[:, :, :], grb[:, :, :], ALU.subtract).then_inc(s_gr, 1)
                dve.wait_ge(s_gr, 3 * g + 3)
                dve.tensor_copy(parts[p][64:64 + R, :, :], gr2[:, :, :]).then_inc(s_pt, 1)
                dve.wait_ge(s_pt, PARTS * (g + 1))
                dve.tensor_tensor(mblk[p][:, :, :], parts[p][:, 1:2, :].to_broadcast([KP, NH, P]),
                                  cbf[0:KP, B_HMASK:B_HMASK + NH].unsqueeze(2).to_broadcast([KP, NH, P]),
                                  ALU.mult).then_inc(s_mb, 1)

            def head_norm(g, p, q):
                dve.wait_ge(s_hrs, g + 1)
                dve.wait_ge(s_ss, g + 1)
                dve.tensor_tensor(sq, u[:, :, 0:DH], hrs[:, :].unsqueeze(2).to_broadcast([P, R, DH]),
                                  ALU.mult).then_inc(s_tt, 1)
                dve.wait_ge(s_tt, g + 1)
                dve.tensor_tensor(xn2[:, :, :], xn2[:, :, :], gam[:, :].unsqueeze(1).to_broadcast([P, G, D]),
                                  ALU.mult).then_inc(s_tg, 1)

            def step(n, t, m):
                if m:
                    x1_norm(*m)
                if n:
                    x_stats(*n)
                if t:
                    scores(*t, 0)
                if n:
                    x_norm(*n)
                if t:
                    scores(*t, 1)
                top_two(t, m)
                if n:
                    gate_sums(*n)
                if t:
                    split_w1(*t)
                gates_and_slots(n, m)
                if t:
                    head_norm(*t)
                if n:
                    scans(*n)
                if t:
                    x1_stats(*t)

            dve.tensor_copy(ident_h[:, :], ident)
            dve.wait_ge(s_cbf, 1)
            dve.tensor_copy(tri_h[:, :], cbf[:, B_TRI:B_TRI + P])
            dve.tensor_copy(tok[:, :], cst[:, C_TOK:C_TOK + G])
            dve.tensor_copy(ones_h[:, :], cbf[:, B_ONES:B_ONES + P]).then_inc(s_prep, 1)
            groups(dve, step)

            step = [0]

            def link(ins):
                step[0] += 1
                ins.then_inc(s_tb, 1)
                dve.wait_ge(s_tb, step[0])

            i_b = cst[:, C_TILE:C_TILE + TILES]
            dve.wait_ge(s_cnt, 1)
            dve.wait_ge(s_lo, NG)
            link(dve.tensor_copy(ncnt[:, :], T0[:, 0:NE]))
            link(dve.tensor_tensor(te3[:, :, :], ncnt[:, :].unsqueeze(2).to_broadcast([P, NE, NB]),
                                   cst[:, C_THR:C_THR + NB].unsqueeze(1).to_broadcast([P, NE, NB]), ALU.is_gt))
            link(dve.reduce_sum(te[:, :], te3[:, :, :], AX.X))
            link(dve.tensor_tensor_scan(ctl[:, :], te[:, :], te[:, :], 0.0, ALU.add, ALU.bypass))
            link(dve.tensor_scalar(wt[:, :], te[:, :], -1.0, float(REGION // P), ALU.mult, ALU.add))
            link(dve.tensor_tensor(le[:, :, :], i_b.unsqueeze(2).to_broadcast([P, TILES, NE]),
                                   ctl[:, :].unsqueeze(1).to_broadcast([P, TILES, NE]), ALU.is_ge))
            link(dve.reduce_sum(idr[:, :], le[:, :, :], AX.X))
            link(dve.tensor_scalar(etab[:, :], idr[:, :], float(NE - 1), None, ALU.min))
            link(dve.tensor_tensor(lw[:, :, :], le[:, :, :], wt[:, :].unsqueeze(1).to_broadcast([P, TILES, NE]),
                                   ALU.mult))
            link(dve.reduce_sum(adr[:, :], lw[:, :, :], AX.X))
            link(dve.tensor_tensor(ad2[:, :], adr[:, :], i_b, ALU.add))
            link(dve.tensor_scalar(adr[:, :], ad2[:, :], float(SPARE // P), float(P), ALU.min, ALU.mult))
            link(dve.memset(chg[:, 0:RING], 1.0))
            link(dve.tensor_tensor(chg[:, RING:TILES], etab[:, RING:TILES], etab[:, 0:TILES - RING], ALU.not_equal))
            link(dve.tensor_copy(tab[:, 0, :], etab[:, :]))
            link(dve.tensor_copy(tab[:, 1, :], adr[:, :]))
            link(dve.tensor_copy(tab[:, 2, :], chg[:, :]))
            dve.tensor_tensor(padr[:, :], ncnt[:, :], cst[:, C_EBASE:C_EBASE + NE], ALU.add).then_inc(s_tab, 1)

            YP = [KE, KO, UB]
            xp = SF[:, 0:CK * P].bitcast(F16)

            def copies(i, k, it):
                dve.wait_ge(s_xtp, i + 1)
                after(dve, s_h, 2 * (i - RING + 1))
                dve.tensor_copy(xT[k][:, :, :], xp.rearrange("p (j n) -> p j n", j=2 * CK)).then_inc(s_xtc, 1)
                after(dve, s_yo, i - RING + 1)
                after(dve, s_yc, i - RING + 1)
                after(dve, s_cw, i)
                dve.tensor_scalar(cw0[:, :], xrow[k][:, D + 3:D + 4], etab[:, bass.ds(i, 1)],
                                  xrow[k][:, D + 1:D + 2], ALU.is_equal, ALU.mult).then_inc(s_cw0, 1)
                dve.wait_ge(s_cw0, i + 1)
                after(dve, s_sa, 16 * (i - RING + 1))
                dve.tensor_copy(dst[k][:, :], xrow[k][:, D:D + 1].bitcast(I32))
                dve.tensor_tensor(cw[k][:, :], cw0[:, :], xrow[k][:, D + 2:D + 3], ALU.add).then_inc(s_cw, 1)

            def low(i, a):
                dve.wait_ge(s_gf, 2 * i + a + 1)
                dve.wait_ge(s_gh, 2 * i + a + 1)
                after(dve, s_m2, 2 * i + a - 1)
                dve.tensor_tensor(gl[a][:, :, :], gf[a].rearrange("p (m n) -> p m n", m=4),
                                  gh[a][:, :, :], ALU.subtract).then_inc(s_glo, 1)

            def sum_up(i, k):
                dve.wait_ge(s_yc, i + 1)
                after(dve, s_sa, 16 * (i - RING + 1))
                dve.scalar_tensor_tensor(yo[k], YP[k][:, 0:D], cw[k][:, 0:1], yc[:, :], ALU.mult, ALU.add
                                         ).then_inc(s_yo, 1)

            def tile(i, k, it):
                low(i, 0)
                if not (isinstance(i, int) and i == 0):
                    sum_up(i - 1, (k - 1) % RING)
                if not (isinstance(i, int) and i == TILES - 1):
                    copies(i + 1, (k + 1) % RING, it + (k + 1) // RING)
                low(i, 1)

            copies(0, 0, 0)
            tiles(dve, tile)
            sum_up(TILES - 1, RING - 1)

        @block.gpsimd
        def _(pool):
            for p in range(2):
                pool.memset(vt[p][:, :, :, DH:DH + 1], 1.0).then_inc(s_prepg, 1)
            pool.memset(mhalf[:, :], -0.5).then_inc(s_prepg, 1)
            pool.wait_ge(s_prepg, 3)
            pool.wait_ge(s_cst, N_CST)

            def x_rstd(g, p, q):
                pool.wait_ge(s_mv1, G * (g + 1))
                after(pool, s_rs1, g)
                apart(pool, s_apart["pool"])
                pool.tensor_scalar(ve1[:, :], mv1[:, :, 1], EPS, None, ALU.add).then_inc(s_ve1, 1)
                pool.wait_ge(s_ve1, g + 1)
                after(pool, s_xn, G * g)
                pool.tensor_tensor(rs1[:, :], ve1[:, :], mhalf[:, 0:G], ALU.pow).then_inc(s_rs1, 1)

            def centre(g, p, q):
                pool.wait_ge(s_gsb, g + 1)
                pool.wait_ge(s_c[p], 16 * (q + 1))
                after(pool, s_pv, G * (g - 1))
                pool.tensor_tensor(vt[p][:, :, :, 0:DH].rearrange("p b h d -> p (b h) d"),
                                   ctn[p][:, :, :].rearrange("p b (h d) -> p (b h) d", h=NH),
                                   gsb[:, 2 * R:3 * R].unsqueeze(2).to_broadcast([P, R, DH]),
                                   ALU.subtract).then_inc(s_vc, 1)

            def head_rstd(g, p, q):
                pool.wait_ge(s_n, 5 * g + 5)
                after(pool, s_tt, g)
                pool.tensor_tensor(hrs[:, :], hv[:, :], mhalf[:, :], ALU.pow).then_inc(s_hrs, 1)

            def residual(g, p, q):
                pool.wait_ge(s_tg, g + 1)
                pool.wait_ge(s_xc[p], 16 * (q + 1))
                pool.tensor_tensor(x1[p][:, :, :], x1[p][:, :, :], xn2[:, :, :], ALU.add).then_inc(s_x1, 1)

            def x1_rstd(g, p, q):
                pool.wait_ge(s_mv2, G * (g + 1))
                after(pool, s_rs2, g)
                apart(pool, s_apart["pool"])
                pool.tensor_scalar(ve2[:, :], mv2[:, :, 1], EPS, None, ALU.add).then_inc(s_ve2, 1)
                pool.wait_ge(s_ve2, g + 1)
                after(pool, s_xn2, G * g)
                pool.tensor_tensor(rs2[:, :], ve2[:, :], mhalf[:, 0:G], ALU.pow).then_inc(s_rs2, 1)

            def split_w2(g, p, q):
                pool.wait_ge(s_wh2, g + 1)
                v = wcv[p][:, 2 * W1:].rearrange("p (m k n) -> p m k n", m=MK, k=2)
                pool.tensor_tensor(v[:, :, 1, :], wst[p][:, W1:W1 + W2].rearrange("p (m n) -> p m n", m=MK),
                                   v[:, :, 0, :], ALU.subtract).then_inc(s_wl2, 1)

            def row_low(g, p, q):
                pool.wait_ge(s_hi, g + 1)
                pool.tensor_tensor(rowb[p][:, :, D // 2:D].bitcast(F16), xn2[:, :, :],
                                   rowb[p][:, :, 0:D // 2].bitcast(F16), ALU.subtract).then_inc(s_lo, 1)

            def scatter(g, p, q, half):
                if half == 0:
                    pool.wait_ge(s_lo, g + 1)
                    pool.wait_ge(s_meta, g + 1)
                    pool.wait_ge(s_slot, 2 * (g + 1))
                    apart(pool, s_apart["pool"])
                for b in (0, 1) if half == 0 else (2, 3):
                    for k in range(2):
                        pool.indirect_dma_start(
                            out=rows[:, :], out_offset=bass.IndirectOffsetOnAxis(ap=slot[p][:, k, b:b + 1], axis=0),
                            in_=rowb[p][:, b, :], in_offset=None).then_inc(s_sc[p], 16)

            def step(n, t, m):
                if n:
                    x_rstd(*n)
                if m:
                    row_low(*m)
                if t:
                    head_rstd(*t)
                if n:
                    centre(*n)
                if m:
                    scatter(*m, 0)
                if t:
                    residual(*t)
                if m:
                    scatter(*m, 1)
                if t:
                    x1_rstd(*t)
                    split_w2(*t)

            groups(pool, step)

            for p in range(2):
                pool.wait_ge(s_x1o[p], 16 * NG // 2)
            pool.wait_ge(s_init, 32)

            def tile(i, k, it):
                pool.wait_ge(s_yo, i + 1)
                pool.wait_ge(s_cw, i + 1)
                after(pool, s_sa, 16 * i)
                apart(pool, s_apart["pool"])
                pool.indirect_dma_start(
                    out=out[:, :], out_offset=bass.IndirectOffsetOnAxis(ap=dst[k][:, 0:1], axis=0),
                    in_=yo[k], in_offset=None, compute_op=ALU.add).then_inc(s_sa, 16)

            tiles(pool, tile)
            pool.wait_ge(s_sa, 16 * TILES)


def constants():
    part = np.arange(P)
    cf = np.zeros((P, C_F32), np.float32)
    cf[:, C_IDENT:C_IDENT + P] = np.eye(P)
    cf[:, C_W8:C_W8 + NE] = NE - np.arange(NE)
    cf[:, C_EBASE:C_EBASE + NE] = REGION * np.arange(NE)
    cf[:, C_THR:C_THR + NB] = P * np.arange(NB)
    cf[:, C_TILE:C_TILE + TILES] = np.arange(TILES)
    cf[:, C_TOK:C_TOK + G] = P * np.arange(G)[None] + part[:, None]
    head = (P * np.arange(CK)[None] + part[:, None]) // DH
    cf[:, C_MEAN:C_F32] = (head[:, :, None] == np.arange(NH)).reshape(P, CK * NH) / DH
    cb = np.zeros((P, C_BF), np.float32)
    cb[:, B_IDENT:B_IDENT + P] = np.eye(P)
    mask = np.where(part[None] < part[:, None], NEG, 0.0)
    cb[:, B_MASK:B_MASK + 2 * P] = np.concatenate([mask, mask], 1)
    for q in range(PARTS):
        for b in range(G):
            for h in range(NH):
                r = 32 * q + NH * b + h
                cb[r, B_SEL + b * P:B_SEL + (b + 1) * P] = 1.0
                col = B_HSEL + ((b * 2 + h % 2) * 2 + h // 2) * P
                cb[r, col:col + P] = -1.0
                cb[r, B_HMASK + 2 * (h % 2) + h // 2] = 1.0
    cb[:, B_TRI:B_TRI + P] = part[:, None] < part[None]
    cb[:, B_ONES:B_ONES + P] = 1.0
    pad = np.zeros((P, ROW), np.float32)
    pad[:, D] = (NT + part).astype(np.int32).view(np.float32)
    return cf, cb, pad


_INS = ["x", "ctx_1024", "L0_xattn_igate_kernel", "L0_xattn_igate_bias", "L0_xattn_fgate_kernel",
        "L0_xattn_fgate_bias", "L0_xattn_outnorm_scale", "L0_ffn_router_w", "L0_ffn_w1", "L0_ffn_w2"]


def kernel(**inputs):
    import concourse.bacc as bacc
    from concourse.bass_utils import run_bass_kernel_spmd

    nc = bacc.Bacc("TRN2", target_bir_lowering=False, num_devices=1)
    arrays, args = {}, []
    named = [(n, np.ascontiguousarray(inputs[n])) for n in _INS]
    named += list(zip(("const_f32", "const_selectors", "const_pad"), constants()))
    for name, a in named:
        arrays[f"in_{name}"] = a
        args.append(nc.dram_tensor(f"in_{name}", a.shape, mybir.dt.from_np(a.dtype), kind="ExternalInput").ap())
    out = nc.dram_tensor("out", (NT + P, D), F32, kind="ExternalOutput").ap()
    build(nc, *args, out)
    r = run_bass_kernel_spmd(nc, [arrays], core_ids=[0])
    return r.results[0]["out"][:NT].reshape(NB, S, D)
```

```python
from contextlib import ExitStack

import numpy as np

import concourse.bass as bass
from concourse import mybir

ALU = mybir.AluOpType
ACT = mybir.ActivationFunctionType
AX = mybir.AxisListType
F32, F16, BF16, I32 = mybir.dt.float32, mybir.dt.float16, mybir.dt.bfloat16, mybir.dt.int32

P = 128
NB, S, D = 32, 128, 256
NH, DH = 4, 64
NE, HID = 8, 1024
G = 4
NG = NB // G
NT = NB * S
CK = D // P
MK = HID // P
R = G * NH
FG = 32
PARTS = 3
KP = 32 * (PARTS - 1) + 32
ROW = D + 4
REGION = NT + P
RING = 3
TILES = -(-(2 * NT // P + NE - 1) // RING) * RING
SPARE = NE * REGION
PIECES = 2
WSCALE = 16.0
W1, W2 = CK * HID, MK * D
EPS = 1e-5
NEG = -1e30

C_IDENT = 0
C_W8 = C_IDENT + P
C_EBASE = C_W8 + NE
C_THR = C_EBASE + NE
C_TILE = C_THR + NB
C_TOK = C_TILE + TILES
C_F32 = C_TOK + G
B_IDENT = 0
B_MASK = B_IDENT + P
B_SEL = B_MASK + 2 * P
B_HSEL = B_SEL + G * P
B_HMASK = B_HSEL + G * NH * P
B_TRI = B_HMASK + NH
B_ONES = B_TRI + P
C_BF = B_ONES + P


def after(eng, sem, value):
    if isinstance(value, int) and value <= 0:
        return
    eng.wait_ge(sem, value)


def apart(eng, sem):
    eng.sem_inc(sem, 1)


def build(nc, x, ctx_in, ig_k, ig_b, fg_k, fg_b, gamma, router_w, w1, w2, cf, cb, pad_rows, out):
    with ExitStack() as stack:
        def sb(name, shape, dt=F32):
            return stack.enter_context(nc.sbuf_tensor(name, shape, dt))

        def ps(name, shape, dt=F32):
            return stack.enter_context(nc.psum_tensor(name, shape, dt))

        def sem(name):
            return stack.enter_context(nc.semaphore(name))

        rows = nc.dram_tensor("rows", (SPARE + P, ROW), F32, kind="Internal").ap()
        wsplit = nc.dram_tensor("wsplit", (NE, P, 2 * (W1 + W2)), F16, kind="Internal").ap()

        cst = sb("cst", [P, C_F32])
        cbf = sb("cbf", [P, C_BF], BF16)
        ident = cst[:, C_IDENT:C_IDENT + P]
        ident_h = sb("ident_h", [P, P], F16)
        tri_h = sb("tri_h", [P, P], F16)
        ones_h = sb("ones_h", [P, P], F16)
        pad = sb("pad", [P, ROW])
        gate_w = sb("gate_w", [P, 3 * CK, 2, NH])
        gate_wb = sb("gate_wb", [P, 2 * CK, G, FG + R])
        gate_b = sb("gate_b", [FG + R, 1])
        gam = sb("gam", [P, D])
        rw = sb("rw", [NE, D])
        rwT = sb("rwT", [P, CK, NE])
        mhalf = sb("mhalf", [P, R])

        xt = [sb(f"xt{p}", [P, G, D]) for p in range(2)]
        vt = [sb(f"vt{p}", [P, G, NH, DH + 1]) for p in range(2)]
        xn = sb("xn", [P, G, D])
        st1 = sb("st1", [P, G, 6])
        mv1 = sb("mv1", [P, G, 2])
        ve1 = sb("ve1", [P, G])
        rs1 = sb("rs1", [P, G])
        qkT = [sb(f"qkT{p}", [P, G, 2 * CK, P]) for p in range(2)]
        vsum = sb("vsum", [P, R])
        vmean = sb("vmean", [P, R])
        ga = sb("ga", [R, P])
        ge = sb("ge", [R, P])
        gl_ = sb("gl_", [R, P])
        gmn = sb("gmn", [R, P])
        gcs = sb("gcs", [R, P])
        gi = sb("gi", [R, P])
        gm = sb("gm", [R, 2, P])
        gr = sb("gr", [R, 2, P])
        gr2 = sb("gr2", [R, 2, P])
        grb = sb("grb", [R, 2, P], BF16)
        gnm = sb("gnm", [R, P])
        parts = [sb(f"parts{p}", [KP, 2, P], BF16) for p in range(2)]
        mblk = [sb(f"mblk{p}", [KP, NH, P], BF16) for p in range(2)]
        en = [sb(f"en{p}", [P, R]) for p in range(2)]
        dt_ = [sb(f"dt{i}", [P, 2, 512]) for i in range(2)]
        ct = [sb(f"ct{i}", [P, 2, 512]) for i in range(2)]
        u = sb("u", [P, R, DH + 1])
        ss = sb("ss", [P, R])
        n0 = sb("n0", [P, R])
        n1 = sb("n1", [P, R])
        n2 = sb("n2", [P, R])
        hv = sb("hv", [P, R])
        hrs = sb("hrs", [P, R])
        x1 = [sb(f"x1_{p}", [P, G, D]) for p in range(2)]
        st2 = sb("st2", [P, G, 6])
        mv2 = sb("mv2", [P, G, 2])
        ve2 = sb("ve2", [P, G])
        rs2 = sb("rs2", [P, G])
        xn2 = sb("xn2", [P, G, D])
        hn = xn2[:, :, :].rearrange("p b (h d) -> p (b h) d", h=NH)
        sq = sb("sq", [P, R, DH])[:, :, :]
        ctn = [sb(f"ctn{p}", [P, G, D]) for p in range(2)]
        rT = sb("rT", [P, G, CK, P])
        rowb = [sb(f"rowb{p}", [P, G, ROW]) for p in range(2)]
        lg = sb("lg", [P, G, NE])
        lg2 = sb("lg2", [P, G, NE])
        eq = sb("eq", [P, G, NE])
        key = sb("key", [P, G, NE])
        m1 = sb("m1", [P, G])
        m2 = sb("m2", [P, G])
        km1 = sb("km1", [P, G])
        km2 = sb("km2", [P, G])
        oh1 = sb("oh1", [P, G, NE])
        oh2 = sb("oh2", [P, G, NE])
        msk = sb("msk", [P, G, NE], F16)
        cum = sb("cum", [P, NE], F16)
        csum = sb("csum", [P, NE])
        sf = sb("sf", [P, 2, G])
        d21 = sb("d21", [P, G])
        e21 = sb("e21", [P, G])
        den = sb("den", [P, G])
        c1 = sb("c1", [P, G])
        c2 = sb("c2", [P, G])
        rb = sb("rb", [P, G, NE])
        a1 = sb("a1", [P, G, NE])
        a2 = sb("a2", [P, G, NE])
        slot = [sb(f"slot{p}", [P, 2, G], I32) for p in range(2)]
        tok = sb("tok", [P, G])
        wcv = [sb(f"wcv{p}", [P, 2 * (W1 + W2)], F16) for p in range(2)]
        wring = sb("wring", [P, RING, 2 * (W1 + W2)], F16)
        wst = [wring[:, p, :].bitcast(F32) for p in range(2)]

        te3 = xn2[:, :, :].rearrange("p r d -> p (r d)")[:, 0:NE * NB].rearrange("p (e j) -> p e j", e=NE)
        te = sb("te", [P, NE])
        ncnt = sb("ncnt", [P, NE])
        ctl = sb("ctl", [P, NE])
        wt = sb("wt", [P, NE])
        le, lw = (t[:, :, :].rearrange("p a n -> p (a n)")[:, 0:TILES * NE].rearrange("p (i e) -> p i e", e=NE)
                  for t in (dt_[0], ct[0]))
        idr = sb("idr", [P, TILES])
        etab = sb("etab", [P, TILES])
        adr = sb("adr", [P, TILES])
        ad2 = sb("ad2", [P, TILES])
        chg = sb("chg", [P, TILES])
        tab = sb("tab", [P, 3, TILES], I32)
        padr = sb("padr", [P, NE], I32)

        xrow = [sb(f"xrow{i}", [P, ROW]) for i in range(RING)]
        free = dt_[0][:, :, :].rearrange("p a n -> p (a n)")
        xT = [free[:, D * i:D * (i + 1)].bitcast(F16).rearrange("p (j n) -> p j n", j=2 * CK) for i in range(RING)]
        gf = [dt_[1][:, a, :] for a in range(2)]
        gh, gl = ([ct[0][:, i, :].bitcast(F16)[:, 4 * P * a:4 * P * (a + 1)].rearrange("p (m n) -> p m n", m=4)
                   for a in range(2)] for i in range(2))
        cw0 = sb("cwd", [P, 1])
        cw = [sb(f"cw{i}", [P, 1]) for i in range(RING)]
        yc = free[:, D * RING:D * (RING + 1)]
        yo = [ct[1][:, :, :].rearrange("p a n -> p (a n)")[:, D * i:D * (i + 1)] for i in range(RING)]
        dst = [sb(f"dst{i}", [P, 1], I32) for i in range(RING)]

        bank = [ps(f"bank{i}", [P, 512]) for i in range(8)]
        T0, T1, KE, KO, DE, DO, UB, SF = bank
        TB, KB, DB = [T0, T1], [KE, KO], [DE, DO]
        VB = [UB, KE, KO, UB]
        LG = DE[:, 0:G * NE]
        RK = T1[:, 0:G * NE]

        s_cst = sem("constants_loaded")
        s_gb = sem("gate_biases_loaded")
        s_cbf = sem("selectors_loaded")
        s_prep = sem("prepared_by_vector")
        s_prepg = sem("prepared_by_pool")
        s_rwt = sem("router_transposed")
        s_rwc = sem("router_copied")
        s_x = [sem(f"x_loaded{p}") for p in range(2)]
        s_c = [sem(f"ctx_loaded{p}") for p in range(2)]
        s_xc = [sem(f"x_copied{p}") for p in range(2)]
        s_vc = sem("values_centred")
        s_wst = [sem(f"weights_loaded{p}") for p in range(2)]
        s_bn1 = sem("x_stats")
        s_mv1 = sem("x_mean_var")
        s_ve1 = sem("x_var_eps")
        s_rs1 = sem("x_rstd")
        s_xn = sem("x_normed")
        s_tq = sem("qk_transposed")
        s_qk = sem("qk_copied")
        s_gt = sem("gates_summed")
        s_vs = sem("ctx_summed")
        s_vm = sem("ctx_means")
        s_ga = sem("gate_abs")
        s_ge = sem("gate_exp")
        s_gl = sem("gate_log")
        s_gmn = sem("gate_min")
        s_gcs = sem("gate_cumsum")
        s_gi = sem("gate_input")
        s_ng = sem("gate_ng")
        s_gmx = sem("gate_cummax")
        s_gnm = sem("gate_neg_logd")
        s_pt = sem("gate_parts")
        s_gr = sem("gate_rests")
        s_mb = sem("gate_blocks")
        s_nT = sem("neg_logd_transposed")
        s_en = sem("neg_logd_exp")
        s_d = sem("logd_summed")
        s_dt = sem("decay_ready")
        s_kq = sem("kq_ready")
        s_ct = sem("scores_ready")
        s_pv = sem("pv_ready")
        s_u = sem("pv_copied")
        s_sq = sem("pv_squared")
        s_ss = sem("pv_sumsq")
        s_n = sem("normaliser_steps")
        s_hrs = sem("head_rstd")
        s_tt = sem("head_scaled")
        s_tg = sem("head_gamma")
        s_x1 = sem("x1_ready")
        s_x1o = [sem(f"x1_stored{p}") for p in range(2)]
        s_bn2 = sem("x1_stats")
        s_mv2 = sem("x1_mean_var")
        s_ve2 = sem("x1_var_eps")
        s_rs2 = sem("x1_rstd")
        s_xn2 = sem("x1_normed")
        s_hi = sem("row_high")
        s_lo = sem("row_low")
        s_rt = sem("x1n_transposed")
        s_rTc = sem("x1n_T_copied")
        s_lg = sem("logits_ready")
        s_lgc = sem("logits_copied")
        s_rk = sem("router_steps")
        s_km = sem("top_two_steps")
        s_sl = sem("slot_steps")
        s_sf = sem("slot_sums")
        s_cu = sem("count_steps")
        s_mt = sem("meta_steps")
        s_msk = sem("expert_masks")
        s_e21 = sem("router_exp")
        s_rank = sem("ranks_ready")
        s_slot = sem("slots_ready")
        s_meta = sem("row_meta")
        s_sc = [sem(f"rows_scattered{p}") for p in range(2)]
        s_w16 = sem("second_weights_scaled")
        s_wh1 = sem("first_weights_high")
        s_wh2 = sem("second_weights_high")
        s_wl1 = sem("first_weights_low")
        s_wl2 = sem("second_weights_low")
        s_wl2v = sem("last_second_weights_low")
        s_x1v = sem("last_x1_ready")
        s_wo = [sem(f"weights_stored{p}") for p in range(2)]
        s_cnt = sem("counts_ready")
        s_tb = sem("table_steps")
        s_pr = sem("pad_rows_known")
        s_tab = sem("table_ready")
        s_pad = sem("pads_stored")
        s_xr = [sem(f"tile_loaded{i}") for i in range(RING)]
        s_wr1 = [sem(f"tile_first_weights{i}") for i in range(RING)]
        s_wr2 = [sem(f"tile_second_weights{i}") for i in range(RING)]
        s_xtp = sem("tile_transposed")
        s_xtc = sem("tile_T_copied")
        s_h = sem("hidden_ready")
        s_gf = sem("gelu_full")
        s_gh = sem("gelu_high")
        s_glo = sem("gelu_low")
        s_m2 = sem("out_half_done")
        s_cw0 = sem("row_weight_step")
        s_cw = sem("row_weight")
        s_yc = sem("out_cross_copied")
        s_yo = sem("out_ready")
        s_sa = sem("out_added")
        s_apart = {n: sem(f"waits_apart_{n}") for n in ("sp", "pe", "dve", "pool")}
        N_CST = 16 * 6
        N_PREP = 6

        def groups(eng, step):
            def group(g):
                return (g, g % 2, g // 2) if 0 <= g < NG else None

            for t in range(-2, 2):
                step(*(group(t + i) for i in (2, 1, 0, -1, -2)))
            with eng.Fori(1, NG // 2 - 1) as q:
                even = [(2 * q + 2 * i, 0, q + i) for i in (1, 0, -1)]
                odd = [(2 * q + 2 * i + 1, 1, q + i) for i in (1, 0, -1)]
                step(even[0], odd[1], even[1], odd[2], even[2])
                step(odd[0], even[0], odd[1], even[1], odd[2])
            for t in range(NG - 2, NG + 2):
                step(*(group(t + i) for i in (2, 1, 0, -1, -2)))

        def tiles(eng, tile):
            for i in range(RING):
                tile(i, i, 0)
            with eng.Fori(1, TILES // RING - 1) as it:
                for i in range(RING):
                    tile(RING * it + i, i, it)
            for i in range(RING):
                tile(TILES - RING + i, i, TILES // RING - 1)

        block = stack.enter_context(nc.Block())

        @block.sync
        def _(sp):
            gk_i = ig_k.rearrange("(c p) h -> p c h", p=P)
            gk_f = fg_k.rearrange("(c p) h -> p c h", p=P)
            sp.dma_start(xt[0][:, :, :], x[0:G].rearrange("b p d -> p b d")).then_inc(s_x[0], 16)
            sp.dma_start(cst[:, :], cf).then_inc(s_cst, 16)
            sp.dma_start(gate_w[:, :, 0, :], gk_i).then_inc(s_cst, 16)
            sp.dma_start(gate_w[:, :, 1, :], gk_f).then_inc(s_cst, 16)
            sp.dma_start(gam[:, :], gamma.rearrange("(o d) -> o d", o=1).to_broadcast([P, D])).then_inc(s_cst, 16)
            sp.dma_start(rw[:, :], router_w).then_inc(s_cst, 16)
            sp.dma_start(pad[:, :], pad_rows).then_inc(s_cst, 16)

            def load_x(g, p, q):
                after(sp, s_xn, G * (g - 1))
                apart(sp, s_apart["sp"])
                after(sp, s_xc[p], 16 * q)
                if isinstance(g, int) and g == 0:
                    return
                sp.dma_start(xt[p][:, :, :], x[bass.ds(g * G, G)].rearrange("b p d -> p b d")).then_inc(s_x[p], 16)

            def load_c(g, p, q):
                after(sp, s_tq, G * (g - 1))
                after(sp, s_vc, g - 1)
                sp.dma_start(ctn[p][:, :, :], ctx_in[bass.ds(g * G, G)].rearrange("b p d -> p b d")
                             ).then_inc(s_c[p], 16)

            def load_w(g, p, q):
                after(sp, s_wl1, g - 1)
                apart(sp, s_apart["sp"])
                after(sp, s_wl2, 2 * (g - 1))
                sp.dma_start(wst[p][:, 0:W1].rearrange("p (c n) -> p c n", c=CK),
                             w1[bass.ds(g, 1)].rearrange("o (c p) n -> p (o c) n", p=P)).then_inc(s_wst[p], 16)
                sp.dma_start(wst[p][:, W1:W1 + W2].rearrange("p (m n) -> p m n", m=MK),
                             w2[bass.ds(g, 1)].rearrange("o (m p) n -> p (o m) n", p=P)).then_inc(s_wst[p], 16)

            def copy_x(g, p, q):
                sp.wait_ge(s_x[p], 16 * (q + 1))
                apart(sp, s_apart["sp"])
                after(sp, s_xn2, G * (g - 1))
                apart(sp, s_apart["sp"])
                after(sp, s_x1o[p], 16 * q)
                sp.dma_start(x1[p][:, :, :], xt[p][:, :, :]).then_inc(s_xc[p], 16)

            def store_x1(g, p, q):
                if isinstance(g, int) and g == NG - 1:
                    sp.wait_ge(s_x1v, 1)
                else:
                    sp.wait_ge(s_x1, g + 1)
                sp.dma_start(out[bass.ds(g * G * P, G * P), :].rearrange("(b p) d -> p b d", p=P),
                             x1[p][:, :, :]).then_inc(s_x1o[p], 16)

            def store_w(g, p, q):
                sp.wait_ge(s_wl1, g + 1)
                if isinstance(g, int) and g == NG - 1:
                    sp.wait_ge(s_wl2v, 1)
                else:
                    apart(sp, s_apart["sp"])
                    sp.wait_ge(s_wl2, 2 * (g + 1))
                sp.dma_start(wsplit[bass.ds(g, 1)].rearrange("o p n -> (o p) n"), wcv[p][:, :]).then_inc(s_wo[p], 16)

            def step(k, n, t, m, l):
                if t:
                    copy_x(*t)
                if k:
                    load_c(*k)
                    load_x(*k)
                if t:
                    load_w(*t)
                if l:
                    store_w(*l)
                if m:
                    store_x1(*m)
                if k and isinstance(k[0], int) and k[0] == 1:
                    sp.dma_start(cbf[:, :], cb.bitcast(BF16)).then_inc(s_cbf, 16)

            groups(sp, step)

            def load_rows(i, k, it):
                after(sp, s_xtp, i - RING + 1)
                after(sp, s_cw, i - RING + 1)
                r = sp.value_load(tab[0:1, 1, bass.ds(i, 1)], min_val=0, max_val=SPARE)
                sp.dma_start(xrow[k][:, :], rows[bass.ds(r, P), :]).then_inc(s_xr[k], 16)

            def load_weights(i, k, it):
                e = sp.value_load(tab[0:1, 0, bass.ds(i, 1)], min_val=0, max_val=NE - 1)
                need = sp.value_load(tab[0:1, 2, bass.ds(i, 1)], min_val=0, max_val=1)
                w_e = wsplit[bass.ds(e, 1)].rearrange("o p n -> (o p) n")
                for half, s_free, s_loaded in ((0, s_h, s_wr1), (1, s_m2, s_wr2)):
                    after(sp, s_free, 2 * (i - RING + 1))
                    for part in range(PIECES):
                        n = 2 * W1 // PIECES
                        at = slice((half * PIECES + part) * n, (half * PIECES + part + 1) * n)
                        sp.dma_start(wring[:, k, at], w_e[:, at], cond=need).then_inc(s_loaded[k], 16)

            def tile(i, k, it):
                load_rows(i, k, it)
                if not (isinstance(i, int) and i == 0):
                    load_weights(i, k, it)

            sp.wait_ge(s_tab, 1)
            for p in range(2):
                sp.wait_ge(s_wo[p], 16 * NG // 2)
            load_weights(0, 0, 0)
            for p in range(2):
                sp.wait_ge(s_sc[p], 16 * (2 * G * NG // 2 + 1))
            sp.wait_ge(s_pad, 16 * NE)
            tiles(sp, tile)
            sp.wait_ge(s_sa, 16 * TILES)

        @block.tensor
        def _(pe):
            pe.wait_ge(s_cst, N_CST)
            for c in range(CK):
                mm = pe.transpose(SF[:, c * NE:(c + 1) * NE], rw[:, c * P:(c + 1) * P], ident[0:NE, 0:NE])
            mm.then_inc(s_rwt, 1)
            pe.wait_ge(s_rwc, 1)
            pe.wait_ge(s_prep, N_PREP)

            def turn(g, p, q, b):
                pe.wait_ge(s_xn, G * g + b + 1)
                after(pe, s_qk, G * g + b - 1)
                if b < 2:
                    after(pe, s_rTc, 2 * (g - 3) + b + 1)
                if b == 0:
                    pe.wait_ge(s_c[p], 16 * (q + 1))
                for j in range(CK):
                    pe.transpose(TB[b % 2][:, j * P:(j + 1) * P], xn[:, b, j * P:(j + 1) * P], ident)
                for j in range(CK):
                    mm = pe.transpose(TB[b % 2][:, (CK + j) * P:(CK + j + 1) * P],
                                      ctn[p][:, b, j * P:(j + 1) * P], ident)
                mm.then_inc(s_tq, 1)

            def gates(g, p, q, b):
                pe.wait_ge(s_qk, G * g + b + 1)
                if b == 0:
                    after(pe, s_gi, g)
                    after(pe, s_gmn, g)
                for j in range(2 * CK):
                    mm = pe.matmul(SF[0:FG + R, 0:P], gate_wb[:, j, b, :], qkT[p][:, b, j, :],
                                   start=(b == 0 and j == 0), stop=(b == G - 1 and j == 2 * CK - 1))
                mm.then_inc(s_gt, 1)

            def neg_logd_turn(g, p, q):
                pe.wait_ge(s_gnm, g + 1)
                after(pe, s_qk, G * (min(g + 2, NG) if isinstance(g, int) else g + 2))
                apart(pe, s_apart["pe"])
                pe.transpose(T0[:, 0:R], gnm[:, :], ident[0:R, 0:R]).then_inc(s_nT, 1)

            def logd(g, p, q, h):
                after(pe, s_dt, 2 * (2 * g + h))
                if h == 0:
                    after(pe, s_lgc, g - 1)
                    pe.wait_ge(s_mb, g + 1)
                    pe.wait_ge(s_pt, PARTS * (g + 1))
                for par in range(2):
                    for b2 in range(2):
                        b = 2 * h + b2
                        o = DB[par][:, b2 * 2 * P:(b2 + 1) * 2 * P]
                        hs = B_HSEL + (b * 2 + par) * 2 * P
                        pe.matmul(o, cbf[0:KP, B_SEL + b * P:B_SEL + (b + 1) * P],
                                  mblk[p][:, 2 * par:2 * par + 2, :], start=True, stop=False)
                        pe.matmul(o, parts[p][:, 0, :], cbf[0:KP, hs:hs + 2 * P], start=False, stop=False)
                        mm = pe.matmul(o, cbf[:, B_IDENT:B_IDENT + P], cbf[:, B_MASK:B_MASK + 2 * P],
                                       start=False, stop=True)
                    mm.then_inc(s_d, 1)

            def scores(g, p, q, h):
                after(pe, s_ct, 2 * (2 * g + h))
                if h == 0:
                    after(pe, s_u, G * g - 1)
                    after(pe, s_sq, G * g - 1)
                for b2 in range(2):
                    b = 2 * h + b2
                    for hp in range(2):
                        for par in range(2):
                            rows_ = slice(DH * par, DH * par + DH)
                            o = KB[par][:, (2 * b2 + hp) * P:(2 * b2 + hp + 1) * P]
                            mm = pe.matmul(o, qkT[p][rows_, b, CK + hp, :], qkT[p][rows_, b, hp, :],
                                           start=True, stop=True)
                mm.then_inc(s_kq, 1)

            def values(g, p, q, b):
                pe.wait_ge(s_ct, 2 * (2 * g + (b + 1) // 2 + 1) if b < 3 else 4 * (g + 1))
                if b == 0:
                    pe.wait_ge(s_vc, g + 1)
                if b in (0, 3):
                    after(pe, s_u, G * g + (1 if b else 0))
                    after(pe, s_sq, G * g + (1 if b else 0))
                for h4 in range(NH):
                    c0 = (2 * (b % 2) + h4 // 2) * P
                    mm = pe.matmul(VB[b][:, h4 * (DH + 1):(h4 + 1) * (DH + 1)],
                                   ct[b // 2][:, h4 % 2, c0:c0 + P], vt[p][:, b, h4, :],
                                   start=True, stop=True)
                mm.then_inc(s_pv, 1)

            def router_turn(g, p, q, h):
                pe.wait_ge(s_xn2, G * g + 2 * h + 2)
                after(pe, s_qk, G * (min(g + 3, NG) if isinstance(g, int) else g + 3))
                if h == 0:
                    after(pe, s_en, min(g + 2, NG) if isinstance(g, int) else g + 2)
                else:
                    after(pe, s_sl, 3 * g - 2)
                for b2 in range(2):
                    for j in range(CK):
                        mm = pe.transpose(TB[h][:, (2 * b2 + j) * P:(2 * b2 + j + 1) * P],
                                          xn2[:, 2 * h + b2, j * P:(j + 1) * P], ident)
                mm.then_inc(s_rt, 1)

            def logits(g, p, q):
                after(pe, s_dt, 4 * (min(g + 2, NG) if isinstance(g, int) else g + 2) - 1)
                for b in range(G):
                    pe.wait_ge(s_rTc, 2 * g + b // 2 + 1)
                    for j in range(CK):
                        mm = pe.matmul(LG[:, b * NE:(b + 1) * NE], rT[:, b, j, :], rwT[:, j, :],
                                       start=(j == 0), stop=(j == CK - 1))
                mm.then_inc(s_lg, 1)

            def ranks(g, p, q):
                pe.wait_ge(s_msk, g + 1)
                after(pe, s_qk, G * (min(g + 4, NG) if isinstance(g, int) else g + 4))
                after(pe, s_cu, 2 * g)
                pe.matmul(RK, tri_h[:, :], msk[:, :, :], start=True, stop=False, skip_group_check=True)
                for n in range(1, G):
                    pe.matmul(RK[:, n * NE:], ones_h[:, :], msk[:, 0:G - n, :], start=False,
                              stop=False, skip_group_check=True)
                for b in range(G):
                    mm = pe.matmul(RK[:, b * NE:(b + 1) * NE], ones_h[:, :], cum[:, :], start=False,
                                   stop=(b == G - 1), skip_group_check=True)
                mm.then_inc(s_rank, 1)

            def step(k, n, t, m, l):
                if n:
                    turn(*n, 0)
                    turn(*n, 1)
                    gates(*n, 0)
                    turn(*n, 2)
                    gates(*n, 1)
                    turn(*n, 3)
                if t and isinstance(t[0], int) and t[0] == 0:
                    pe.wait_ge(s_cbf, 16)
                    pe.wait_ge(s_prep, N_PREP + 1)
                    pe.wait_ge(s_prepg, 3)
                if t:
                    neg_logd_turn(*t)
                if t:
                    for h in range(2):
                        logd(*t, h)
                        scores(*t, h)
                if l:
                    ranks(*l)
                if t:
                    values(*t, 0)
                if t and not n:
                    for b in range(1, G):
                        values(*t, b)
                if n:
                    gates(*n, 2)
                if t and n:
                    values(*t, 1)
                if m:
                    router_turn(*m, 0)
                    router_turn(*m, 1)
                if n:
                    gates(*n, 3)
                if t and n:
                    values(*t, 2)
                if m:
                    logits(*m)
                if t and n:
                    values(*t, 3)

            groups(pe, step)

            pe.wait_ge(s_cu, 2 * NG)
            pe.matmul(T0[:, 0:NE], ones_h[:, :], cum[:, :], start=True, stop=True).then_inc(s_cnt, 1)

            XP, YP, HPS = SF, [KE, KO, UB], [DE, DO]
            xp = XP[:, 0:CK * P].bitcast(F16)

            def turn(i, k, it):
                pe.wait_ge(s_xr[k], 16 * (it + 1))
                after(pe, s_xtc, i)
                xr = xrow[k][:, :].bitcast(F16)
                for j in range(2 * CK):
                    mm = pe.transpose(xp[:, j * P:(j + 1) * P], xr[:, j * P:(j + 1) * P], ident_h[:, :])
                mm.then_inc(s_xtp, 1)

            def hidden(i, k, it, a):
                if a == 0:
                    pe.wait_ge(s_wr1[k], 16 * PIECES * (it + 1))
                    pe.wait_ge(s_xtc, i + 1)
                after(pe, s_gf, 2 * i + a - 1)
                after(pe, s_gh, 2 * i + a - 1)
                for m4 in range(4):
                    m = 4 * a + m4
                    o = HPS[a][:, m4 * P:(m4 + 1) * P]
                    for c in range(CK):
                        hi = wring[:, k, c * HID + m * P:c * HID + (m + 1) * P]
                        lo = wring[:, k, W1 + c * HID + m * P:W1 + c * HID + (m + 1) * P]
                        pe.matmul(o, hi, xT[k][:, c, :], start=(c == 0), stop=False)
                        pe.matmul(o, hi, xT[k][:, CK + c, :], start=False, stop=False)
                        mm = pe.matmul(o, lo, xT[k][:, c, :], start=False, stop=(c == CK - 1))
                mm.then_inc(s_h, 1)

            def output(i, k, it, a):
                if a == 0:
                    pe.wait_ge(s_wr2[k], 16 * PIECES * (it + 1))
                pe.wait_ge(s_gh, 2 * i + a + 1)
                pe.wait_ge(s_glo, 2 * i + a + 1)
                if a == 0:
                    after(pe, s_yo, i - RING + 1)
                for m4 in range(4):
                    w = 2 * W1 + (4 * a + m4) * 2 * D
                    pe.matmul(YP[k][:, 0:2 * D], gh[a][:, m4, :], wring[:, k, w:w + 2 * D],
                              start=(a == 0 and m4 == 0), stop=False, skip_group_check=True)
                    mm = pe.matmul(YP[k][:, D:2 * D], gl[a][:, m4, :], wring[:, k, w:w + D],
                                   start=False, stop=(a == 1 and m4 == 3), skip_group_check=True)
                mm.then_inc(s_m2, 1)

            def tile(i, k, it):
                hidden(i, k, it, 0)
                if not (isinstance(i, int) and i == 0):
                    output(i - 1, (k - 1) % RING, it, 1)
                hidden(i, k, it, 1)
                if not (isinstance(i, int) and i == TILES - 1):
                    turn(i + 1, (k + 1) % RING, it + (k + 1) // RING)
                output(i, k, it, 0)

            pe.wait_ge(s_slot, 2 * NG)
            turn(0, 0, 0)
            tiles(pe, tile)
            output(TILES - 1, RING - 1, 0, 1)

        @block.scalar
        def _(act):
            def turned(g, p, q, b):
                act.wait_ge(s_tq, G * g + b + 1)
                if b == 0:
                    after(act, s_kq, 2 * (g - 1))
                act.activation(qkT[p][:, b, :, :], TB[b % 2][:, :].rearrange("p (j n) -> p j n", j=2 * CK),
                               ACT.Copy).then_inc(s_qk, 1)

            def log_sigmoid(g, p, q):
                act.wait_ge(s_gt, G * (g + 1))
                after(act, s_gcs, g)
                if isinstance(g, int) and g == 0:
                    act.wait_ge(s_gb, 16 * 2 * G)
                act.activation(ga[:, :], SF[FG:FG + R, 0:P], ACT.Abs, bias=gate_b[FG:FG + R, :]).then_inc(s_ga, 1)
                act.wait_ge(s_ga, g + 1)
                act.activation(ge[:, :], ga[:, :], ACT.Exp, scale=-1.0).then_inc(s_ge, 1)
                act.wait_ge(s_ge, g + 1)
                act.activation(gl_[:, :], ge[:, :], ACT.Ln, bias=1.0).then_inc(s_gl, 1)

            def exp_neg_logd(g, p, q):
                act.wait_ge(s_nT, g + 1)
                after(act, s_n, 5 * (g - 1))
                act.activation(en[p][:, :], T0[:, 0:R], ACT.Exp).then_inc(s_en, 1)

            def decay(g, p, q, h):
                for par in range(2):
                    act.wait_ge(s_d, 2 * (2 * g + h) + par + 1)
                    after(act, s_ct, 2 * (2 * g + h - 2) + par + 1)
                    act.activation(dt_[h][:, par, :], DB[par][:, :], ACT.Exp).then_inc(s_dt, 1)

            def values(g, p, q, b):
                act.wait_ge(s_pv, G * g + b + 1)
                if b == 0:
                    after(act, s_tt, g)
                    after(act, s_n, 5 * g)
                    after(act, s_ss, g)
                hd = VB[b][:, 0:NH * (DH + 1)].rearrange("p (h d) -> p h d", h=NH)
                act.activation(u[:, NH * b:NH * (b + 1), :], hd, ACT.Copy).then_inc(s_u, 1)
                act.activation(sq[:, NH * b:NH * (b + 1), :], hd[:, :, 0:DH], ACT.Square).then_inc(s_sq, 1)

            def split_w1(g, p, q):
                after(act, s_wo[p], 16 * q)
                act.activation(wcv[p][:, 0:W1], wst[p][:, 0:W1], ACT.Copy, scale=WSCALE).then_inc(s_wh1, 1)

            def scale_w2(g, p, q):
                act.wait_ge(s_wst[p], 32 * (q + 1))
                act.activation(wst[p][:, W1:W1 + W2], wst[p][:, W1:W1 + W2], ACT.Copy, scale=WSCALE).then_inc(s_w16, 1)

            def split_w2(g, p, q):
                act.wait_ge(s_w16, g + 1)
                act.activation(wcv[p][:, 2 * W1:].rearrange("p (m k n) -> p m k n", m=MK, k=2)[:, :, 0, :],
                               wst[p][:, W1:W1 + W2].rearrange("p (m n) -> p m n", m=MK), ACT.Copy
                               ).then_inc(s_wh2, 1)

            def row_high(g, p, q):
                act.wait_ge(s_xn2, G * (g + 1))
                act.wait_ge(s_sc[p], 16 * (2 * G * q + 1))
                act.activation(rowb[p][:, :, 0:D // 2].bitcast(F16), xn2[:, :, :], ACT.Copy).then_inc(s_hi, 1)

            def router_turned(g, p, q, h):
                act.wait_ge(s_rt, 2 * g + h + 1)
                if h == 0:
                    after(act, s_lg, g)
                act.activation(rT[:, 2 * h:2 * h + 2, :, :],
                               TB[h][:, :].rearrange("p (b j n) -> p b j n", b=2, j=CK),
                               ACT.Copy).then_inc(s_rTc, 1)

            def router_exp(g, p, q):
                act.wait_ge(s_rk, 10 * g + 7)
                after(act, s_meta, g)
                act.activation(e21[:, :], d21[:, :], ACT.Exp).then_inc(s_e21, 1)

            def step(k, n, t, m, l):
                if n:
                    turned(*n, 0)
                    turned(*n, 1)
                    turned(*n, 2)
                    turned(*n, 3)
                if t:
                    exp_neg_logd(*t)
                if l:
                    router_exp(*l)
                if t:
                    decay(*t, 0)
                    scale_w2(*t)
                    decay(*t, 1)
                    split_w1(*t)
                    split_w2(*t)
                    values(*t, 0)
                if t and n:
                    values(*t, 1)
                if m:
                    row_high(*m)
                if t and not n:
                    for b in range(1, G):
                        values(*t, b)
                if m:
                    router_turned(*m, 0)
                    router_turned(*m, 1)
                if t and n:
                    values(*t, 2)
                if n:
                    log_sigmoid(*n)
                if t and n:
                    values(*t, 3)

            for b in range(G):
                act.dma_start(gate_b[NH * b:NH * b + NH, :], ig_b.rearrange("(h o) -> h o", o=1)).then_inc(s_gb, 16)
                act.dma_start(gate_b[FG + NH * b:FG + NH * b + NH, :], fg_b.rearrange("(h o) -> h o", o=1)
                              ).then_inc(s_gb, 16)
            groups(act, step)

            act.wait_ge(s_pr, 1)
            act.wait_ge(s_cst, N_CST)
            for e in range(NE):
                r = act.value_load(padr[0:1, e:e + 1], min_val=e * REGION, max_val=e * REGION + NT)
                act.dma_start(rows[bass.ds(r, P), :], pad[:, :]).then_inc(s_pad, 16)
            act.wait_ge(s_prepg, 3)
            act.wait_ge(s_n, 5 * NG)
            act.activation(en[0][:, 0:1], mhalf[:, 0:1], ACT.Gelu)

            HPS, YP = [DE, DO], [KE, KO, UB]

            def gelu(i, a):
                act.wait_ge(s_h, 2 * i + a + 1)
                after(act, s_glo, 2 * i + a - 1)
                act.activation(gf[a], HPS[a][:, :], ACT.Gelu, scale=1.0 / WSCALE).then_inc(s_gf, 1)
                after(act, s_m2, 2 * i + a - 1)
                act.activation(gh[a][:, :, :], HPS[a][:, :].rearrange("p (m n) -> p m n", m=4), ACT.Gelu,
                               scale=1.0 / WSCALE).then_inc(s_gh, 1)

            def cross(i, k):
                act.wait_ge(s_m2, 2 * i + 2)
                act.wait_ge(s_cw, i + 1)
                after(act, s_yo, i)
                act.activation(yc, YP[k][:, D:2 * D], ACT.Copy, scale=cw[k][:, :]).then_inc(s_yc, 1)

            def tile(i, k, it):
                gelu(i, 0)
                if not (isinstance(i, int) and i == 0):
                    cross(i - 1, (k - 1) % RING)
                gelu(i, 1)

            act.wait_ge(s_ct, 4 * NG)
            tiles(act, tile)
            cross(TILES - 1, RING - 1)

        @block.vector
        def _(dve):
            def x_stats(g, p, q):
                dve.wait_ge(s_x[p], 16 * (q + 1))
                for b in range(G):
                    after(dve, s_mv1, G * (g - 1) + b + 1)
                    dve.bn_stats(st1[:, b, :], xt[p][:, b, :]).then_inc(s_bn1, 1)
                after(dve, s_xn, G * g)
                after(dve, s_ve1, g)
                for b in range(G):
                    dve.wait_ge(s_bn1, G * g + b + 1)
                    apart(dve, s_apart["dve"])
                    dve.bn_aggr(mv1[:, b, :], st1[:, b, :]).then_inc(s_mv1, 1)

            x_stats(0, 0, 0)
            for p in range(2):
                dve.memset(parts[p][:, :, :], 0.0).then_inc(s_prep, 1)
            dve.memset(cum[:, :], 0.0).then_inc(s_prep, 1)
            dve.memset(gate_wb[:, :, :, :], 0.0).then_inc(s_prep, 1)
            dve.wait_ge(s_cst, N_CST)
            dve.tensor_tensor(gate_w[:, CK:2 * CK, :, :], gate_w[:, CK:2 * CK, :, :],
                              gate_w[:, 2 * CK:3 * CK, :, :], ALU.add).then_inc(s_prep, 1)
            dve.wait_ge(s_prep, N_PREP - 1)
            for b in range(G):
                for i in range(2):
                    cp = dve.tensor_copy(gate_wb[:, :, b, FG * i + NH * b:FG * i + NH * (b + 1)],
                                         gate_w[:, 0:2 * CK, i, :])
            cp.then_inc(s_prep, 1)
            dve.wait_ge(s_rwt, 1)
            dve.tensor_copy(rwT[:, :, :], SF[:, 0:CK * NE].rearrange("p (c e) -> p c e", c=CK)).then_inc(s_rwc, 1)
            dve.wait_ge(s_prep, N_PREP)

            w8 = cst[:, C_W8:C_W8 + NE].unsqueeze(1).to_broadcast([P, G, NE])

            def spread(t):
                return t[:, :].unsqueeze(2).to_broadcast([P, G, NE])

            def x_norm(g, p, q):
                dve.wait_ge(s_rs1, g + 1)
                after(dve, s_tq, G * g)
                for b in range(G):
                    dve.tensor_scalar(xn[:, b, :], xt[p][:, b, :], mv1[:, b, 0:1], rs1[:, b:b + 1],
                                      ALU.subtract, ALU.mult).then_inc(s_xn, 1)

            def ctx_means(g, p, q):
                dve.wait_ge(s_c[p], 16 * (q + 1))
                after(dve, s_vm, g)
                dve.reduce_sum(vsum[:, :], ctn[p][:, :, :].rearrange("p b (h d) -> p (b h) d", h=NH), AX.X
                               ).then_inc(s_vs, 1)
                dve.wait_ge(s_vs, g + 1)
                after(dve, s_vc, g)
                dve.tensor_scalar(vmean[:, :], vsum[:, :], 1.0 / DH, None, ALU.mult).then_inc(s_vm, 1)

            def scores(g, p, q, h):
                dve.wait_ge(s_kq, 2 * g + h + 1)
                after(dve, s_pv, G * (g - 1) + 2 * h + 2)
                for par in range(2):
                    dve.wait_ge(s_dt, 2 * (2 * g + h) + par + 1)
                    dve.scalar_tensor_tensor(ct[h][:, par, :], KB[par][:, :], DH ** -0.5, dt_[h][:, par, :],
                                             ALU.mult, ALU.mult).then_inc(s_ct, 1)

            def x1_stats(g, p, q):
                if isinstance(g, int) and g == NG - 1:
                    dve.wait_ge(s_x1v, 1)
                else:
                    dve.wait_ge(s_x1, g + 1)
                for b in range(G):
                    after(dve, s_mv2, G * (g - 1) + b + 1)
                    dve.bn_stats(st2[:, b, :], x1[p][:, b, :]).then_inc(s_bn2, 1)
                after(dve, s_xn2, G * g)
                after(dve, s_ve2, g)
                for b in range(G):
                    dve.wait_ge(s_bn2, G * g + b + 1)
                    apart(dve, s_apart["dve"])
                    dve.bn_aggr(mv2[:, b, :], st2[:, b, :]).then_inc(s_mv2, 1)

            def x1_norm(g, p, q):
                dve.wait_ge(s_rs2, g + 1)
                for b in range(G):
                    dve.tensor_scalar(xn2[:, b, :], x1[p][:, b, :], mv2[:, b, 0:1], rs2[:, b:b + 1],
                                      ALU.subtract, ALU.mult).then_inc(s_xn2, 1)

            def split_w1(g, p, q):
                dve.wait_ge(s_wh1, g + 1)
                dve.scalar_tensor_tensor(wcv[p][:, W1:2 * W1], wst[p][:, 0:W1], WSCALE, wcv[p][:, 0:W1],
                                         ALU.mult, ALU.subtract).then_inc(s_wl1, 1)

            def parts_and_top_two(n, m):
                if n:
                    gn, pn, _ = n
                    after(dve, s_d, 4 * (gn - 1))
                    dve.tensor_copy(parts[pn][0:R, :, :], gm[:, :, :]).then_inc(s_pt, 1)
                if m:
                    g = m[0]
                    dve.wait_ge(s_lg, g + 1)
                    after(dve, s_rk, 10 * g)
                    dve.tensor_copy(lg[:, :, :], LG.rearrange("p (b e) -> p b e", b=G)).then_inc(s_lgc, 1)
                if n:
                    dve.wait_ge(s_pt, PARTS * gn + 1)
                    dve.tensor_tensor(gr[:, :, :], gm[:, :, :], parts[pn][0:R, :, :], ALU.subtract).then_inc(s_gr, 1)
                if m:
                    dve.wait_ge(s_lgc, g + 1)
                    dve.reduce_max(m1[:, :], lg[:, :, :], AX.X).then_inc(s_rk, 1)
                if n:
                    dve.wait_ge(s_gr, 3 * gn + 1)
                    dve.tensor_copy(parts[pn][32:32 + R, :, :], gr[:, :, :]).then_inc(s_pt, 1)
                if m:
                    dve.wait_ge(s_rk, 10 * g + 1)
                    dve.tensor_tensor(eq[:, :, :], lg[:, :, :], spread(m1), ALU.is_equal).then_inc(s_rk, 1)
                if n:
                    dve.tensor_copy(grb[:, :, :], gr[:, :, :]).then_inc(s_gr, 1)
                if m:
                    dve.wait_ge(s_rk, 10 * g + 2)
                    dve.tensor_tensor(key[:, :, :], eq[:, :, :], w8, ALU.mult).then_inc(s_rk, 1)
                if n:
                    dve.wait_ge(s_gr, 3 * gn + 2)
                    dve.tensor_tensor(gr2[:, :, :], gr[:, :, :], grb[:, :, :], ALU.subtract).then_inc(s_gr, 1)
                if m:
                    dve.wait_ge(s_rk, 10 * g + 3)
                    dve.reduce_max(km1[:, :], key[:, :, :], AX.X).then_inc(s_km, 1)
                if n:
                    dve.wait_ge(s_gr, 3 * gn + 3)
                    dve.tensor_copy(parts[pn][64:64 + R, :, :], gr2[:, :, :]).then_inc(s_pt, 1)
                if m:
                    dve.wait_ge(s_km, 4 * g + 1)
                    dve.tensor_tensor(oh1[:, :, :], w8, spread(km1), ALU.is_equal).then_inc(s_km, 1)
                if m:
                    dve.wait_ge(s_km, 4 * g + 2)
                    dve.scalar_tensor_tensor(lg2[:, :, :], oh1[:, :, :], -3e38, lg[:, :, :], ALU.mult, ALU.add
                                             ).then_inc(s_rk, 1)
                if m:
                    dve.wait_ge(s_rk, 10 * g + 4)
                    dve.reduce_max(m2[:, :], lg2[:, :, :], AX.X).then_inc(s_rk, 1)
                if n:
                    if isinstance(gn, int) and gn == 0:
                        dve.wait_ge(s_cbf, 16)
                    dve.wait_ge(s_pt, PARTS * (gn + 1))
                    dve.tensor_tensor(mblk[pn][:, :, :], parts[pn][:, 1:2, :].to_broadcast([KP, NH, P]),
                                      cbf[0:KP, B_HMASK:B_HMASK + NH].unsqueeze(2).to_broadcast([KP, NH, P]),
                                      ALU.mult).then_inc(s_mb, 1)
                if m:
                    dve.wait_ge(s_rk, 10 * g + 5)
                    dve.tensor_tensor(eq[:, :, :], lg2[:, :, :], spread(m2), ALU.is_equal).then_inc(s_rk, 1)
                    after(dve, s_e21, g)
                    dve.tensor_tensor(d21[:, :], m2[:, :], m1[:, :], ALU.subtract).then_inc(s_rk, 1)

            def masks(g, p, q):
                dve.wait_ge(s_km, 4 * g + 4)
                dve.tensor_tensor(key[:, :, :], oh1[:, :, :], oh2[:, :, :], ALU.add).then_inc(s_rk, 1)
                dve.wait_ge(s_rk, 10 * g + 9)
                dve.tensor_copy(msk[:, :, :], key[:, :, :]).then_inc(s_msk, 1)
                dve.reduce_sum(csum[:, :], key[:, :, :].rearrange("p b e -> p e b"), AX.X).then_inc(s_rk, 1)

            def gates_biased(g, p, q):
                dve.wait_ge(s_ga, g + 1)
                if isinstance(g, int) and g == 0:
                    dve.wait_ge(s_gb, 16 * 2 * G)
                dve.tensor_scalar(gmn[:, :], SF[FG:FG + R, 0:P], gate_b[FG:FG + R, :], 0.0, ALU.add, ALU.min
                                  ).then_inc(s_gmn, 1)
                dve.tensor_scalar(gi[:, :], SF[0:R, 0:P], gate_b[0:R, :], -1.0, ALU.add, ALU.mult
                                  ).then_inc(s_gi, 1)

            def slots(g, p, q):
                dve.wait_ge(s_rank, g + 1)
                dve.wait_ge(s_rk, 10 * g + 10)
                dve.tensor_tensor(rb[:, :, :], RK.rearrange("p (b e) -> p b e", b=G),
                                  cst[:, C_EBASE:C_EBASE + NE].unsqueeze(1).to_broadcast([P, G, NE]),
                                  ALU.add).then_inc(s_sl, 1)
                dve.tensor_tensor(cum[:, :], cum[:, :], csum[:, :], ALU.add).then_inc(s_cu, 2)
                dve.wait_ge(s_e21, g + 1)
                dve.tensor_scalar(den[:, :], e21[:, :], 1.0, None, ALU.add).then_inc(s_mt, 1)
                dve.wait_ge(s_sl, 3 * g + 1)
                dve.tensor_tensor(a1[:, :, :], oh1[:, :, :], rb[:, :, :], ALU.mult).then_inc(s_sl, 1)
                dve.tensor_tensor(a2[:, :, :], oh2[:, :, :], rb[:, :, :], ALU.mult).then_inc(s_sl, 1)
                dve.wait_ge(s_mt, 5 * g + 1)
                dve.reciprocal(c1[:, :], den[:, :]).then_inc(s_mt, 1)
                dve.wait_ge(s_sc[p], 16 * (2 * G * q + 1))
                dve.wait_ge(s_sl, 3 * g + 3)
                for k, a in enumerate((a1, a2)):
                    dve.reduce_sum(sf[:, k, :], a[:, :, :], AX.X).then_inc(s_sf, 1)
                dve.wait_ge(s_mt, 5 * g + 2)
                dve.tensor_tensor(c2[:, :], e21[:, :], c1[:, :], ALU.mult).then_inc(s_mt, 1)
                dve.wait_ge(s_sf, 2 * g + 2)
                dve.tensor_copy(slot[p][:, :, :], sf[:, :, :]).then_inc(s_slot, 2)
                dve.wait_ge(s_mt, 5 * g + 3)
                dve.tensor_tensor(den[:, :], c1[:, :], c2[:, :], ALU.subtract).then_inc(s_mt, 1)
                dve.tensor_scalar(rowb[p][:, :, D + 2], c2[:, :], 1.0 / WSCALE, None, ALU.mult)
                dve.tensor_scalar(rowb[p][:, :, D + 3], km1[:, :], -1.0, float(NE), ALU.mult, ALU.add)
                dve.tensor_copy(rowb[p][:, :, D].bitcast(I32), tok[:, :]).then_inc(s_mt, 1)
                dve.wait_ge(s_mt, 5 * g + 5)
                dve.tensor_scalar(tok[:, :], tok[:, :], float(G * P), None, ALU.add)
                dve.tensor_scalar(rowb[p][:, :, D + 1], den[:, :], 1.0 / WSCALE, None, ALU.mult
                                  ).then_inc(s_meta, 1)

            def scans_and_head_var(n, t):
                if t:
                    gt, pt, _ = t
                    dve.wait_ge(s_u, G * (gt + 1))
                    after(dve, s_n, 5 * gt)
                    dve.scalar_tensor_tensor(n0[:, :], u[:, :, DH], -1.0, u[:, :, DH], ALU.mult, ALU.max
                                             ).then_inc(s_n, 1)
                if n:
                    g = n[0]
                    dve.wait_ge(s_gl, g + 1)
                    dve.wait_ge(s_gmn, g + 1)
                    dve.tensor_tensor_scan(gcs[:, :], gmn[:, :], gl_[:, :], 0.0, ALU.add, ALU.subtract).then_inc(s_gcs, 1)
                if t:
                    dve.wait_ge(s_en, gt + 1)
                    dve.wait_ge(s_n, 5 * gt + 1)
                    dve.tensor_tensor(n2[:, :], n0[:, :], en[pt][:, :], ALU.max).then_inc(s_n, 1)
                if n:
                    dve.wait_ge(s_gcs, g + 1)
                    dve.wait_ge(s_gi, g + 1)
                    dve.tensor_tensor(gm[:, 0, :], gi[:, :], gcs[:, :], ALU.add).then_inc(s_ng, 1)
                if t:
                    dve.wait_ge(s_n, 5 * gt + 2)
                    dve.tensor_scalar(n1[:, :], n2[:, :], 1e-6, None, ALU.add).then_inc(s_n, 1)
                if n:
                    dve.wait_ge(s_ng, g + 1)
                    dve.tensor_tensor_scan(gm[:, 1, :], gm[:, 0, :], gm[:, 0, :], 3e38, ALU.min, ALU.min).then_inc(s_gmx, 1)
                if t:
                    dve.wait_ge(s_sq, G * (gt + 1))
                    dve.reduce_sum(ss[:, :], sq, AX.X).then_inc(s_ss, 1)
                    dve.wait_ge(s_n, 5 * gt + 3)
                    dve.scalar_tensor_tensor(n2[:, :], n1[:, :], EPS, n1[:, :], ALU.mult, ALU.mult
                                             ).then_inc(s_n, 1)
                if n:
                    dve.wait_ge(s_gmx, g + 1)
                    after(dve, s_nT, g)
                    dve.tensor_tensor(gnm[:, :], gm[:, 1, :], gcs[:, :], ALU.subtract).then_inc(s_gnm, 1)
                if t:
                    dve.wait_ge(s_ss, gt + 1)
                    dve.wait_ge(s_n, 5 * gt + 4)
                    after(dve, s_hrs, gt)
                    dve.scalar_tensor_tensor(hv[:, :], ss[:, :], 1.0 / DH, n2[:, :], ALU.mult, ALU.add
                                             ).then_inc(s_n, 1)

            def row_low(g, p, q):
                dve.wait_ge(s_hi, g + 1)
                dve.tensor_tensor(rowb[p][:, :, D // 2:D].bitcast(F16), xn2[:, :, :],
                                   rowb[p][:, :, 0:D // 2].bitcast(F16), ALU.subtract).then_inc(s_lo, 1)

            def head_norm_and_second(m, l):
                if l:
                    gl, _, _ = l
                    dve.wait_ge(s_rk, 10 * gl + 6)
                    dve.tensor_tensor(key[:, :, :], eq[:, :, :], w8, ALU.mult).then_inc(s_rk, 1)
                if m:
                    g = m[0]
                    dve.wait_ge(s_hrs, g + 1)
                    after(dve, s_rt, 2 * g)
                    after(dve, s_hi, g)
                    after(dve, s_lo, g)
                    dve.tensor_tensor(hn, u[:, :, 0:DH], hrs[:, :].unsqueeze(2).to_broadcast([P, R, DH]),
                                      ALU.mult).then_inc(s_tt, 1)
                if l:
                    dve.wait_ge(s_rk, 10 * gl + 8)
                    dve.reduce_max(km2[:, :], key[:, :, :], AX.X).then_inc(s_km, 1)
                if m:
                    dve.wait_ge(s_tt, g + 1)
                    dve.tensor_tensor(xn2[:, :, :], xn2[:, :, :], gam[:, :].unsqueeze(1).to_broadcast([P, G, D]),
                                      ALU.mult).then_inc(s_tg, 1)
                if l:
                    dve.wait_ge(s_km, 4 * gl + 3)
                    dve.tensor_tensor(oh2[:, :, :], w8, spread(km2), ALU.is_equal).then_inc(s_km, 1)

            def split_w2(g, p, q):
                dve.wait_ge(s_wh2, g + 1)
                v = wcv[p][:, 2 * W1:].rearrange("p (m k n) -> p m k n", m=MK, k=2)
                dve.tensor_tensor(v[:, :, 1, :], wst[p][:, W1:W1 + W2].rearrange("p (m n) -> p m n", m=MK),
                                  v[:, :, 0, :], ALU.subtract).then_inc(s_wl2v, 1)

            def residual(g, p, q):
                dve.wait_ge(s_tg, g + 1)
                dve.wait_ge(s_xc[p], 16 * (q + 1))
                dve.tensor_tensor(x1[p][:, :, :], x1[p][:, :, :], xn2[:, :, :], ALU.add).then_inc(s_x1v, 1)

            def step(k, n, t, m, l):
                head_norm_and_second(m, l if t or not m else None)
                if n:
                    ctx_means(*n)
                if t:
                    scores(*t, 0)
                if m and not t:
                    residual(*m)
                if m:
                    x1_stats(*m)
                if l and (t or not m):
                    masks(*l)
                if l and m and not t:
                    parts_and_top_two(None, l)
                    head_norm_and_second(None, l)
                    masks(*l)
                if t:
                    scores(*t, 1)
                if m:
                    x1_norm(*m)
                if l:
                    slots(*l)
                if k and not (isinstance(k[0], int) and k[0] == 0):
                    x_stats(*k)
                if t:
                    split_w1(*t)
                if m:
                    row_low(*m)
                if m and not t:
                    split_w2(*m)
                if k:
                    x_norm(*k)
                if n:
                    gates_biased(*n)
                scans_and_head_var(n, t)
                parts_and_top_two(n, m if n or not t else None)
                if n and isinstance(n[0], int) and n[0] == 0:
                    dve.tensor_copy(ident_h[:, :], ident)
                    dve.tensor_copy(tok[:, :], cst[:, C_TOK:C_TOK + G])
                    dve.tensor_copy(tri_h[:, :], cbf[:, B_TRI:B_TRI + P])
                    dve.tensor_copy(ones_h[:, :], cbf[:, B_ONES:B_ONES + P]).then_inc(s_prep, 1)

            groups(dve, step)

            step = [0]

            def link(ins):
                step[0] += 1
                ins.then_inc(s_tb, 1)
                dve.wait_ge(s_tb, step[0])

            i_b = cst[:, C_TILE:C_TILE + TILES]
            dve.wait_ge(s_cnt, 1)
            dve.wait_ge(s_lo, NG)
            link(dve.tensor_copy(ncnt[:, :], T0[:, 0:NE]))
            dve.tensor_tensor(padr[:, :], ncnt[:, :], cst[:, C_EBASE:C_EBASE + NE], ALU.add).then_inc(s_pr, 1)
            link(dve.tensor_tensor(te3[:, :, :], ncnt[:, :].unsqueeze(2).to_broadcast([P, NE, NB]),
                                   cst[:, C_THR:C_THR + NB].unsqueeze(1).to_broadcast([P, NE, NB]), ALU.is_gt))
            link(dve.reduce_sum(te[:, :], te3[:, :, :], AX.X))
            link(dve.tensor_tensor_scan(ctl[:, :], te[:, :], te[:, :], 0.0, ALU.add, ALU.bypass))
            link(dve.tensor_scalar(wt[:, :], te[:, :], -1.0, float(REGION // P), ALU.mult, ALU.add))
            link(dve.tensor_tensor(le[:, :, :], i_b.unsqueeze(2).to_broadcast([P, TILES, NE]),
                                   ctl[:, :].unsqueeze(1).to_broadcast([P, TILES, NE]), ALU.is_ge))
            link(dve.reduce_sum(idr[:, :], le[:, :, :], AX.X))
            link(dve.tensor_scalar(etab[:, :], idr[:, :], float(NE - 1), None, ALU.min))
            link(dve.tensor_tensor(lw[:, :, :], le[:, :, :], wt[:, :].unsqueeze(1).to_broadcast([P, TILES, NE]),
                                   ALU.mult))
            link(dve.reduce_sum(adr[:, :], lw[:, :, :], AX.X))
            link(dve.tensor_tensor(ad2[:, :], adr[:, :], i_b, ALU.add))
            link(dve.tensor_scalar(adr[:, :], ad2[:, :], float(SPARE // P), float(P), ALU.min, ALU.mult))
            link(dve.memset(chg[:, 0:RING], 1.0))
            link(dve.tensor_tensor(chg[:, RING:TILES], etab[:, RING:TILES], etab[:, 0:TILES - RING], ALU.not_equal))
            link(dve.tensor_copy(tab[:, 0, :], etab[:, :]))
            link(dve.tensor_copy(tab[:, 1, :], adr[:, :]))
            dve.tensor_copy(tab[:, 2, :], chg[:, :]).then_inc(s_tab, 1)

            YP = [KE, KO, UB]
            xp = SF[:, 0:CK * P].bitcast(F16)

            def copies(i, k, it):
                dve.wait_ge(s_xtp, i + 1)
                after(dve, s_h, 2 * (i - RING + 1))
                dve.tensor_copy(xT[k], xp.rearrange("p (j n) -> p j n", j=2 * CK)).then_inc(s_xtc, 1)
                after(dve, s_yo, i - RING + 1)
                after(dve, s_yc, i - RING + 1)
                after(dve, s_cw, i)
                dve.tensor_scalar(cw0[:, :], xrow[k][:, D + 3:D + 4], etab[:, bass.ds(i, 1)],
                                  xrow[k][:, D + 1:D + 2], ALU.is_equal, ALU.mult).then_inc(s_cw0, 1)
                dve.wait_ge(s_cw0, i + 1)
                after(dve, s_sa, 16 * (i - RING + 1))
                dve.tensor_copy(dst[k][:, :], xrow[k][:, D:D + 1].bitcast(I32))
                dve.tensor_tensor(cw[k][:, :], cw0[:, :], xrow[k][:, D + 2:D + 3], ALU.add).then_inc(s_cw, 1)

            def low(i, a):
                dve.wait_ge(s_gf, 2 * i + a + 1)
                dve.wait_ge(s_gh, 2 * i + a + 1)
                after(dve, s_m2, 2 * i + a - 1)
                dve.tensor_tensor(gl[a][:, :, :], gf[a].rearrange("p (m n) -> p m n", m=4),
                                  gh[a][:, :, :], ALU.subtract).then_inc(s_glo, 1)

            def sum_up(i, k):
                dve.wait_ge(s_yc, i + 1)
                after(dve, s_sa, 16 * (i - RING + 1))
                dve.scalar_tensor_tensor(yo[k], YP[k][:, 0:D], cw[k][:, 0:1], yc, ALU.mult, ALU.add
                                         ).then_inc(s_yo, 1)

            def tile(i, k, it):
                low(i, 0)
                if not (isinstance(i, int) and i == 0):
                    sum_up(i - 1, (k - 1) % RING)
                if not (isinstance(i, int) and i == TILES - 1):
                    copies(i + 1, (k + 1) % RING, it + (k + 1) // RING)
                low(i, 1)

            copies(0, 0, 0)
            tiles(dve, tile)
            sum_up(TILES - 1, RING - 1)

        @block.gpsimd
        def _(pool):
            for p in range(2):
                pool.memset(vt[p][:, :, :, DH:DH + 1], 1.0).then_inc(s_prepg, 1)
            pool.memset(mhalf[:, :], -0.5).then_inc(s_prepg, 1)
            def x_rstd(g, p, q):
                pool.wait_ge(s_mv1, G * (g + 1))
                after(pool, s_rs1, g)
                apart(pool, s_apart["pool"])
                pool.tensor_scalar(ve1[:, :], mv1[:, :, 1], EPS, None, ALU.add).then_inc(s_ve1, 1)
                pool.wait_ge(s_ve1, g + 1)
                after(pool, s_xn, G * g)
                pool.tensor_tensor(rs1[:, :], ve1[:, :], mhalf[:, 0:G], ALU.pow).then_inc(s_rs1, 1)

            pool.wait_ge(s_prepg, 3)
            x_rstd(0, 0, 0)
            pool.wait_ge(s_cst, N_CST)
            pool.dma_start(rows[SPARE:SPARE + P, :], pad[:, :]).then_inc(s_sc[0], 16)
            pool.dma_start(out[NT:NT + P, :], pad[:, 0:D]).then_inc(s_sc[1], 16)

            def centre(g, p, q):
                pool.wait_ge(s_vm, g + 1)
                pool.wait_ge(s_c[p], 16 * (q + 1))
                after(pool, s_pv, G * (g - 1))
                pool.tensor_tensor(vt[p][:, :, :, 0:DH].rearrange("p b h d -> p (b h) d"),
                                   ctn[p][:, :, :].rearrange("p b (h d) -> p (b h) d", h=NH),
                                   vmean[:, :].unsqueeze(2).to_broadcast([P, R, DH]),
                                   ALU.subtract).then_inc(s_vc, 1)

            def head_rstd(g, p, q):
                pool.wait_ge(s_n, 5 * g + 5)
                after(pool, s_tt, g)
                pool.tensor_tensor(hrs[:, :], hv[:, :], mhalf[:, :], ALU.pow).then_inc(s_hrs, 1)

            def residual(g, p, q):
                pool.wait_ge(s_tg, g + 1)
                pool.wait_ge(s_xc[p], 16 * (q + 1))
                pool.tensor_tensor(x1[p][:, :, :], x1[p][:, :, :], xn2[:, :, :], ALU.add).then_inc(s_x1, 1)

            def x1_rstd(g, p, q):
                pool.wait_ge(s_mv2, G * (g + 1))
                after(pool, s_rs2, g)
                apart(pool, s_apart["pool"])
                pool.tensor_scalar(ve2[:, :], mv2[:, :, 1], EPS, None, ALU.add).then_inc(s_ve2, 1)
                pool.wait_ge(s_ve2, g + 1)
                after(pool, s_xn2, G * g)
                pool.tensor_tensor(rs2[:, :], ve2[:, :], mhalf[:, 0:G], ALU.pow).then_inc(s_rs2, 1)

            def split_w2(g, p, q, half):
                pool.wait_ge(s_wh2, g + 1)
                m = slice(MK // 2 * half, MK // 2 * (half + 1))
                v = wcv[p][:, 2 * W1:].rearrange("p (m k n) -> p m k n", m=MK, k=2)
                pool.tensor_tensor(v[:, m, 1, :], wst[p][:, W1:W1 + W2].rearrange("p (m n) -> p m n", m=MK)[:, m, :],
                                   v[:, m, 0, :], ALU.subtract).then_inc(s_wl2, 1)

            def scatter(g, p, q, batches):
                if 0 in batches:
                    pool.wait_ge(s_lo, g + 1)
                    pool.wait_ge(s_meta, g + 1)
                    pool.wait_ge(s_slot, 2 * (g + 1))
                    apart(pool, s_apart["pool"])
                for b in batches:
                    for k in range(2):
                        pool.indirect_dma_start(
                            out=rows[:, :], out_offset=bass.IndirectOffsetOnAxis(ap=slot[p][:, k, b:b + 1], axis=0),
                            in_=rowb[p][:, b, :], in_offset=None).then_inc(s_sc[p], 16)

            def step(k, n, t, m, l):
                if m and t:
                    split_w2(*m, 0)
                    residual(*m)
                if n:
                    centre(*n)
                if m:
                    x1_rstd(*m)
                if m and t:
                    split_w2(*m, 1)
                if l:
                    scatter(*l, (0,))
                if k and not (isinstance(k[0], int) and k[0] == 0):
                    x_rstd(*k)
                if l:
                    scatter(*l, (1,))
                if t and not n:
                    head_rstd(*t)
                if l:
                    scatter(*l, (2, 3))
                if t and n:
                    head_rstd(*t)

            groups(pool, step)

            for p in range(2):
                pool.wait_ge(s_x1o[p], 16 * NG // 2)
            pool.wait_ge(s_sc[1], 16 * (2 * G * NG // 2 + 1))

            def tile(i, k, it):
                pool.wait_ge(s_yo, i + 1)
                pool.wait_ge(s_cw, i + 1)
                after(pool, s_sa, 16 * i)
                apart(pool, s_apart["pool"])
                pool.indirect_dma_start(
                    out=out[:, :], out_offset=bass.IndirectOffsetOnAxis(ap=dst[k][:, 0:1], axis=0),
                    in_=yo[k], in_offset=None, compute_op=ALU.add).then_inc(s_sa, 16)

            tiles(pool, tile)
            pool.wait_ge(s_sa, 16 * TILES)


def constants():
    part = np.arange(P)
    cf = np.zeros((P, C_F32), np.float32)
    cf[:, C_IDENT:C_IDENT + P] = np.eye(P)
    cf[:, C_W8:C_W8 + NE] = NE - np.arange(NE)
    cf[:, C_EBASE:C_EBASE + NE] = REGION * np.arange(NE)
    cf[:, C_THR:C_THR + NB] = P * np.arange(NB)
    cf[:, C_TILE:C_TILE + TILES] = np.arange(TILES)
    cf[:, C_TOK:C_TOK + G] = P * np.arange(G)[None] + part[:, None]
    cb = np.zeros((P, C_BF), np.float32)
    cb[:, B_IDENT:B_IDENT + P] = np.eye(P)
    mask = np.where(part[None] < part[:, None], NEG, 0.0)
    cb[:, B_MASK:B_MASK + 2 * P] = np.concatenate([mask, mask], 1)
    for q in range(PARTS):
        for b in range(G):
            for h in range(NH):
                r = 32 * q + NH * b + h
                cb[r, B_SEL + b * P:B_SEL + (b + 1) * P] = 1.0
                col = B_HSEL + ((b * 2 + h % 2) * 2 + h // 2) * P
                cb[r, col:col + P] = -1.0
                cb[r, B_HMASK + 2 * (h % 2) + h // 2] = 1.0
    cb[:, B_TRI:B_TRI + P] = part[:, None] < part[None]
    cb[:, B_ONES:B_ONES + P] = 1.0
    pad = np.zeros((P, ROW), np.float32)
    pad[:, D] = (NT + part).astype(np.int32).view(np.float32)
    return cf, (cb.view(np.uint32) >> 16).astype(np.uint16), pad


_INS = ["x", "ctx_1024", "L0_xattn_igate_kernel", "L0_xattn_igate_bias", "L0_xattn_fgate_kernel",
        "L0_xattn_fgate_bias", "L0_xattn_outnorm_scale", "L0_ffn_router_w", "L0_ffn_w1", "L0_ffn_w2"]


def kernel(**inputs):
    import concourse.bacc as bacc
    from concourse.bass_utils import run_bass_kernel_spmd

    nc = bacc.Bacc("TRN2", target_bir_lowering=False, num_devices=1)
    arrays, args = {}, []
    named = [(n, np.ascontiguousarray(inputs[n])) for n in _INS]
    named += list(zip(("const_f32", "const_selectors", "const_pad"), constants()))
    for name, a in named:
        arrays[f"in_{name}"] = a
        args.append(nc.dram_tensor(f"in_{name}", a.shape, mybir.dt.from_np(a.dtype), kind="ExternalInput").ap())
    out = nc.dram_tensor("out", (NT + P, D), F32, kind="ExternalOutput").ap()
    build(nc, *args, out)
    r = run_bass_kernel_spmd(nc, [arrays], core_ids=[0])
    return r.results[0]["out"][:NT].reshape(NB, S, D)
```
